# Optimizing a Trainium2 kernel written in Bass

```python
import numpy as np
import jax
import jax.numpy as jnp

def _softmax(x, axis=-1):
    return jax.nn.softmax(x, axis=axis)

def _gelu(x):
    return jax.nn.gelu(x, approximate=True)

def _silu(x):
    return jax.nn.silu(x)

def _sigmoid(x):
    return jax.nn.sigmoid(x)

def _layernorm(x, axis=-1, eps=1e-05):
    m = jnp.mean(x, axis=axis, keepdims=True)
    v = jnp.var(x, axis=axis, keepdims=True)
    return (x - m) / jnp.sqrt(v + eps)

def _scatter_add(tgt, idx, src, axis=0):
    return tgt.at[idx].add(src)

def _segment_sum(src, seg, n):
    return jax.ops.segment_sum(src, seg, n)
kernel_name = 'mk_decoder_preln_d2_seqx_r8_aa986b'

def setup_inputs(seed: int=0):
    np.random.seed(seed)
    _w = jnp.asarray

    def _rec_inputs():
        import jax
        import jax.numpy as jnp
        _rk = jax.random.key(seed)
        x = -0.0002928 + 1 * jax.random.normal(jax.random.fold_in(_rk, 1), (32, 128, 128), jnp.float32)
        _lenS = 128 - jax.random.randint(jax.random.fold_in(_rk, 7), (32,), 0, max(1, 128 // 4) + 1, jnp.int32)
        _lenS2 = 77 - jax.random.randint(jax.random.fold_in(_rk, 8), (32,), 0, max(1, 77 // 4) + 1, jnp.int32)
        _ctx_1024P = jax.random.normal(jax.random.fold_in(_rk, 11), (32, 16, 128), jnp.float32)
        _ctx_1024c = jax.random.dirichlet(jax.random.fold_in(_rk, 511), 0.3 * jnp.ones((16,), jnp.float32), (32, 77))
        _ctx_1024t = jnp.einsum('bsk,bkd->bsd', _ctx_1024c, _ctx_1024P)
        _ctx_1024t = _ctx_1024t * jax.lax.rsqrt(jnp.mean(jnp.square(_ctx_1024t)) + 1e-12) * 0.953939
        ctx_1024 = -1.39393e-06 + 0.999914 * (_ctx_1024t + 0.3 * jax.random.normal(jax.random.fold_in(_rk, 611), (32, 77, 128), jnp.float32))
        return (x, ctx_1024)
    x, ctx_1024 = _rec_inputs()

    def _L0_attn_setup():
        import jax, jax.numpy as jnp
        import numpy as np
        D_MODEL = 128
        H = 8
        S = 128
        HD = 128
        LV = 12
        B = 2
        T = 256

        def _level_structure(t, num_levels):
            idx = np.arange(t)
            d = idx[:, None] - idx[None, :]
            lvl = np.where(d <= 0, 0, np.floor(np.log2(np.maximum(d, 1))).astype(np.int64) + 1)
            lvl = np.minimum(lvl, num_levels - 1)
            mask = d >= 0
            return (jnp.asarray(lvl), jnp.asarray(mask))
        key = jax.random.key(seed)
        ks = jax.random.split(key, 8)
        sd = 1.0 / np.sqrt(D_MODEL)
        return {'x': jax.random.normal(ks[0], (B, T, D_MODEL), jnp.float32), 'Wq': jax.random.normal(ks[1], (H * S, D_MODEL), jnp.float32) * sd, 'Wk': jax.random.normal(ks[2], (H * S, D_MODEL), jnp.float32) * sd, 'Wv': jax.random.normal(ks[3], (H * HD, D_MODEL), jnp.float32) * sd, 'Wg': jax.random.normal(ks[4], (H, D_MODEL), jnp.float32) * sd, 'bg': jnp.zeros((H,), jnp.float32), 'Wdl': jax.random.normal(ks[5], (H * LV, D_MODEL), jnp.float32) * sd, 'Lparam': jnp.ones((H, LV), jnp.float32), 'Wo': jax.random.normal(ks[6], (D_MODEL, H * HD), jnp.float32) / np.sqrt(H * HD), 'ln_g': jnp.ones((D_MODEL,), jnp.float32), 'ln_b': jnp.zeros((D_MODEL,), jnp.float32)}
    _L0_attn_all = _L0_attn_setup()
    _L0_attn_in = {k: v for k, v in _L0_attn_all.items() if k in ('Wq', 'Wk', 'Wv', 'Wg', 'bg', 'Wdl', 'Lparam', 'Wo', 'ln_g', 'ln_b')}
    del _L0_attn_all

    def _L0_xattn_setup():
        import jax, jax.numpy as jnp
        import numpy as np
        DIM = 128
        N_HEADS = 16
        HEAD_DIM = DIM // N_HEADS
        B, N, M = (2, 256, 256)
        key = jax.random.key(seed)
        ks = jax.random.split(key, 10)
        s = 1.0 / np.sqrt(DIM)
        return {'x1': jax.random.normal(ks[0], (B, N, DIM), dtype=jnp.float32), 'x2': jax.random.normal(ks[1], (B, M, DIM), dtype=jnp.float32), 'Wq': jax.random.normal(ks[2], (DIM, DIM), dtype=jnp.float32) * s, 'bq': jnp.zeros((DIM,), dtype=jnp.float32), 'Wk': jax.random.normal(ks[3], (DIM, DIM), dtype=jnp.float32) * s, 'bk': jnp.zeros((DIM,), dtype=jnp.float32), 'Wv': jax.random.normal(ks[4], (DIM, DIM), dtype=jnp.float32) * s, 'bv': jnp.zeros((DIM,), dtype=jnp.float32), 'Wo': jax.random.normal(ks[5], (DIM, DIM), dtype=jnp.float32) * s, 'bo': jnp.zeros((DIM,), dtype=jnp.float32)}
    _L0_xattn_all = _L0_xattn_setup()
    _L0_xattn_in = {k: v for k, v in _L0_xattn_all.items() if k in ('Wq', 'bq', 'Wk', 'bk', 'Wv', 'bv', 'Wo', 'bo')}
    del _L0_xattn_all

    def _L0_ffn_setup():
        import jax, jax.numpy as jnp
        import numpy as np
        D_MODEL, HIDDEN, N_EXPERTS, TOP_K = (128, 256, 8, 2)
        RMS_EPS = 1e-06
        key = jax.random.key(seed)
        ks = jax.random.split(key, 6)
        B, S = (4, 256)
        return {'x': jax.random.normal(ks[0], (B, S, D_MODEL), jnp.float32), 'norm_weight': jnp.ones((D_MODEL,), jnp.float32), 'gate_w': jax.random.normal(ks[1], (N_EXPERTS, D_MODEL), jnp.float32) * 0.02, 'w1': jax.random.normal(ks[2], (N_EXPERTS, HIDDEN, D_MODEL), jnp.float32) * 0.02, 'b1': jnp.zeros((N_EXPERTS, HIDDEN), jnp.float32), 'w2': jax.random.normal(ks[3], (N_EXPERTS, D_MODEL, HIDDEN), jnp.float32) * 0.02, 'b2': jnp.zeros((N_EXPERTS, D_MODEL), jnp.float32)}
    _L0_ffn_all = _L0_ffn_setup()
    _L0_ffn_in = {k: v for k, v in _L0_ffn_all.items() if k in ('norm_weight', 'gate_w', 'w1', 'b1', 'w2', 'b2')}
    del _L0_ffn_all

    def _L1_attn_setup():
        import jax, jax.numpy as jnp
        import numpy as np
        DIM = 128
        HEADS = 16
        HEAD_DIM = DIM // HEADS
        NUM_FILTERS = 4
        NUM_TAPS = 101
        RES = 64

        def _fir_fft(c, sig):
            R = sig.shape[0]
            L = R + c.shape[0] - 1
            out = jnp.fft.ifft(jnp.fft.fft(sig, n=L) * jnp.fft.fft(c, n=L)).real
            return out[:R]
        key = jax.random.key(seed)
        ks = jax.random.split(key, 5)
        B, S = (2, 256)
        x = jax.random.normal(ks[0], (B, S, DIM), dtype=jnp.float32)
        Wqkv = jax.random.normal(ks[1], (3 * DIM, DIM), dtype=jnp.float32) * DIM ** (-0.5)
        Wout = jax.random.normal(ks[2], (DIM, DIM), dtype=jnp.float32) * DIM ** (-0.5)
        Wpos = jax.random.normal(ks[3], (HEADS, NUM_FILTERS), dtype=jnp.float32) * 0.5
        coeffs = jax.random.normal(ks[4], (NUM_FILTERS, NUM_TAPS), dtype=jnp.float32) * 0.05
        return {'x': x, 'Wqkv': Wqkv, 'Wout': Wout, 'Wpos': Wpos, 'coeffs': coeffs}
    _L1_attn_all = _L1_attn_setup()
    _L1_attn_in = {k: v for k, v in _L1_attn_all.items() if k in ('Wqkv', 'Wout', 'Wpos', 'coeffs')}
    del _L1_attn_all

    def _L1_xattn_setup():
        import jax, jax.numpy as jnp
        import numpy as np
        DIM = 128
        NUM_HEADS = 16
        DIM_HEAD = 64
        INNER = NUM_HEADS * DIM_HEAD
        SCALE = DIM_HEAD ** (-0.5)

        def _layernorm(x, gamma, beta, eps=1e-05):
            mu = jnp.mean(x, axis=-1, keepdims=True)
            var = jnp.mean(jnp.square(x - mu), axis=-1, keepdims=True)
            return (x - mu) * jax.lax.rsqrt(var + eps) * gamma + beta
        key = jax.random.key(seed)
        ks = jax.random.split(key, 8)
        B, SQ, SK = (2, 256, 512)
        x = jax.random.normal(ks[0], (B, SQ, DIM), dtype=jnp.float32)
        context = jax.random.normal(ks[1], (B, SK, DIM), dtype=jnp.float32)
        ln_gamma = jnp.ones((DIM,), jnp.float32)
        ln_beta = jnp.zeros((DIM,), jnp.float32)
        w_q = jax.random.normal(ks[2], (DIM, INNER), dtype=jnp.float32) / np.sqrt(DIM)
        w_kv = jax.random.normal(ks[3], (DIM, 2 * INNER), dtype=jnp.float32) / np.sqrt(DIM)
        w_out = jax.random.normal(ks[4], (INNER, DIM), dtype=jnp.float32) / np.sqrt(INNER)
        b_out = jnp.zeros((DIM,), jnp.float32)
        gate = jnp.array([0.5], jnp.float32)
        return {'x': x, 'context': context, 'ln_gamma': ln_gamma, 'ln_beta': ln_beta, 'w_q': w_q, 'w_kv': w_kv, 'w_out': w_out, 'b_out': b_out, 'gate': gate}
    _L1_xattn_all = _L1_xattn_setup()
    _L1_xattn_in = {k: v for k, v in _L1_xattn_all.items() if k in ('ln_gamma', 'ln_beta', 'w_q', 'w_kv', 'w_out', 'b_out', 'gate')}
    del _L1_xattn_all

    def _L1_ffn_setup():
        import jax, jax.numpy as jnp
        import numpy as np
        B, S, H = (2, 256, 128)
        N, F, SF, K = (16, 128, 512, 1)
        key = jax.random.key(seed)
        ks = jax.random.split(key, 7)
        std = 0.02
        return {'hidden_states': jax.random.normal(ks[0], (B, S, H), dtype=jnp.float32), 'router_w': jax.random.normal(ks[1], (N, H), dtype=jnp.float32) * std, 'gate_up_proj': jax.random.normal(ks[2], (N, H, 2 * F), dtype=jnp.float32) * std, 'down_proj': jax.random.normal(ks[3], (N, F, H), dtype=jnp.float32) * std, 'shared_gate_w': jax.random.normal(ks[4], (SF, H), dtype=jnp.float32) * std, 'shared_up_w': jax.random.normal(ks[5], (SF, H), dtype=jnp.float32) * std, 'shared_down_w': jax.random.normal(ks[6], (H, SF), dtype=jnp.float32) * std}
    _L1_ffn_all = _L1_ffn_setup()
    _L1_ffn_in = {k: v for k, v in _L1_ffn_all.items() if k in ('router_w', 'gate_up_proj', 'down_proj', 'shared_gate_w', 'shared_up_w', 'shared_down_w')}
    del _L1_ffn_all
    return {'x': x, 'ctx_1024': ctx_1024, 'L0_attn_Wq': _L0_attn_in['Wq'], 'L0_attn_Wk': _L0_attn_in['Wk'], 'L0_attn_Wv': _L0_attn_in['Wv'], 'L0_attn_Wg': _L0_attn_in['Wg'], 'L0_attn_bg': _L0_attn_in['bg'], 'L0_attn_Wdl': _L0_attn_in['Wdl'], 'L0_attn_Lparam': _L0_attn_in['Lparam'], 'L0_attn_Wo': _L0_attn_in['Wo'], 'L0_attn_ln_g': _L0_attn_in['ln_g'], 'L0_attn_ln_b': _L0_attn_in['ln_b'], 'L0_xattn_Wq': _L0_xattn_in['Wq'], 'L0_xattn_bq': _L0_xattn_in['bq'], 'L0_xattn_Wk': _L0_xattn_in['Wk'], 'L0_xattn_bk': _L0_xattn_in['bk'], 'L0_xattn_Wv': _L0_xattn_in['Wv'], 'L0_xattn_bv': _L0_xattn_in['bv'], 'L0_xattn_Wo': _L0_xattn_in['Wo'], 'L0_xattn_bo': _L0_xattn_in['bo'], 'L0_ffn_norm_weight': _L0_ffn_in['norm_weight'], 'L0_ffn_gate_w': _L0_ffn_in['gate_w'], 'L0_ffn_w1': _L0_ffn_in['w1'], 'L0_ffn_b1': _L0_ffn_in['b1'], 'L0_ffn_w2': _L0_ffn_in['w2'], 'L0_ffn_b2': _L0_ffn_in['b2'], 'L1_attn_Wqkv': _L1_attn_in['Wqkv'], 'L1_attn_Wout': _L1_attn_in['Wout'], 'L1_attn_Wpos': _L1_attn_in['Wpos'], 'L1_attn_coeffs': _L1_attn_in['coeffs'], 'L1_xattn_ln_gamma': _L1_xattn_in['ln_gamma'], 'L1_xattn_ln_beta': _L1_xattn_in['ln_beta'], 'L1_xattn_w_q': _L1_xattn_in['w_q'], 'L1_xattn_w_kv': _L1_xattn_in['w_kv'], 'L1_xattn_w_out': _L1_xattn_in['w_out'], 'L1_xattn_b_out': _L1_xattn_in['b_out'], 'L1_xattn_gate': _L1_xattn_in['gate'], 'L1_ffn_router_w': _L1_ffn_in['router_w'], 'L1_ffn_gate_up_proj': _L1_ffn_in['gate_up_proj'], 'L1_ffn_down_proj': _L1_ffn_in['down_proj'], 'L1_ffn_shared_gate_w': _L1_ffn_in['shared_gate_w'], 'L1_ffn_shared_up_w': _L1_ffn_in['shared_up_w'], 'L1_ffn_shared_down_w': _L1_ffn_in['shared_down_w']}

def reference(x, ctx_1024, L0_attn_Wq, L0_attn_Wk, L0_attn_Wv, L0_attn_Wg, L0_attn_bg, L0_attn_Wdl, L0_attn_Lparam, L0_attn_Wo, L0_attn_ln_g, L0_attn_ln_b, L0_xattn_Wq, L0_xattn_bq, L0_xattn_Wk, L0_xattn_bk, L0_xattn_Wv, L0_xattn_bv, L0_xattn_Wo, L0_xattn_bo, L0_ffn_norm_weight, L0_ffn_gate_w, L0_ffn_w1, L0_ffn_b1, L0_ffn_w2, L0_ffn_b2, L1_attn_Wqkv, L1_attn_Wout, L1_attn_Wpos, L1_attn_coeffs, L1_xattn_ln_gamma, L1_xattn_ln_beta, L1_xattn_w_q, L1_xattn_w_kv, L1_xattn_w_out, L1_xattn_b_out, L1_xattn_gate, L1_ffn_router_w, L1_ffn_gate_up_proj, L1_ffn_down_proj, L1_ffn_shared_gate_w, L1_ffn_shared_up_w, L1_ffn_shared_down_w):
    import jax
    import jax.numpy as jnp

    def _L0_attn_ref(x, Wq, Wk, Wv, Wg, bg, Wdl, Lparam, Wo, ln_g, ln_b):
        import jax, jax.numpy as jnp
        import numpy as np
        D_MODEL = 128
        H = 8
        S = 128
        HD = 128
        LV = 12
        B = 2
        T = 256

        def _level_structure(t, num_levels):
            idx = np.arange(t)
            d = idx[:, None] - idx[None, :]
            lvl = np.where(d <= 0, 0, np.floor(np.log2(np.maximum(d, 1))).astype(np.int64) + 1)
            lvl = np.minimum(lvl, num_levels - 1)
            mask = d >= 0
            return (jnp.asarray(lvl), jnp.asarray(mask))
        b, t, _ = x.shape
        q = (x @ Wq.T).reshape(b, t, H, S)
        k = (x @ Wk.T).reshape(b, t, H, S)
        v = (x @ Wv.T).reshape(b, t, H, HD)
        g = -jax.nn.softplus(x @ Wg.T + bg)
        dl = (x @ Wdl.T).reshape(b, t, H, LV)
        lam = jax.nn.softplus(dl + Lparam[None, None])
        G = jnp.cumsum(g, axis=1)
        lvl, mask = _level_structure(t, LV)
        scale = 1.0 / np.sqrt(S)
        scores = jnp.einsum('bthd,bshd->bhts', q, k) * scale
        Gh = G.transpose(0, 2, 1)
        logdecay = Gh[:, :, :, None] - Gh[:, :, None, :]
        logdecay = jnp.where(mask[None, None], logdecay, -jnp.inf)
        decay = jnp.exp(logdecay)
        lvl_oh = jax.nn.one_hot(lvl, LV, dtype=x.dtype)
        lamw = jnp.einsum('bthl,tsl->bhts', lam, lvl_oh)
        A = scores * decay * lamw
        y = jnp.einsum('bhts,bshd->bthd', A, v).reshape(b, t, H * HD)
        out = y @ Wo.T + x
        mu = out.mean(-1, keepdims=True)
        var = out.var(-1, keepdims=True)
        return (out - mu) * jax.lax.rsqrt(var + 1e-05) * ln_g + ln_b

    def _L0_xattn_ref(x1, x2, Wq, bq, Wk, bk, Wv, bv, Wo, bo):
        import jax, jax.numpy as jnp
        import numpy as np
        DIM = 128
        N_HEADS = 16
        HEAD_DIM = DIM // N_HEADS
        B, N, M = (2, 256, 256)
        b, n, _ = x1.shape
        m = x2.shape[1]
        q = x1 @ Wq.T + bq
        k = x2 @ Wk.T + bk
        v = x2 @ Wv.T + bv
        q = q.reshape(b, n, N_HEADS, HEAD_DIM).transpose(0, 2, 1, 3)
        k = k.reshape(b, m, N_HEADS, HEAD_DIM).transpose(0, 2, 1, 3)
        v = v.reshape(b, m, N_HEADS, HEAD_DIM).transpose(0, 2, 1, 3)
        scale = 1.0 / jnp.sqrt(jnp.asarray(HEAD_DIM, dtype=q.dtype))
        scores = jnp.einsum('bhnd,bhmd->bhnm', q, k) * scale
        attn = jax.nn.softmax(scores, axis=-1)
        o = jnp.einsum('bhnm,bhmd->bhnd', attn, v)
        o = o.transpose(0, 2, 1, 3).reshape(b, n, DIM)
        return o @ Wo.T + bo

    def _L0_ffn_ref(x, norm_weight, gate_w, w1, b1, w2, b2):
        import jax, jax.numpy as jnp
        import numpy as np
        D_MODEL, HIDDEN, N_EXPERTS, TOP_K = (128, 256, 8, 2)
        RMS_EPS = 1e-06
        B, S, D = x.shape
        E = gate_w.shape[0]
        t = x * jax.lax.rsqrt(jnp.mean(x * x, axis=-1, keepdims=True) + RMS_EPS) * norm_weight
        tokens = t.reshape(-1, D)
        T = tokens.shape[0]
        gate_logits = tokens @ gate_w.T
        gate_scores, expert_idx = jax.lax.top_k(gate_logits, TOP_K)
        routing_weights = jax.nn.softmax(gate_scores, axis=-1)
        combine = jnp.zeros((T, E), tokens.dtype).at[jnp.arange(T)[:, None], expert_idx].add(routing_weights)

        def body(acc, params):
            W1, B1, W2, B2, c = params
            h = jax.nn.gelu(tokens @ W1.T + B1, approximate=False)
            o = h @ W2.T + B2
            return (acc + c[:, None] * o, None)
        out, _ = jax.lax.scan(body, jnp.zeros_like(tokens), (w1, b1, w2, b2, combine.T))
        return x + out.reshape(B, S, D)

    def _L1_attn_ref(x, Wqkv, Wout, Wpos, coeffs):
        import jax, jax.numpy as jnp
        import numpy as np
        DIM = 128
        HEADS = 16
        HEAD_DIM = DIM // HEADS
        NUM_FILTERS = 4
        NUM_TAPS = 101
        RES = 64

        def _fir_fft(c, sig):
            R = sig.shape[0]
            L = R + c.shape[0] - 1
            out = jnp.fft.ifft(jnp.fft.fft(sig, n=L) * jnp.fft.fft(c, n=L)).real
            return out[:R]
        B, S, D = x.shape
        scale = HEAD_DIM ** (-0.5)
        proto = jnp.linspace(0.0, 1.0, RES).astype(x.dtype)
        table = jax.vmap(_fir_fft, in_axes=(0, None))(coeffs, proto).T
        r = jnp.arange(S)
        rel = jnp.abs(r[None, :] - r[:, None]).astype(jnp.float32) / max(S - 1, 1)
        idx = jnp.clip(jnp.round(rel * (RES - 1)).astype(jnp.int32), 0, RES - 1)
        pos_feat = table[idx]
        pos_bias = jnp.einsum('ijf,hf->hij', pos_feat, Wpos)
        qkv = jnp.einsum('bsd,ed->bse', x, Wqkv)
        q, k, v = jnp.split(qkv, 3, axis=-1)
        q = q.reshape(B, S, HEADS, HEAD_DIM)
        k = k.reshape(B, S, HEADS, HEAD_DIM)
        v = v.reshape(B, S, HEADS, HEAD_DIM)
        logits = jnp.einsum('bihd,bjhd->bhij', q, k) * scale + pos_bias[None]
        attn = jax.nn.softmax(logits, axis=-1)
        out = jnp.einsum('bhij,bjhd->bihd', attn, v).reshape(B, S, D)
        return jnp.einsum('bsd,ed->bse', out, Wout)

    def _L1_xattn_ref(x, context, ln_gamma, ln_beta, w_q, w_kv, w_out, b_out, gate):
        import jax, jax.numpy as jnp
        import numpy as np
        DIM = 128
        NUM_HEADS = 16
        DIM_HEAD = 64
        INNER = NUM_HEADS * DIM_HEAD
        SCALE = DIM_HEAD ** (-0.5)

        def _layernorm(x, gamma, beta, eps=1e-05):
            mu = jnp.mean(x, axis=-1, keepdims=True)
            var = jnp.mean(jnp.square(x - mu), axis=-1, keepdims=True)
            return (x - mu) * jax.lax.rsqrt(var + eps) * gamma + beta
        B, SQ, _ = x.shape
        SK = context.shape[1]
        xn = _layernorm(x, ln_gamma, ln_beta)
        q = (xn @ w_q).reshape(B, SQ, NUM_HEADS, DIM_HEAD)
        kv = context @ w_kv
        k, v = jnp.split(kv, 2, axis=-1)
        k = k.reshape(B, SK, NUM_HEADS, DIM_HEAD)
        v = v.reshape(B, SK, NUM_HEADS, DIM_HEAD)
        scores = jnp.einsum('bqhd,bkhd->bhqk', q * SCALE, k)
        attn = jax.nn.softmax(scores, axis=-1)
        out = jnp.einsum('bhqk,bkhd->bqhd', attn, v).reshape(B, SQ, INNER)
        out = out @ w_out + b_out
        return out * jnp.tanh(gate[0])

    def _L1_ffn_ref(hidden_states, router_w, gate_up_proj, down_proj, shared_gate_w, shared_up_w, shared_down_w):
        import jax, jax.numpy as jnp
        import numpy as np
        B, S, H = (2, 256, 128)
        N, F, SF, K = (16, 128, 512, 1)
        b, s, h = hidden_states.shape
        hidden = hidden_states.reshape(-1, h)
        t = hidden.shape[0]
        logits = hidden @ router_w.T
        top_vals, top_idx = jax.lax.top_k(logits, K)
        scores = jnp.full_like(logits, -jnp.inf)
        scores = scores.at[jnp.arange(t)[:, None], top_idx].set(top_vals)
        scores = jax.nn.sigmoid(scores.astype(jnp.float32)).astype(hidden.dtype)
        routed_in = hidden[None, :, :] * scores.T[:, :, None]
        gate_up = jnp.einsum('nth,nhf->ntf', routed_in, gate_up_proj)
        gate, up = jnp.split(gate_up, 2, axis=-1)
        routed_out = jnp.einsum('ntf,nfh->nth', up * jax.nn.silu(gate), down_proj)
        expert_sum = routed_out.sum(axis=0)
        shared = jax.nn.silu(hidden @ shared_gate_w.T) * (hidden @ shared_up_w.T) @ shared_down_w.T
        return (shared + expert_sum).reshape(b, s, h)
    x = x + _L0_attn_ref(_layernorm(x, axis=-1), L0_attn_Wq, L0_attn_Wk, L0_attn_Wv, L0_attn_Wg, L0_attn_bg, L0_attn_Wdl, L0_attn_Lparam, L0_attn_Wo, L0_attn_ln_g, L0_attn_ln_b)
    x = x + _L0_xattn_ref(_layernorm(x, axis=-1), ctx_1024, L0_xattn_Wq, L0_xattn_bq, L0_xattn_Wk, L0_xattn_bk, L0_xattn_Wv, L0_xattn_bv, L0_xattn_Wo, L0_xattn_bo)
    x = x + _L0_ffn_ref(_layernorm(x, axis=-1), L0_ffn_norm_weight, L0_ffn_gate_w, L0_ffn_w1, L0_ffn_b1, L0_ffn_w2, L0_ffn_b2)
    x = x + _L1_attn_ref(_layernorm(x, axis=-1), L1_attn_Wqkv, L1_attn_Wout, L1_attn_Wpos, L1_attn_coeffs)
    x = x + _L1_xattn_ref(_layernorm(x, axis=-1), ctx_1024, L1_xattn_ln_gamma, L1_xattn_ln_beta, L1_xattn_w_q, L1_xattn_w_kv, L1_xattn_w_out, L1_xattn_b_out, L1_xattn_gate)
    x = x + _L1_ffn_ref(_layernorm(x, axis=-1), L1_ffn_router_w, L1_ffn_gate_up_proj, L1_ffn_down_proj, L1_ffn_shared_gate_w, L1_ffn_shared_up_w, L1_ffn_shared_down_w)
    return x

_drawn_inputs = setup_inputs


def setup_inputs(seed=0):
    import zlib

    import numpy as np

    out = dict(_drawn_inputs(seed))
    spreads = {'L0_attn_bg': (0.0, 0.8),
     'L0_attn_Lparam': (1.0, 0.2),
     'L0_attn_ln_g': (1.0, 0.2),
     'L0_attn_ln_b': (0.0, 0.1),
     'L0_xattn_bq': (0.0, 0.524),
     'L0_xattn_bk': (0.0, 0.8),
     'L0_xattn_bv': (0.0, 0.1),
     'L0_xattn_bo': (0.0, 0.1),
     'L0_ffn_norm_weight': (1.0, 0.6),
     'L0_ffn_b1': (0.0, 0.8),
     'L0_ffn_b2': (0.0, 0.326),
     'L1_xattn_ln_gamma': (1.0, 0.6),
     'L1_xattn_ln_beta': (0.0, 0.8),
     'L1_xattn_b_out': (0.0, 0.443)}
    factors = {'L0_ffn_w1': 5.974,
     'L0_ffn_w2': 5.396,
     'L1_attn_Wpos': 8.0,
     'L1_attn_coeffs': 8.0,
     'L1_ffn_router_w': 8.0,
     'L1_ffn_gate_up_proj': 8.0,
     'L1_ffn_down_proj': 8.0,
     'L1_ffn_shared_gate_w': 8.0,
     'L1_ffn_shared_up_w': 8.0,
     'L1_ffn_shared_down_w': 8.0}
    for name, (base, spread) in spreads.items():
        noise = np.random.default_rng([zlib.crc32(name.encode()), seed]).standard_normal(out[name].shape)
        drawn = base * np.exp(spread * noise) if base else spread * noise
        out[name] = jnp.asarray(drawn.astype(out[name].dtype))
    for name, factor in factors.items():
        out[name] = (out[name] * factor).astype(out[name].dtype)
    return out
```

```python
from contextlib import ExitStack

import numpy as np
import concourse.bass as bass
from concourse import mybir

F32 = mybir.dt.float32
BF16 = mybir.dt.bfloat16
U32 = mybir.dt.uint32
ALU = mybir.AluOpType
ACT = mybir.ActivationFunctionType
AX = mybir.AxisListType

P = 128
BATCH = 32
T = 128
D = 128
M = 77
G = 4
GROUPS = BATCH // G
GT = G * T
GM = G * M
LN_EPS = 1e-5
RMS_EPS = 1e-6
CREDIT = 1


def at(i, per_group, k):
    return i * per_group + (k + CREDIT)


class Chain:

    def __init__(self, engine, semaphore, i, per_group):
        self.engine, self.semaphore, self.i, self.per_group, self.links = engine, semaphore, i, per_group, 0

    def link(self, instruction):
        self.links += 1
        instruction.then_inc(self.semaphore, 1)
        self.engine.wait_ge(self.semaphore, at(self.i, self.per_group, self.links))

    def end(self):
        assert self.links == self.per_group, (self.links, self.per_group)


class Core:

    def __init__(self, nc, ctx):
        self.nc, self.ctx = nc, ctx
        self.local = ctx
        self.fresh = []
        self.x = self.sbuf("x_all", [P, BATCH, D])
        self.ident = self.sbuf("ident", [P, P])
        self.ident_bf = self.sbuf("ident_bf", [P, P], BF16)
        self.minus_half = self.sbuf("minus_half", [P, G])
        self.eps = {LN_EPS: self.sbuf("ln_eps", [P, G]), RMS_EPS: self.sbuf("rms_eps", [P, G])}
        self.spare = self.sbuf("spare", [P, 1])
        self.bank = ctx.enter_context(nc.psum_tensor("bank", [P, 8, 512], F32))

    def sbuf(self, name, shape, dtype=F32):
        return self.ctx.enter_context(self.nc.sbuf_tensor(name, shape, dtype))

    def semaphore(self, name):
        s = self.local.enter_context(self.nc.semaphore(name))
        self.fresh.append((s, CREDIT))
        return s

    def plain_semaphore(self, name):
        s = self.local.enter_context(self.nc.semaphore(name))
        self.fresh.append((s, 0))
        return s

    def hold_vector(self):
        self.nc.vector.tensor_copy(self.spare[:, :], self.minus_half[:, 0:1])

    def start_stage(self, weights_landed, count):
        nc, fresh, self.fresh = self.nc, self.fresh, []
        with nc.Block() as block:
            @block.gpsimd
            def _(pool):
                for s, start in fresh:
                    pool.sem_clear(s)
                    if start:
                        pool.sem_inc(s, start)

            @block.sync
            def _(sp):
                sp.wait_ge(weights_landed, count)


class Moments:

    def __init__(self, core, sbuf, name, eps=LN_EPS):
        self.core, self.nc, self.eps = core, core.nc, eps
        self.stats = sbuf(name + "_stats", [P, G, 6])
        self.moments = sbuf(name + "_moments", [P, G, 2])
        self.variance = sbuf(name + "_variance", [P, G])
        self.rstd = sbuf(name + "_rstd", [P, G])
        self.moments_ready = core.semaphore(name + "_moments_ready")
        self.variance_ready = core.semaphore(name + "_variance_ready")
        self.rstd_ready = core.semaphore(name + "_rstd_ready")

    def moments_by_vector(self, chain, source):
        nc = self.nc
        for n in range(G):
            last = nc.vector.bn_stats(self.stats[:, n, :], source(n))
        chain.link(last)
        self.core.hold_vector()
        for n in range(G):
            last = nc.vector.bn_aggr(self.moments[:, n, :], self.stats[:, n, :])
        last.then_inc(self.moments_ready, 1)

    def rstd_by_gpsimd(self, pool, i):
        nc = self.nc
        pool.wait_ge(self.moments_ready, at(i, 1, 1))
        nc.gpsimd.tensor_tensor(self.variance[:, :], self.moments[:, :, 1], self.core.eps[self.eps][:, :],
                                ALU.add).then_inc(self.variance_ready, 1)
        pool.wait_ge(self.variance_ready, at(i, 1, 1))
        nc.gpsimd.tensor_tensor(self.rstd[:, :], self.variance[:, :], self.core.minus_half[:, :],
                                ALU.pow).then_inc(self.rstd_ready, 1)

    def scaled_by_vector(self, dve, i, out, source, ready):
        nc = self.nc
        dve.wait_ge(self.rstd_ready, at(i, 1, 1))
        for n in range(G):
            nc.vector.tensor_scalar(out[:, n, :], source(n), self.moments[:, n, 0:1], self.rstd[:, n:n + 1],
                                    ALU.subtract, ALU.mult).then_inc(ready, 1)


class Norm(Moments):

    def __init__(self, core, sbuf, name):
        super().__init__(core, sbuf, name)
        self.xn = sbuf(name + "_xn", [P, G, D])
        self.xnT = sbuf(name + "_xnT", [P, GT])
        self.xn_ready = core.semaphore(name + "_xn_ready")
        self.flipped = core.semaphore(name + "_flipped")
        self.xnT_ready = core.semaphore(name + "_xnT_ready")

    def source(self, i):
        return lambda n: self.core.x[:, bass.ds(i * G + n, 1), :]

    def norm_by_vector(self, dve, i, chain):
        self.moments_by_vector(chain, self.source(i))
        self.scaled_by_vector(dve, i, self.xn, self.source(i), self.xn_ready)

    def flip_by_tensor(self, pe, i, bank):
        nc = self.nc
        for n in range(G):
            pe.wait_ge(self.xn_ready, at(i, G, n + 1))
            last = nc.tensor.transpose(bank[:, n * T:(n + 1) * T], self.xn[:, n, :], self.core.ident[:, :])
        last.then_inc(self.flipped, 1)

    def xnT_by_scalar(self, act, i, bank):
        act.wait_ge(self.flipped, at(i, 1, 1))
        self.nc.scalar.copy(self.xnT[:, :], bank[:, :]).then_inc(self.xnT_ready, 1)


class Weights:

    def __init__(self, core):
        self.core, self.loads, self.landed, self.count = core, [], {}, {}

    def load(self, stage, name, shape, source, dtype=F32):
        if stage not in self.landed:
            self.landed[stage] = self.core.ctx.enter_context(self.core.nc.semaphore(f"{stage}_weights_landed"))
            self.count[stage] = 0
        tile = self.core.sbuf(name, shape, dtype)
        self.loads.append((stage, tile, source))
        self.count[stage] += 16
        return tile



H1 = 8
LEVELS = 8
TB = P // LEVELS
NB = T // TB
SMALL = H1 + LEVELS * H1
HALF = NB // 2 * H1 * TB


def level_constants():
    band = np.zeros((LEVELS, TB, 2 * T - TB), np.float32)
    for b in range(TB):
        for c in range(2 * T - TB):
            distance = b - (c - (T - TB))
            if 0 <= distance < T:
                band[0 if distance == 0 else int(np.log2(distance)) + 1, b, c] = 1.0
    u, t = np.arange(T)[:, None], np.arange(T)[None, :]
    upto = (u <= t).astype(np.float32)
    minus_after = -(u > t).astype(np.float32)
    own = np.tile(np.eye(TB, dtype=np.float32), (LEVELS, 1))
    return band.reshape(P, 2 * T - TB), upto, minus_after, own


def stage1_weights(w, a):
    heads = "(h s) d -> s h d"
    w.s1_wq = w.load("s1", "w_s1_q", [P, H1, D], a["s1_wq"].rearrange(heads, s=P))
    w.s1_wk = w.load("s1", "w_s1_k", [P, H1, D], a["s1_wk"].rearrange(heads, s=P))
    w.s1_wv = w.load("s1", "w_s1_v", [P, H1, D], a["s1_wv"].rearrange(heads, s=P))
    w.s1_woT = w.load("s1", "w_s1_oT", [P, H1, D], a["s1_woT"].rearrange(heads, s=P))
    w.s1_small = w.load("s1", "w_s1_small", [P, SMALL], a["s1_small"])
    w.s1_bias = w.load("s1", "w_s1_bias", [P, SMALL], a["s1_bias"].unsqueeze(0).to_broadcast([P, SMALL]))
    w.s1_g = w.load("s1", "w_s1_g", [P, D], a["s1_g"].unsqueeze(0).to_broadcast([P, D]))
    w.s1_b = w.load("s1", "w_s1_b", [P, D], a["s1_b"].unsqueeze(0).to_broadcast([P, D]))
    w.band = w.load("s1", "w_band", [P, 2 * T - TB], a["band"])
    w.upto = w.load("s1", "w_upto", [P, T], a["upto"])
    w.minus_after = w.load("s1", "w_minus_after", [P, T], a["minus_after"])
    w.own = w.load("s1", "w_own", [P, TB], a["own"])


def stage1(nc, core, w, scratch):
    with ExitStack() as local:
        core.local = local
        def sbuf(name, shape, dtype=F32):
            return local.enter_context(nc.sbuf_tensor(name, shape, dtype))

        ln = Norm(core, sbuf, "s1_ln")
        ln2 = Moments(core, sbuf, "s1_ln2")
        qk = sbuf("s1_qk", [P, H1, D])
        vo = sbuf("s1_vo", [P, H1, D])
        qT = sbuf("s1_qT", [P, G * NB, H1, TB])
        v = sbuf("s1_v", [P, G, H1 * D])
        pre = sbuf("s1_pre", [P, 1 + LEVELS, G, H1])
        log = sbuf("s1_log", [P, 1 + LEVELS, G, H1])
        soft = sbuf("s1_soft", [P, 1 + LEVELS, G, H1])
        lam = sbuf("s1_lam", [P, NB, G, H1])
        gate = sbuf("s1_gate", [P, 2, NB, H1, TB])
        level = sbuf("s1_level", [P, 2, NB, H1, TB])
        decay = sbuf("s1_decay", [P, 2, 2, HALF])
        weight = sbuf("s1_weight", [P, 2, HALF])
        aT = sbuf("s1_aT", [P, 2, H1, T])
        y = sbuf("s1_y", [P, G, D])
        z = sbuf("s1_z", [P, G, D])

        fold_done = core.plain_semaphore("s1_fold_done")
        fold_kept = core.plain_semaphore("s1_fold_kept")
        chain_v = core.semaphore("s1_chain_v")
        chain_p = core.semaphore("s1_chain_p")
        small_done = core.semaphore("s1_small_done")
        pre_kept = core.semaphore("s1_pre_kept")
        magnitude_ready = core.semaphore("s1_magnitude_ready")
        exp_ready = core.semaphore("s1_exp_ready")
        log_ready = core.semaphore("s1_log_ready")
        soft_ready = core.semaphore("s1_soft_ready")
        projected = core.semaphore("s1_projected")
        kept_by_scalar = core.semaphore("s1_kept_by_scalar")
        kept_by_vector = core.semaphore("s1_kept_by_vector")
        gate_ready = core.semaphore("s1_gate_ready")
        level_ready = core.semaphore("s1_level_ready")
        logdecay_done = core.semaphore("s1_logdecay_done")
        decay_ready = core.semaphore("s1_decay_ready")
        level_done = core.semaphore("s1_level_done")
        weight_ready = core.semaphore("s1_weight_ready")
        score_done = core.semaphore("s1_score_done")
        aT_ready = core.semaphore("s1_aT_ready")
        out_done = core.semaphore("s1_out_done")
        y_ready = core.semaphore("s1_y_ready")
        z_ready = core.semaphore("s1_z_ready")
        x_ready = core.semaphore("s1_x_ready")
        spilled = core.plain_semaphore("s1_spilled")
        lam_landed = core.plain_semaphore("s1_lam_landed")

        core.start_stage(w.landed["s1"], w.count["s1"])
        bank = core.bank
        LOGDECAY, LEVEL, SCORE, WORK = 0, 2, 4, 6
        PROJ = H1 + 2 * G

        with nc.Block() as block:
            @block.tensor
            def _(pe):
                for h in range(H1):
                    if h >= 2:
                        pe.wait_ge(fold_kept, h - 1)
                    nc.tensor.matmul(bank[:, h % 2, 0:D], w.s1_wq[:, h, :], w.s1_wk[:, h, :], start=True, stop=True)
                    nc.tensor.matmul(bank[:, h % 2, D:2 * D], w.s1_wv[:, h, :], w.s1_woT[:, h, :], start=True,
                                     stop=True).then_inc(fold_done, 1)

            @block.vector
            def _(dve):
                for h in range(H1):
                    dve.wait_ge(fold_done, h + 1)
                    nc.vector.tensor_scalar(qk[:, h, :], bank[:, h % 2, 0:D], float(D) ** -0.5, None, ALU.mult)
                    nc.vector.tensor_copy(vo[:, h, :], bank[:, h % 2, D:2 * D]).then_inc(fold_kept, 1)

        def keep(copy, k):
            source = bank[:, WORK + k % 2, :]
            if k < H1:
                return copy(qT[:, :, k, :], source.rearrange("p (a b) -> p a b", b=TB))
            n, c = (k - H1) // 2, (k - H1) % 2
            return copy(v[:, n, c * 512:(c + 1) * 512], source)

        with nc.Block() as block:
            @block.sync
            def _(sp):
                with sp.Fori(0, GROUPS) as i:
                    sp.wait_ge(soft_ready, at(i, 1, 1))
                    sp.dma_start(scratch[:, :, :],
                                 soft[:, 1:, :, :].rearrange("p l n h -> p l (n h)")).then_inc(spilled, 16)
                    sp.wait_ge(spilled, (i + 1) * 16)
                    for l in range(LEVELS):
                        sp.dma_start(lam[l * TB:(l + 1) * TB, :, :, :].rearrange("b a n h -> b a (n h)"),
                                     scratch[:, l, :].rearrange("(a b) c -> b a c", b=TB)).then_inc(lam_landed, 16)
                sp.wait_ge(lam_landed, GROUPS * 16 * LEVELS)

            @block.gpsimd
            def _(pool):
                with pool.Fori(0, GROUPS) as i:
                    chain = Chain(pool, chain_p, i, 2)
                    ln.rstd_by_gpsimd(pool, i)
                    for n in range(G):
                        free = 2 * max(n - 1, 0)
                        if n == 0:
                            pool.wait_ge(soft_ready, at(i, 1, 1))
                        pool.wait_ge(logdecay_done, at(i, 2 * G, free))
                        nc.gpsimd.tensor_tensor(
                            gate[:, n % 2, :, :, :],
                            w.upto[:, :].rearrange("p (a b) -> p a b", b=TB).unsqueeze(2).to_broadcast([P, NB, H1, TB]),
                            soft[:, 0, n, :].unsqueeze(1).unsqueeze(3).to_broadcast([P, NB, H1, TB]),
                            ALU.mult).then_inc(gate_ready, 1)
                        if n == 0:
                            pool.wait_ge(lam_landed, (i + 1) * (16 * LEVELS))
                        pool.wait_ge(level_done, at(i, 2 * G, free))
                        nc.gpsimd.tensor_tensor(
                            level[:, n % 2, :, :, :],
                            lam[:, :, n, :].unsqueeze(3).to_broadcast([P, NB, H1, TB]),
                            w.own[:, :].unsqueeze(1).unsqueeze(1).to_broadcast([P, NB, H1, TB]),
                            ALU.mult).then_inc(level_ready, 1)
                    ln2.rstd_by_gpsimd(pool, i)
                    pool.wait_ge(z_ready, at(i, G, G))
                    chain.link(nc.gpsimd.tensor_tensor(
                        z[:, :, :], z[:, :, :], w.s1_g[:, :].unsqueeze(1).to_broadcast([P, G, D]), ALU.mult))
                    chain.link(nc.gpsimd.tensor_tensor(
                        z[:, :, :], z[:, :, :], w.s1_b[:, :].unsqueeze(1).to_broadcast([P, G, D]), ALU.add))
                    x = core.x[:, bass.ts(i, G), :]
                    nc.gpsimd.tensor_tensor(x, x, z[:, :, :], ALU.add).then_inc(x_ready, 1)
                    chain.end()

            @block.scalar
            def _(act):
                nc.scalar.preload_act_table_set("natural_log_exp_and_others")
                with act.Fori(0, GROUPS) as i:
                    ln.xnT_by_scalar(act, i, bank[:, WORK, :])
                    act.wait_ge(magnitude_ready, at(i, 1, 1))
                    nc.scalar.activation(log[:, :, :, :], log[:, :, :, :], ACT.Exp).then_inc(exp_ready, 1)
                    act.wait_ge(exp_ready, at(i, 1, 1))
                    nc.scalar.activation(log[:, :, :, :], log[:, :, :, :], ACT.Ln, bias=1.0).then_inc(log_ready, 1)
                    for k in range(0, PROJ, 2):
                        act.wait_ge(projected, at(i, PROJ, k + 1))
                        keep(nc.scalar.copy, k).then_inc(kept_by_scalar, 1)
                    for n in range(G):
                        act.wait_ge(weight_ready, at(i, 2 * G, 2 * max(n - 1, 0)))
                        for j in range(2):
                            act.wait_ge(logdecay_done, at(i, 2 * G, 2 * n + j + 1))
                            nc.scalar.activation(decay[:, n % 2, j, :], bank[:, LOGDECAY + j, :],
                                                 ACT.Exp).then_inc(decay_ready, 1)

            @block.vector
            def _(dve):
                with dve.Fori(0, GROUPS) as i:
                    chain = Chain(dve, chain_v, i, 3)
                    ln.norm_by_vector(dve, i, chain)

                    dve.wait_ge(small_done, at(i, 1, 1))
                    chain.link(nc.vector.tensor_tensor(
                        pre[:, :, :, :].rearrange("p l n h -> p n l h"),
                        bank[:, WORK + 1, 0:G * SMALL].rearrange("p (n l h) -> p n l h", n=G, h=H1),
                        w.s1_bias[:, :].rearrange("p (l h) -> p l h", h=H1).unsqueeze(1).to_broadcast(
                            [P, G, 1 + LEVELS, H1]), ALU.add))
                    nc.vector.scalar_tensor_tensor(out=log[:, :, :, :], in0=pre[:, :, :, :], scalar=-1.0,
                                                   in1=pre[:, :, :, :], op0=ALU.mult,
                                                   op1=ALU.min).then_inc(magnitude_ready, 1)
                    for k in range(1, PROJ, 2):
                        dve.wait_ge(projected, at(i, PROJ, k + 1))
                        keep(nc.vector.tensor_copy, k).then_inc(kept_by_vector, 1)
                        if k == 1:
                            dve.wait_ge(log_ready, at(i, 1, 1))
                            nc.vector.scalar_tensor_tensor(out=soft[:, :, :, :], in0=pre[:, :, :, :], scalar=0.0,
                                                           in1=log[:, :, :, :], op0=ALU.max,
                                                           op1=ALU.add).then_inc(soft_ready, 1)

                    def y_of(n):
                        dve.wait_ge(out_done, at(i, G, n + 1))
                        nc.vector.tensor_tensor(y[:, n, :], bank[:, WORK + n % 2, 0:D], ln.xn[:, n, :],
                                                ALU.add).then_inc(y_ready, 1)

                    for n in range(G):
                        if n >= 1:
                            y_of(n - 1)
                        for j in range(2):
                            dve.wait_ge(decay_ready, at(i, 2 * G, 2 * n + j + 1))
                            dve.wait_ge(level_done, at(i, 2 * G, 2 * n + j + 1))
                            nc.vector.tensor_tensor(weight[:, j, :], bank[:, LEVEL + j, :], decay[:, n % 2, j, :],
                                                    ALU.mult).then_inc(weight_ready, 1)
                        dve.wait_ge(out_done, at(i, G, max(n - 1, 0)))
                        for j in range(2):
                            dve.wait_ge(weight_ready, at(i, 2 * G, 2 * n + j + 1))
                            dve.wait_ge(score_done, at(i, 2 * G, 2 * n + j + 1))
                            nc.vector.tensor_tensor(
                                aT[:, n % 2, :, j * (T // 2):(j + 1) * (T // 2)].rearrange("p h (a b) -> p a h b", b=TB),
                                bank[:, SCORE + j, :].rearrange("p (a h b) -> p a h b", h=H1, b=TB),
                                weight[:, j, :].rearrange("p (a h b) -> p a h b", h=H1, b=TB),
                                ALU.mult).then_inc(aT_ready, 1)
                    y_of(G - 1)
                    dve.wait_ge(y_ready, at(i, G, G))
                    ln2.moments_by_vector(chain, lambda n: y[:, n, :])
                    dve.wait_ge(x_ready, at(i, 1, 0))
                    ln2.scaled_by_vector(dve, i, z, lambda n: y[:, n, :], z_ready)
                    chain.end()

            @block.tensor
            def _(pe):
                with pe.Fori(0, GROUPS) as i:
                    pe.wait_ge(y_ready, at(i, G, 0))
                    ln.flip_by_tensor(pe, i, bank[:, WORK, :])
                    pe.wait_ge(ln.xnT_ready, at(i, 1, 1))
                    for n in range(G):
                        last = nc.tensor.matmul(bank[:, WORK + 1, n * SMALL:(n + 1) * SMALL],
                                                ln.xnT[:, n * T:(n + 1) * T], w.s1_small[:, :], start=True, stop=True)
                    last.then_inc(small_done, 1)
                    for k in range(PROJ):
                        if k == 1:
                            pe.wait_ge(magnitude_ready, at(i, 1, 1))
                        if k >= 2:
                            pe.wait_ge(kept_by_vector if k % 2 else kept_by_scalar, at(i, PROJ // 2, k // 2))
                        if k < H1:
                            nc.tensor.matmul(bank[:, WORK + k % 2, :], qk[:, k, :], ln.xnT[:, :], start=True,
                                             stop=True).then_inc(projected, 1)
                        else:
                            n, c = (k - H1) // 2, (k - H1) % 2
                            nc.tensor.matmul(bank[:, WORK + k % 2, :], ln.xnT[:, n * T:(n + 1) * T],
                                             vo[:, c * (H1 // 2):(c + 1) * (H1 // 2), :].rearrange("p h d -> p (h d)"),
                                             start=True, stop=True).then_inc(projected, 1)

                    def out_of(n):
                        pe.wait_ge(aT_ready, at(i, 2 * G, 2 * n + 2))
                        pe.wait_ge(y_ready, at(i, G, max(n - 1, 0)))
                        for h in range(H1):
                            last = nc.tensor.matmul(bank[:, WORK + n % 2, 0:D], aT[:, n % 2, h, :],
                                                    v[:, n, h * D:(h + 1) * D], start=(h == 0), stop=(h == H1 - 1))
                        last.then_inc(out_done, 1)

                    for n in range(G):
                        pe.wait_ge(gate_ready, at(i, G, n + 1))
                        for j in range(2):
                            pe.wait_ge(decay_ready, at(i, 2 * G, max(2 * n + j - 1, 0)))
                            nc.tensor.matmul(bank[:, LOGDECAY + j, :], w.minus_after[:, :],
                                             gate[:, n % 2, j * (NB // 2):(j + 1) * (NB // 2), :, :].rearrange(
                                                 "p a h b -> p (a h b)"), start=True,
                                             stop=True).then_inc(logdecay_done, 1)
                        if n == 0:
                            pe.wait_ge(kept_by_scalar, at(i, PROJ // 2, PROJ // 2))
                            pe.wait_ge(kept_by_vector, at(i, PROJ // 2, PROJ // 2))
                        if n >= 1:
                            out_of(n - 1)
                        pe.wait_ge(level_ready, at(i, G, n + 1))
                        for j in range(2):
                            pe.wait_ge(weight_ready, at(i, 2 * G, max(2 * n + j - 1, 0)))
                            for c in range(NB // 2):
                                a = j * (NB // 2) + c
                                start = T - TB - TB * a
                                last = nc.tensor.matmul(
                                    bank[:, LEVEL + j, c * H1 * TB:(c + 1) * H1 * TB], w.band[:, start:start + T],
                                    level[:, n % 2, a, :, :].rearrange("p h b -> p (h b)"), start=True, stop=True)
                            last.then_inc(level_done, 1)
                        for j in range(2):
                            pe.wait_ge(aT_ready, at(i, 2 * G, max(2 * n + j - 1, 0)))
                            first = n * NB + j * (NB // 2)
                            nc.tensor.matmul(bank[:, SCORE + j, :], ln.xnT[:, n * T:(n + 1) * T],
                                             qT[:, first:first + NB // 2, :, :].rearrange("p a h b -> p (a h b)"),
                                             start=True, stop=True).then_inc(score_done, 1)
                    out_of(G - 1)



H = 16
SCORE, FLIP, WORK = 0, 4, 6
QUADS = H // 4


class Softmax:

    def __init__(self, core, sbuf, name, keys, bias=None):
        self.core, self.nc, self.keys, self.bias = core, core.nc, keys, bias
        self.p = sbuf(name + "_p", [P, 2, H, keys])
        self.peak = sbuf(name + "_peak", [P, 2, H])
        self.pT = sbuf(name + "_pT", [P, 2, H, T])
        self.scored = core.semaphore(name + "_scored")
        self.biased = core.semaphore(name + "_biased")
        self.peak_ready = core.semaphore(name + "_peak_ready")
        self.lowered = core.semaphore(name + "_lowered")
        self.exp_ready = core.semaphore(name + "_exp_ready")
        self.p_flipped = core.semaphore(name + "_p_flipped")
        self.pT_ready = core.semaphore(name + "_pT_ready")
        self.weighed = core.semaphore(name + "_weighed")

    def scores(self):
        return self.core.bank[:, SCORE:SCORE + QUADS, 0:4 * self.keys].rearrange("p g (j m) -> p g j m", m=self.keys)

    def lower_by_vector(self, dve, i, n):
        nc = self.nc
        p = self.p[:, n % 2, :, :]
        p4 = p.rearrange("p (g j) m -> p g j m", j=4)
        peak = self.peak[:, n % 2, :]
        dve.wait_ge(self.scored, at(i, G, n + 1))
        dve.wait_ge(self.p_flipped, at(i, G * QUADS, QUADS * max(n - 1, 0)))
        if self.bias is None:
            nc.vector.tensor_reduce(peak.rearrange("p (g j) -> p g j", j=4), self.scores(), AX.X,
                                    ALU.max).then_inc(self.peak_ready, 1)
            dve.wait_ge(self.peak_ready, at(i, G, n + 1))
            nc.vector.tensor_tensor(p4, self.scores(), peak.rearrange("p (g j) -> p g j", j=4).unsqueeze(3).to_broadcast(
                [P, QUADS, 4, self.keys]), ALU.subtract).then_inc(self.lowered, 1)
        else:
            nc.vector.tensor_tensor(p.rearrange("p h m -> p (h m)"),
                                    self.core.bank[:, SCORE:SCORE + QUADS, :].rearrange("p g c -> p (g c)"),
                                    self.bias[:, :, :].rearrange("p h m -> p (h m)"), ALU.add).then_inc(self.biased, 1)
            dve.wait_ge(self.biased, at(i, G, n + 1))
            nc.vector.tensor_reduce(peak, p, AX.X, ALU.max).then_inc(self.peak_ready, 1)
            dve.wait_ge(self.peak_ready, at(i, G, n + 1))
            nc.vector.tensor_tensor(p, p, peak.unsqueeze(2).to_broadcast([P, H, self.keys]),
                                    ALU.subtract).then_inc(self.lowered, 1)

    def banks_read(self):
        return self.lowered if self.bias is None else self.biased

    def exp_by_scalar(self, act, i, n):
        p = self.p[:, n % 2, :, :]
        act.wait_ge(self.lowered, at(i, G, n + 1))
        self.nc.scalar.activation(p, p, ACT.Exp).then_inc(self.exp_ready, 1)

    def flip_by_tensor(self, pe, i, n, kept):
        nc = self.nc
        pe.wait_ge(self.exp_ready, at(i, G, n + 1))
        for g in range(QUADS):
            kept(g)
            for j in range(4):
                last = nc.tensor.transpose(self.core.bank[0:self.keys, FLIP + g % 2, j * T:(j + 1) * T],
                                           self.p[:, n % 2, 4 * g + j, :], self.core.ident[:, :])
            last.then_inc(self.p_flipped, 1)

    def pT_by_scalar(self, act, i, n):
        act.wait_ge(self.weighed, at(i, G, max(n - 1, 0)))
        for g in range(QUADS):
            act.wait_ge(self.p_flipped, at(i, G * QUADS, QUADS * n + g + 1))
            self.nc.scalar.copy(self.pT[0:self.keys, n % 2, 4 * g:4 * g + 4, :].rearrange("m h t -> m (h t)"),
                                self.core.bank[0:self.keys, FLIP + g % 2, :]).then_inc(self.pT_ready, 1)



DH = D // H


def narrow_constants():
    e = np.arange(P)
    return (e[:, None] % 32 // DH == np.arange(4)[None, :]).astype(np.float32)


def narrow_weights(w, a, s):
    t = {}
    for name in ("q", "k", "v", "o"):
        t[name] = w.load(s, f"w_{s}_{name}", [P, D], a[f"{s}_w{name}T"])
    if s == "s2":
        t["bq"] = w.load(s, f"w_{s}_bq", [P, 1], a[f"{s}_bq"].unsqueeze(1))
        t["bk"] = w.load(s, f"w_{s}_bk", [P, 1], a[f"{s}_bk"].unsqueeze(1))
        t["bv"] = w.load(s, f"w_{s}_bv", [M, D], a[f"{s}_bv"].unsqueeze(0).to_broadcast([M, D]))
        t["bo"] = w.load(s, f"w_{s}_bo", [P, D], a[f"{s}_bo"].unsqueeze(0).to_broadcast([P, D]))
    t["head_of"] = w.load(s, f"w_{s}_head_of", [P, 4], a["head_of"])
    return t


def narrow_attention(nc, core, w, s, t, ctxT_dram=None, bias=None):
    cross = ctxT_dram is not None
    keys = M if cross else T
    with ExitStack() as local:
        core.local = local
        def sbuf(name, shape, dtype=F32):
            return local.enter_context(nc.sbuf_tensor(name, shape, dtype))

        ln = Norm(core, sbuf, s + "_ln")
        sm = Softmax(core, sbuf, s, keys, bias)
        source = sbuf(s + "_ctxT", [P, GM]) if cross else ln.xnT
        qT = sbuf(s + "_qT", [P, GT])
        kT = sbuf(s + "_kT", [P, G, 4, keys])
        v = sbuf(s + "_v", [P, G, H, DH + 1])
        inverse = sbuf(s + "_inverse", [P, 2, H])
        o = sbuf(s + "_o", [P, 2, D])
        oT = sbuf(s + "_oT", [P, 2, T])

        chain_v = core.semaphore(s + "_chain_v")
        q_done = core.semaphore(s + "_q_done")
        k_done = core.semaphore(s + "_k_done")
        v_done = core.semaphore(s + "_v_done")
        q_kept = core.semaphore(s + "_q_kept")
        k_kept = core.semaphore(s + "_k_kept")
        v_kept = core.semaphore(s + "_v_kept")
        inverse_ready = core.semaphore(s + "_inverse_ready")
        o_ready = core.semaphore(s + "_o_ready")
        o_flipped = core.semaphore(s + "_o_flipped")
        oT_ready = core.semaphore(s + "_oT_ready")
        out_done = core.semaphore(s + "_out_done")
        x_ready = core.semaphore(s + "_x_ready")
        x_biased = core.semaphore(s + "_x_biased")
        ones_ready = core.plain_semaphore(s + "_ones_ready")
        ctx_landed = core.plain_semaphore(s + "_ctx_landed")
        core.start_stage(w.landed[s], w.count[s])
        bank = core.bank
        OT, OUT = 2 * D, 3 * D

        with nc.Block() as block:
            if cross:
                @block.sync
                def _(sp):
                    with sp.Fori(0, GROUPS) as i:
                        sp.wait_ge(v_done, at(i, 1, 0))
                        sp.dma_start(source[:, :], ctxT_dram[:, bass.ts(i, GM)]).then_inc(ctx_landed, 16)

            @block.gpsimd
            def _(pool):
                nc.gpsimd.memset(v[:, :, :, :], 1.0).then_inc(ones_ready, 1)
                with pool.Fori(0, GROUPS) as i:
                    ln.rstd_by_gpsimd(pool, i)
                    if cross:
                        pool.wait_ge(ln.xn_ready, at(i, G, G))
                        x = core.x[:, bass.ts(i, G), :]
                        nc.gpsimd.tensor_tensor(x, x, t["bo"][:, :].unsqueeze(1).to_broadcast([P, G, D]),
                                                ALU.add).then_inc(x_biased, 1)

            @block.scalar
            def _(act):
                nc.scalar.preload_act_table_set("exp_and_others")
                with act.Fori(0, GROUPS) as i:
                    ln.xnT_by_scalar(act, i, bank[:, WORK, :])
                    for n in range(G + 2):
                        if n >= 2:
                            act.wait_ge(o_flipped, at(i, G, n - 1))
                            nc.scalar.copy(oT[:, n % 2, :], bank[:, WORK + n % 2, OT:OT + T]).then_inc(oT_ready, 1)
                        if 1 <= n <= G:
                            sm.pT_by_scalar(act, i, n - 1)
                        if n < G:
                            sm.exp_by_scalar(act, i, n)

            @block.vector
            def _(dve):
                dve.wait_ge(ones_ready, 1)
                with dve.Fori(0, GROUPS) as i:
                    chain = Chain(dve, chain_v, i, 1)
                    ln.norm_by_vector(dve, i, chain)
                    dve.wait_ge(q_done, at(i, 1, 1))
                    if cross:
                        nc.vector.tensor_scalar(qT[:, :], bank[:, WORK + 1, :], t["bq"][:, 0:1], float(DH) ** -0.5,
                                                ALU.add, ALU.mult).then_inc(q_kept, 1)
                    else:
                        nc.vector.tensor_scalar(qT[:, :], bank[:, WORK + 1, :], float(DH) ** -0.5, None,
                                                ALU.mult).then_inc(q_kept, 1)
                    dve.wait_ge(k_done, at(i, 1, 1))
                    for j in range(4):
                        k_in = bank[:, WORK, 0:G * keys].rearrange("p (n m) -> p n m", m=keys)
                        if cross:
                            last = nc.vector.tensor_scalar(kT[:, :, j, :], k_in, t["bk"][:, 0:1],
                                                           t["head_of"][:, j:j + 1], ALU.add, ALU.mult)
                        else:
                            last = nc.vector.tensor_scalar(kT[:, :, j, :], k_in, t["head_of"][:, j:j + 1], None,
                                                           ALU.mult)
                    last.then_inc(k_kept, 1)
                    dve.wait_ge(v_done, at(i, 1, 1))
                    v_in = bank[0:keys, WORK + 1, :].rearrange("m (n h d) -> m n h d", h=H, d=DH)
                    v_out = v[0:keys, :, :, 0:DH]
                    if cross:
                        nc.vector.tensor_tensor(v_out, v_in, t["bv"][:, :].rearrange("m (h d) -> m h d", d=DH).unsqueeze(
                            1).to_broadcast([M, G, H, DH]), ALU.add).then_inc(v_kept, 1)
                    else:
                        nc.vector.tensor_copy(v_out, v_in).then_inc(v_kept, 1)
                    for n in range(G + 2):
                        if n < G:
                            sm.lower_by_vector(dve, i, n)
                        if n >= 2:
                            dve.wait_ge(out_done, at(i, G, n - 1))
                            if cross:
                                dve.wait_ge(x_biased, at(i, 1, 1))
                            x = core.x[:, bass.ds(i * G + (n - 2), 1), :]
                            nc.vector.tensor_tensor(x, bank[:, WORK + n % 2, OUT:OUT + D].unsqueeze(1), x,
                                                    ALU.add).then_inc(x_ready, 1)
                        if 1 <= n <= G:
                            m = n - 1
                            out = bank[:, WORK + m % 2, 0:H * (DH + 1)].rearrange("p (h d) -> p h d", d=DH + 1)
                            dve.wait_ge(sm.weighed, at(i, G, m + 1))
                            nc.vector.reciprocal(inverse[:, m % 2, :], out[:, :, DH]).then_inc(inverse_ready, 1)
                            dve.wait_ge(inverse_ready, at(i, G, m + 1))
                            nc.vector.tensor_tensor(
                                o[:, m % 2, :].rearrange("p (h d) -> p h d", d=DH), out[:, :, 0:DH],
                                inverse[:, m % 2, :].unsqueeze(2).to_broadcast([P, H, DH]),
                                ALU.mult).then_inc(o_ready, 1)
                    chain.end()

            @block.tensor
            def _(pe):
                with pe.Fori(0, GROUPS) as i:
                    pe.wait_ge(x_ready, at(i, G, 0))
                    ln.flip_by_tensor(pe, i, bank[:, WORK, :])
                    pe.wait_ge(ln.xnT_ready, at(i, 1, 1))
                    nc.tensor.matmul(bank[:, WORK + 1, :], t["q"][:, :], ln.xnT[:, :], start=True,
                                     stop=True).then_inc(q_done, 1)
                    if cross:
                        pe.wait_ge(ctx_landed, (i + 1) * 16)
                    nc.tensor.matmul(bank[:, WORK, 0:G * keys], t["k"][:, :], source[:, :], start=True,
                                     stop=True).then_inc(k_done, 1)
                    pe.wait_ge(q_kept, at(i, 1, 1))
                    for n in range(G):
                        last = nc.tensor.matmul(bank[0:keys, WORK + 1, n * D:(n + 1) * D],
                                                source[:, n * keys:(n + 1) * keys], t["v"][:, :], start=True, stop=True)
                    last.then_inc(v_done, 1)
                    pe.wait_ge(k_kept, at(i, 1, 1))
                    for n in range(G + 2):
                        if n < G:
                            pe.wait_ge(sm.banks_read(), at(i, G, n))
                            for g in range(QUADS):
                                rows = slice(32 * g, 32 * g + 32)
                                last = nc.tensor.matmul(bank[:, SCORE + g, 0:4 * keys], qT[rows, n * T:(n + 1) * T],
                                                        kT[rows, n, :, :].rearrange("p j m -> p (j m)"), start=True,
                                                        stop=True)
                            last.then_inc(sm.scored, 1)
                        if n >= 2:
                            pe.wait_ge(o_ready, at(i, G, n - 1))
                            nc.tensor.transpose(bank[:, WORK + n % 2, OT:OT + T], o[:, n % 2, :],
                                                core.ident[:, :]).then_inc(o_flipped, 1)
                        if 1 <= n <= G:
                            sm.flip_by_tensor(pe, i, n - 1, lambda g: pe.wait_ge(
                                sm.pT_ready, at(i, G * QUADS, max(QUADS * (n - 1) + g - 1, 0))))
                        if n >= 2:
                            pe.wait_ge(oT_ready, at(i, G, n - 1))
                            nc.tensor.matmul(bank[:, WORK + n % 2, OUT:OUT + D], oT[:, n % 2, :], t["o"][:, :],
                                             start=True, stop=True).then_inc(out_done, 1)
                        if 1 <= n <= G:
                            m = n - 1
                            pe.wait_ge(v_kept, at(i, 1, 1))
                            pe.wait_ge(x_ready, at(i, G, max(m - 1, 0)))
                            pe.wait_ge(sm.pT_ready, at(i, G * QUADS, QUADS * (m + 1)))
                            for h in range(H):
                                last = nc.tensor.matmul(bank[:, WORK + m % 2, h * (DH + 1):(h + 1) * (DH + 1)],
                                                        sm.pT[0:keys, m % 2, h, :], v[0:keys, m, h, :], start=True,
                                                        stop=True)
                            last.then_inc(sm.weighed, 1)



E3, HID = 8, 256
CHUNKS = HID // P


def stage3_weights(w, a):
    w.s3_norm = w.load("s3", "w_s3_norm", [P, 1], a["s3_norm"].unsqueeze(1))
    w.s3_gateT = w.load("s3", "w_s3_gateT", [P, E3], a["s3_gateT"])
    w.s3_w1T = w.load("s3", "w_s3_w1T", [P, E3 * HID], a["s3_w1T"])
    w.s3_b1 = w.load("s3", "w_s3_b1", [P, E3 * CHUNKS], a["s3_b1T"])
    w.s3_w2T = w.load("s3", "w_s3_w2T", [P, E3 * CHUNKS, D], a["s3_w2T"].rearrange("(c p) d -> p c d", p=P))
    w.s3_b2 = w.load("s3", "w_s3_b2", [E3, D], a["s3_b2"])
    w.s3_count = w.load("s3", "w_s3_count", [P, E3], a["count"][0:E3].unsqueeze(0).to_broadcast([P, E3]))


def stage3(nc, core, w):
    with ExitStack() as local:
        core.local = local
        def sbuf(name, shape, dtype=F32):
            return local.enter_context(nc.sbuf_tensor(name, shape, dtype))

        ln = Norm(core, sbuf, "s3_ln")
        rms = Moments(core, sbuf, "s3_rms", RMS_EPS)
        tokens = sbuf("s3_tokens", [P, G, D])
        square = sbuf("s3_square", [P, G])
        hT = sbuf("s3_hT", [P, 2, CHUNKS, GT])
        best = sbuf("s3_best", [P, G, 8])
        where = sbuf("s3_where", [P, G, 8], U32)
        index = sbuf("s3_index", [P, G, 2])
        logits = sbuf("s3_logits", [P, G, E3])
        gap = sbuf("s3_gap", [P, G])
        share = sbuf("s3_share", [P, G, 2])
        combine = sbuf("s3_combine", [P, G, E3])
        second = sbuf("s3_second", [P, G, E3])
        combineT = sbuf("s3_combineT", [E3, GT])
        total = sbuf("s3_total", [P, G, D])

        sem = core.semaphore
        chain_v = sem("s3_chain_v")
        square_ready = sem("s3_square_ready")
        tokens_ready = sem("s3_tokens_ready")
        logits_done = sem("s3_logits_done")
        gap_ready = sem("s3_gap_ready")
        tanh_ready = sem("s3_tanh_ready")
        combine_ready = sem("s3_combine_ready")
        combine_flipped = sem("s3_combine_flipped")
        combineT_ready = sem("s3_combineT_ready")
        offset_done = sem("s3_offset_done")
        total_started = sem("s3_total_started")
        hidden_done = sem("s3_hidden_done")
        hT_ready = sem("s3_hT_ready")
        expert_done = sem("s3_expert_done")
        added = sem("s3_added")
        x_ready = sem("s3_x_ready")
        core.start_stage(w.landed["s3"], w.count["s3"])
        bank = core.bank
        MISC, LOGITS, HIDDEN, OUT = 0, 1, 2, 6

        with nc.Block() as block:
            @block.gpsimd
            def _(pool):
                with pool.Fori(0, GROUPS) as i:
                    ln.rstd_by_gpsimd(pool, i)
                    rms.rstd_by_gpsimd(pool, i)
                    pool.wait_ge(total_started, at(i, 1, 1))
                    pool.wait_ge(added, at(i, E3 * G, E3 * G))
                    x = core.x[:, bass.ts(i, G), :]
                    nc.gpsimd.tensor_tensor(x, x, total[:, :, :], ALU.add).then_inc(x_ready, 1)

            @block.scalar
            def _(act):
                nc.scalar.preload_act_table_set("gelu_and_others")
                with act.Fori(0, GROUPS) as i:
                    act.wait_ge(ln.flipped, at(i, 1, 1))
                    nc.scalar.activation(ln.xnT[:, :], bank[:, MISC, :], ACT.Copy,
                                         scale=w.s3_norm[:, 0:1]).then_inc(ln.xnT_ready, 1)
                    act.wait_ge(gap_ready, at(i, 1, 1))
                    nc.scalar.activation(gap[:, :], gap[:, :], ACT.Tanh, scale=0.5).then_inc(tanh_ready, 1)
                    act.wait_ge(combine_flipped, at(i, 1, 1))
                    nc.scalar.copy(combineT[:, :], bank[0:E3, MISC, :]).then_inc(combineT_ready, 1)
                    for e in range(E3):
                        act.wait_ge(expert_done, at(i, E3, max(e - 1, 0)))
                        for c in range(CHUNKS):
                            k = e * CHUNKS + c
                            act.wait_ge(hidden_done, at(i, E3 * CHUNKS, k + 1))
                            nc.scalar.activation(hT[:, e % 2, c, :], bank[:, HIDDEN + k % 4, :], ACT.Gelu,
                                                 bias=w.s3_b1[:, k:k + 1]).then_inc(hT_ready, 1)

            @block.vector
            def _(dve):
                with dve.Fori(0, GROUPS) as i:
                    chain = Chain(dve, chain_v, i, 9)
                    ln.norm_by_vector(dve, i, chain)
                    dve.wait_ge(ln.xn_ready, at(i, G, G))
                    for n in range(G):
                        last = nc.vector.bn_stats(rms.stats[:, n, :], ln.xn[:, n, :])
                    chain.link(last)
                    core.hold_vector()
                    for n in range(G):
                        last = nc.vector.bn_aggr(rms.moments[:, n, :], rms.stats[:, n, :])
                    chain.link(last)
                    chain.link(nc.vector.tensor_tensor(square[:, :], rms.moments[:, :, 0], rms.moments[:, :, 0], ALU.mult))
                    nc.vector.tensor_tensor(rms.moments[:, :, 1], rms.moments[:, :, 1], square[:, :],
                                            ALU.add).then_inc(rms.moments_ready, 1)
                    dve.wait_ge(rms.rstd_ready, at(i, 1, 1))
                    for n in range(G):
                        nc.vector.tensor_scalar(tokens[:, n, :], ln.xn[:, n, :], rms.rstd[:, n:n + 1], None,
                                                ALU.mult).then_inc(tokens_ready, 1)

                    dve.wait_ge(logits_done, at(i, 1, 1))
                    chain.link(nc.vector.tensor_copy(
                        logits[:, :, :], bank[:, LOGITS, 0:G * E3].rearrange("p (n e) -> p n e", e=E3)))
                    core.hold_vector()
                    for n in range(G):
                        last = nc.vector.max(best[:, n, :], logits[:, n, :])
                    chain.link(last)
                    nc.vector.tensor_tensor(gap[:, :], best[:, :, 0], best[:, :, 1], ALU.subtract).then_inc(gap_ready, 1)
                    core.hold_vector()
                    for n in range(G):
                        last = nc.vector.max_index(where[:, n, :], best[:, n, :], logits[:, n, :])
                    chain.link(last)
                    nc.vector.tensor_copy(index[:, :, :], where[:, :, 0:2])
                    dve.wait_ge(tanh_ready, at(i, 1, 1))
                    nc.vector.tensor_scalar(share[:, :, 0], gap[:, :], 0.5, 0.5, ALU.mult, ALU.add)
                    chain.link(nc.vector.tensor_scalar(share[:, :, 1], gap[:, :], -0.5, 0.5, ALU.mult, ALU.add))
                    for n in range(G):
                        last = nc.vector.tensor_scalar(second[:, n, :], w.s3_count[:, :], index[:, n, 1:2],
                                                       share[:, n, 1:2], ALU.is_equal, ALU.mult)
                        last = nc.vector.tensor_scalar(combine[:, n, :], w.s3_count[:, :], index[:, n, 0:1],
                                                       share[:, n, 0:1], ALU.is_equal, ALU.mult)
                    chain.link(last)
                    nc.vector.tensor_tensor(combine[:, :, :], combine[:, :, :], second[:, :, :],
                                            ALU.add).then_inc(combine_ready, 1)

                    dve.wait_ge(offset_done, at(i, 1, 1))
                    dve.wait_ge(x_ready, at(i, 1, 0))
                    nc.vector.tensor_tensor(total[:, :, :], bank[:, LOGITS, :].rearrange("p (n d) -> p n d", d=D),
                                            ln.xn[:, :, :], ALU.add).then_inc(total_started, 1)
                    dve.wait_ge(total_started, at(i, 1, 1))
                    for e in range(E3):
                        dve.wait_ge(expert_done, at(i, E3, e + 1))
                        if e > 0:
                            dve.wait_ge(added, at(i, E3 * G, e * G))
                        for n in range(G):
                            nc.vector.scalar_tensor_tensor(
                                out=total[:, n, :], in0=bank[:, OUT + e % 2, n * D:(n + 1) * D],
                                scalar=combine[:, n, e:e + 1], in1=total[:, n, :], op0=ALU.mult,
                                op1=ALU.add).then_inc(added, 1)
                    chain.end()

            @block.tensor
            def _(pe):
                with pe.Fori(0, GROUPS) as i:
                    pe.wait_ge(combineT_ready, at(i, 1, 0))
                    for n in range(G):
                        pe.wait_ge(tokens_ready, at(i, G, n + 1))
                        last = nc.tensor.transpose(bank[:, MISC, n * T:(n + 1) * T], tokens[:, n, :], core.ident[:, :])
                    last.then_inc(ln.flipped, 1)
                    pe.wait_ge(ln.xnT_ready, at(i, 1, 1))
                    pe.wait_ge(total_started, at(i, 1, 0))
                    for n in range(G):
                        last = nc.tensor.matmul(bank[:, LOGITS, n * E3:(n + 1) * E3], ln.xnT[:, n * T:(n + 1) * T],
                                                w.s3_gateT[:, :], start=True, stop=True)
                    last.then_inc(logits_done, 1)

                    def hidden_of(e):
                        for c in range(CHUNKS):
                            k = e * CHUNKS + c
                            pe.wait_ge(hT_ready, at(i, E3 * CHUNKS, max(k - 3, 0)))
                            nc.tensor.matmul(bank[:, HIDDEN + k % 4, :], w.s3_w1T[:, k * P:(k + 1) * P], ln.xnT[:, :],
                                             start=True, stop=True).then_inc(hidden_done, 1)

                    def output_of(e):
                        pe.wait_ge(hT_ready, at(i, E3 * CHUNKS, (e + 1) * CHUNKS))
                        pe.wait_ge(added, at(i, E3 * G, max(e - 1, 0) * G))
                        for n in range(G):
                            for c in range(CHUNKS):
                                last = nc.tensor.matmul(bank[:, OUT + e % 2, n * D:(n + 1) * D],
                                                        hT[:, e % 2, c, n * T:(n + 1) * T],
                                                        w.s3_w2T[:, e * CHUNKS + c, :], start=(c == 0),
                                                        stop=(c == CHUNKS - 1))
                        last.then_inc(expert_done, 1)

                    hidden_of(0)
                    hidden_of(1)
                    for n in range(G):
                        pe.wait_ge(combine_ready, at(i, 1, 1))
                        last = nc.tensor.transpose(bank[0:E3, MISC, n * T:(n + 1) * T], combine[:, n, :],
                                                   core.ident[:, :])
                    last.then_inc(combine_flipped, 1)
                    pe.wait_ge(combineT_ready, at(i, 1, 1))
                    for n in range(G):
                        last = nc.tensor.matmul(bank[:, LOGITS, n * D:(n + 1) * D], combineT[:, n * T:(n + 1) * T],
                                                w.s3_b2[:, :], start=True, stop=True)
                    last.then_inc(offset_done, 1)
                    for e in range(E3):
                        if e >= 1 and e + 1 < E3:
                            hidden_of(e + 1)
                        output_of(e)



FILTERS, TAPS, RES = 4, 101, 64
SPAN = 2 * T - 1


def ramp_constants():
    signal = np.linspace(0.0, 1.0, RES).astype(np.float32)
    distance = np.abs(np.arange(SPAN) - (T - 1)).astype(np.float32) / np.float32(T - 1)
    row = np.clip(np.round(distance * (RES - 1)).astype(np.int64), 0, RES - 1)
    before = row[None, :] - np.arange(TAPS)[:, None]
    return np.where(before >= 0, signal[np.maximum(before, 0)], 0.0).astype(np.float32)


def bias_weights(w, a):
    w.ramp = w.load("s4", "w_ramp", [TAPS, SPAN], a["ramp"])
    w.coeffsT = w.load("s4", "w_coeffsT", [TAPS, FILTERS], a["s4_coeffsT"])
    w.wposT = w.load("s4", "w_wposT", [FILTERS, H], a["s4_wposT"])
    w.flip = w.load("s4", "w_flip", [P, P], a["flip"])
    w.bias = w.core.sbuf("pos_bias", [P, H, T])


def make_bias(nc, core, w, bias_dram):
    with ExitStack() as local:
        core.local = local
        filtered = local.enter_context(nc.sbuf_tensor("filtered", [FILTERS, SPAN], F32))
        by_head = local.enter_context(nc.sbuf_tensor("by_head", [H, SPAN], F32))
        reversed_bias = local.enter_context(nc.sbuf_tensor("reversed_bias", [P, H, T], F32))
        made = core.plain_semaphore("bias_made")
        kept = core.plain_semaphore("bias_kept")
        spilled = core.plain_semaphore("bias_spilled")
        landed = core.plain_semaphore("bias_landed")
        core.start_stage(w.landed["s4"], w.count["s4"])
        with nc.Block() as block:
            @block.tensor
            def _(pe):
                nc.tensor.matmul(core.bank[0:FILTERS, 0, 0:SPAN], w.coeffsT[:, :], w.ramp[:, :], start=True,
                                 stop=True).then_inc(made, 1)
                pe.wait_ge(kept, 1)
                nc.tensor.matmul(core.bank[0:H, 1, 0:SPAN], w.wposT[:, :], filtered[:, :], start=True,
                                 stop=True).then_inc(made, 1)
                pe.wait_ge(landed, 16)
                for g in range(4):
                    nc.tensor.matmul(core.bank[:, 2 + g, :], w.flip[:, :],
                                     reversed_bias[:, 4 * g:4 * g + 4, :].rearrange("p h t -> p (h t)"), start=True,
                                     stop=True).then_inc(made, 1)

            @block.vector
            def _(dve):
                dve.wait_ge(made, 1)
                nc.vector.tensor_copy(filtered[:, :], core.bank[0:FILTERS, 0, 0:SPAN]).then_inc(kept, 1)
                dve.wait_ge(made, 2)
                nc.vector.tensor_copy(by_head[:, :], core.bank[0:H, 1, 0:SPAN]).then_inc(kept, 1)
                for g in range(4):
                    dve.wait_ge(made, 3 + g)
                    nc.vector.tensor_copy(w.bias[:, 4 * g:4 * g + 4, :].rearrange("p h t -> p (h t)"),
                                          core.bank[:, 2 + g, :])

            @block.sync
            def _(sp):
                sp.wait_ge(kept, 2)
                sp.dma_start(bias_dram[:, :], by_head[:, :]).then_inc(spilled, 16)
                sp.wait_ge(spilled, 16)
                runs = bass.AP(bias_dram.tensor, 0, [[1, P], [SPAN, H], [1, T]])
                sp.dma_start(reversed_bias[:, :, :], runs).then_inc(landed, 16)



DH5 = 64
PAIRS = H * DH5 // P


def place_of(h):
    return 8 * (h // 8) + 4 * (h % 2) + h % 8 // 2


def stage5_weights(w, a):
    w.s5_gamma = w.load("s5", "w_s5_gamma", [P, 1], a["s5_gamma"].unsqueeze(1))
    w.s5_beta = w.load("s5", "w_s5_beta", [P, 1], a["s5_beta"].unsqueeze(1))
    w.s5_wq = w.load("s5", "w_s5_q", [P, H * DH5], a["s5_wq"])
    w.s5_wkv = w.load("s5", "w_s5_kv", [P, 2 * H * DH5], a["s5_wkv"])
    w.s5_wo = w.load("s5", "w_s5_o", [P, PAIRS, D], a["s5_wo"].rearrange("(c p) d -> p c d", p=P))
    w.s5_bo = w.load("s5", "w_s5_bo", [P, D], a["s5_bo"].unsqueeze(0).to_broadcast([P, D]))
    w.s5_gate = w.load("s5", "w_s5_gate", [P, 1], a["s5_gate"].unsqueeze(0).to_broadcast([P, 1]))


def stage5(nc, core, w, ctxT_dram):
    with ExitStack() as local:
        core.local = local
        def sbuf(name, shape, dtype=F32):
            return local.enter_context(nc.sbuf_tensor(name, shape, dtype))

        ln = Norm(core, sbuf, "s5_ln")
        ln2 = Moments(core, sbuf, "s5_ln2")
        sm = Softmax(core, sbuf, "s5", M)
        xn2 = sbuf("s5_xn2", [P, G, D])
        ctxT = sbuf("s5_ctxT", [P, GM])
        qT = sbuf("s5_qT", [P, PAIRS, GT])
        kT = sbuf("s5_kT", [P, PAIRS, GM])
        v = sbuf("s5_v", [P, G, H * DH5])
        total = sbuf("s5_total", [P, 2, H])
        inverse = sbuf("s5_inverse", [P, 2, H])
        o = sbuf("s5_o", [P, H * DH5])
        oT = sbuf("s5_oT", [P, PAIRS, T])

        sem = core.semaphore
        chain_v = sem("s5_chain_v")
        xn2_ready = sem("s5_xn2_ready")
        projected = sem("s5_projected")
        kept_by_scalar = sem("s5_kept_by_scalar")
        kept_by_vector = sem("s5_kept_by_vector")
        total_ready = sem("s5_total_ready")
        inverse_ready = sem("s5_inverse_ready")
        o_ready = sem("s5_o_ready")
        o_flipped = sem("s5_o_flipped")
        oT_ready = sem("s5_oT_ready")
        out_done = sem("s5_out_done")
        x_ready = sem("s5_x_ready")
        x_biased = sem("s5_x_biased")
        ctx_landed = core.plain_semaphore("s5_ctx_landed")
        tanh_ready = core.plain_semaphore("s5_tanh_ready")
        core.start_stage(w.landed["s5"], w.count["s5"])
        bank = core.bank
        PROJ = 2 * PAIRS + 2 * G

        with nc.Block() as block:
            @block.scalar
            def _(act):
                nc.scalar.activation(w.s5_gate[:, :], w.s5_gate[:, :], ACT.Tanh).then_inc(tanh_ready, 1)

            @block.vector
            def _(dve):
                dve.wait_ge(tanh_ready, 1)
                nc.vector.tensor_scalar(w.s5_wo[:, :, :], w.s5_wo[:, :, :], w.s5_gate[:, 0:1], None, ALU.mult)
                nc.vector.tensor_scalar(w.s5_bo[:, :], w.s5_bo[:, :], w.s5_gate[:, 0:1], None, ALU.mult)

        def keep(copy, k):
            work = bank[:, WORK + k % 2, :]
            if k < PAIRS:
                return copy(qT[:, k, :], work, float(DH5) ** -0.5)
            if k < 2 * PAIRS:
                return copy(kT[:, k - PAIRS, :], work[:, 0:GM], 1.0)
            n, c = (k - 2 * PAIRS) // 2, (k - 2 * PAIRS) % 2
            return copy(v[0:M, n, c * 512:(c + 1) * 512], work[0:M, :], 1.0)

        with nc.Block() as block:
            @block.sync
            def _(sp):
                with sp.Fori(0, GROUPS) as i:
                    sp.wait_ge(projected, at(i, PROJ, 0))
                    sp.dma_start(ctxT[:, :], ctxT_dram[:, bass.ts(i, GM)]).then_inc(ctx_landed, 16)

            @block.gpsimd
            def _(pool):
                with pool.Fori(0, GROUPS) as i:
                    ln.rstd_by_gpsimd(pool, i)
                    ln2.rstd_by_gpsimd(pool, i)
                    pool.wait_ge(ln.xn_ready, at(i, G, G))
                    x = core.x[:, bass.ts(i, G), :]
                    nc.gpsimd.tensor_tensor(x, x, w.s5_bo[:, :].unsqueeze(1).to_broadcast([P, G, D]),
                                            ALU.add).then_inc(x_biased, 1)

            @block.scalar
            def _(act):
                def copy(out, source, scale):
                    return nc.scalar.activation(out, source, ACT.Copy, scale=scale)

                nc.scalar.preload_act_table_set("exp_and_others")
                with act.Fori(0, GROUPS) as i:
                    act.wait_ge(ln.flipped, at(i, 1, 1))
                    nc.scalar.activation(ln.xnT[:, :], bank[:, WORK, :], ACT.Identity, bias=w.s5_beta[:, 0:1],
                                         scale=w.s5_gamma[:, 0:1]).then_inc(ln.xnT_ready, 1)
                    for k in range(0, PROJ, 2):
                        act.wait_ge(projected, at(i, PROJ, k + 1))
                        keep(copy, k).then_inc(kept_by_scalar, 1)
                    for n in range(G + 2):
                        if n >= 2:
                            for c in range(2):
                                act.wait_ge(o_flipped, at(i, 2 * G, 2 * (n - 2) + c + 1))
                                nc.scalar.copy(oT[:, 4 * c:4 * c + 4, :].rearrange("p c t -> p (c t)"),
                                               bank[:, FLIP + c, :]).then_inc(oT_ready, 1)
                        if 1 <= n <= G:
                            sm.pT_by_scalar(act, i, n - 1)
                        if n < G:
                            sm.exp_by_scalar(act, i, n)

            @block.vector
            def _(dve):
                def copy(out, source, scale):
                    return nc.vector.tensor_scalar(out, source, scale, None, ALU.mult)

                with dve.Fori(0, GROUPS) as i:
                    chain = Chain(dve, chain_v, i, 2)
                    ln.norm_by_vector(dve, i, chain)
                    dve.wait_ge(ln.xn_ready, at(i, G, G))
                    ln2.moments_by_vector(chain, lambda n: ln.xn[:, n, :])
                    ln2.scaled_by_vector(dve, i, xn2, lambda n: ln.xn[:, n, :], xn2_ready)
                    for k in range(1, PROJ, 2):
                        dve.wait_ge(projected, at(i, PROJ, k + 1))
                        keep(copy, k).then_inc(kept_by_vector, 1)
                    for n in range(G + 2):
                        if n < G:
                            sm.lower_by_vector(dve, i, n)
                        if n >= 2:
                            dve.wait_ge(out_done, at(i, G, n - 1))
                            dve.wait_ge(x_biased, at(i, 1, 1))
                            x = core.x[:, bass.ds(i * G + (n - 2), 1), :]
                            nc.vector.tensor_tensor(x, bank[:, WORK, 0:D].unsqueeze(1), x, ALU.add).then_inc(x_ready, 1)
                        if 1 <= n <= G:
                            m = n - 1
                            dve.wait_ge(sm.exp_ready, at(i, G, m + 1))
                            nc.vector.tensor_reduce(total[:, m % 2, :], sm.p[:, m % 2, :, :], AX.X,
                                                    ALU.add).then_inc(total_ready, 1)
                            dve.wait_ge(total_ready, at(i, G, m + 1))
                            nc.vector.reciprocal(inverse[:, m % 2, :], total[:, m % 2, :]).then_inc(inverse_ready, 1)
                            dve.wait_ge(inverse_ready, at(i, G, m + 1))
                            dve.wait_ge(sm.weighed, at(i, G, m + 1))
                            for c in range(2):
                                nc.vector.tensor_tensor(
                                    o[:, c * 512:(c + 1) * 512].rearrange("p (j r d) -> p j r d", r=2, d=DH5),
                                    bank[:, WORK + c, :].rearrange("p (j r d) -> p j r d", r=2, d=DH5),
                                    inverse[:, m % 2, 8 * c:8 * c + 8].rearrange("p (r j) -> p j r", r=2).unsqueeze(
                                        3).to_broadcast([P, 4, 2, DH5]), ALU.mult).then_inc(o_ready, 1)
                    chain.end()

            @block.tensor
            def _(pe):
                with pe.Fori(0, GROUPS) as i:
                    pe.wait_ge(x_ready, at(i, G, 0))
                    for n in range(G):
                        pe.wait_ge(xn2_ready, at(i, G, n + 1))
                        last = nc.tensor.transpose(bank[:, WORK, n * T:(n + 1) * T], xn2[:, n, :], core.ident[:, :])
                    last.then_inc(ln.flipped, 1)
                    pe.wait_ge(ln.xnT_ready, at(i, 1, 1))
                    for k in range(PROJ):
                        if k >= 2:
                            pe.wait_ge(kept_by_vector if k % 2 else kept_by_scalar, at(i, PROJ // 2, k // 2))
                        if k == PAIRS:
                            pe.wait_ge(ctx_landed, (i + 1) * 16)
                        work = bank[:, WORK + k % 2, :]
                        if k < PAIRS:
                            last = nc.tensor.matmul(work, w.s5_wq[:, k * P:(k + 1) * P], ln.xnT[:, :], start=True,
                                                    stop=True)
                        elif k < 2 * PAIRS:
                            last = nc.tensor.matmul(work[:, 0:GM], w.s5_wkv[:, (k - PAIRS) * P:(k - PAIRS + 1) * P],
                                                    ctxT[:, :], start=True, stop=True)
                        else:
                            n, c = (k - 2 * PAIRS) // 2, (k - 2 * PAIRS) % 2
                            column = H * DH5 + c * 512
                            last = nc.tensor.matmul(work[0:M, :], ctxT[:, n * M:(n + 1) * M],
                                                    w.s5_wkv[:, column:column + 512], start=True, stop=True)
                        last.then_inc(projected, 1)
                    pe.wait_ge(kept_by_scalar, at(i, PROJ // 2, PROJ // 2))
                    pe.wait_ge(kept_by_vector, at(i, PROJ // 2, PROJ // 2))
                    for n in range(G + 2):
                        if n < G:
                            pe.wait_ge(sm.lowered, at(i, G, n))
                            for h in range(H):
                                rows = slice(DH5 * (h % 2), DH5 * (h % 2) + DH5)
                                g, j = place_of(h) // 4, place_of(h) % 4
                                last = nc.tensor.matmul(bank[:, SCORE + g, j * M:(j + 1) * M],
                                                        qT[rows, h // 2, n * T:(n + 1) * T],
                                                        kT[rows, h // 2, n * M:(n + 1) * M], start=True, stop=True)
                            last.then_inc(sm.scored, 1)
                        if n >= 2:
                            pe.wait_ge(o_ready, at(i, 2 * G, 2 * (n - 1)))
                            for c in range(2):
                                for j in range(4):
                                    pair = 4 * c + j
                                    last = nc.tensor.transpose(bank[:, FLIP + c, j * T:(j + 1) * T],
                                                               o[:, pair * P:(pair + 1) * P], core.ident[:, :])
                                last.then_inc(o_flipped, 1)
                        if 1 <= n <= G:
                            def kept(g):
                                if g < 2:
                                    pe.wait_ge(oT_ready, at(i, 2 * G, max(2 * (n - 2) + g + 1, 0) if n >= 2 else 0))
                                else:
                                    pe.wait_ge(sm.pT_ready, at(i, G * QUADS, QUADS * (n - 1) + g - 1))
                            sm.flip_by_tensor(pe, i, n - 1, kept)
                        if n >= 2:
                            pe.wait_ge(oT_ready, at(i, 2 * G, 2 * (n - 1)))
                            for c in range(PAIRS):
                                last = nc.tensor.matmul(bank[:, WORK, 0:D], oT[:, c, :], w.s5_wo[:, c, :],
                                                        start=(c == 0), stop=(c == PAIRS - 1))
                            last.then_inc(out_done, 1)
                        if 1 <= n <= G:
                            m = n - 1
                            pe.wait_ge(sm.pT_ready, at(i, G * QUADS, QUADS * (m + 1)))
                            for h in list(range(8, H)) + list(range(8)):
                                if h == 0:
                                    pe.wait_ge(x_ready, at(i, G, m))
                                last = nc.tensor.matmul(bank[:, WORK + h // 8, h % 8 * DH5:(h % 8 + 1) * DH5],
                                                        sm.pT[0:M, m % 2, place_of(h), :],
                                                        v[0:M, m, h * DH5:(h + 1) * DH5], start=True, stop=True)
                            last.then_inc(sm.weighed, 1)



E6 = 16
SHARED = 4
EXP6 = 2 * P


def stage6_weights(w, a):
    w.s6_routerT = w.load("s6", "w_s6_routerT", [P, E6], a["s6_routerT"])
    w.s6_count = w.load("s6", "w_s6_count", [P, E6], a["count"].unsqueeze(0).to_broadcast([P, E6]))
    w.s6_gateup = w.load("s6", "w_s6_gateup", [P, E6, EXP6], a["s6_gateup"].rearrange("e d f -> d e f"))
    w.s6_down = w.load("s6", "w_s6_down", [P, E6, D], a["s6_down"].rearrange("e f d -> f e d"))
    w.s6_sgateT = w.load("s6", "w_s6_sgateT", [P, SHARED * P], a["s6_sgateT"])
    w.s6_supT = w.load("s6", "w_s6_supT", [P, SHARED * P], a["s6_supT"])
    w.s6_sdownT = w.load("s6", "w_s6_sdownT", [P, SHARED, D], a["s6_sdownT"].rearrange("(c p) d -> p c d", p=P))


def stage6(nc, core, w, out):
    with ExitStack() as local:
        core.local = local
        def sbuf(name, shape, dtype=F32):
            return local.enter_context(nc.sbuf_tensor(name, shape, dtype))

        ln = Norm(core, sbuf, "s6_ln")
        logits = sbuf("s6_logits", [P, G, E6])
        best = sbuf("s6_best", [P, G, 8])
        where = sbuf("s6_where", [P, G, 8], U32)
        index = sbuf("s6_index", [P, G])
        chosen = sbuf("s6_chosen", [P, G, E6], BF16)
        score = sbuf("s6_score", [P, G])
        scaled = sbuf("s6_scaled", [P, G, D])
        scaledT = sbuf("s6_scaledT", [P, GT])
        silu = sbuf("s6_silu", [P, 2, GT])
        shared = sbuf("s6_shared", [P, 2, GT])
        mask = sbuf("s6_mask", [P, E6, GT], BF16)
        masked = sbuf("s6_masked", [P, 2, GT])
        hidden = sbuf("s6_hidden", [P, GT])
        yT = sbuf("s6_yT", [P, GT])

        sem = core.semaphore
        chain_v = sem("s6_chain_v")
        logits_done = sem("s6_logits_done")
        best_ready = sem("s6_best_ready")
        tanh_ready = sem("s6_tanh_ready")
        chosen_ready = sem("s6_chosen_ready")
        scaled_ready = sem("s6_scaled_ready")
        scaled_flipped = sem("s6_scaled_flipped")
        scaledT_ready = sem("s6_scaledT_ready")
        shared_done = sem("s6_shared_done")
        silu_ready = sem("s6_silu_ready")
        shared_ready = sem("s6_shared_ready")
        shared_read = sem("s6_shared_read")
        mask_done = sem("s6_mask_done")
        mask_ready = sem("s6_mask_ready")
        masked_ready = sem("s6_masked_ready")
        masked_read = sem("s6_masked_read")
        hidden_ready = sem("s6_hidden_ready")
        yT_ready = sem("s6_yT_ready")
        y_flipped = sem("s6_y_flipped")
        x_ready = sem("s6_x_ready")
        out_landed = core.plain_semaphore("s6_out_landed")
        core.start_stage(w.landed["s6"], w.count["s6"])
        bank = core.bank
        MISC, LOGITS, MASK, GATE, UP, SUM, OUT = 0, 1, 2, 4, 5, 6, 7

        with nc.Block() as block:
            @block.sync
            def _(sp):
                with sp.Fori(0, GROUPS) as i:
                    sp.wait_ge(x_ready, at(i, 1, 1))
                    sp.dma_start(out.rearrange("n t d -> t n d")[:, bass.ts(i, G), :],
                                 core.x[:, bass.ts(i, G), :]).then_inc(out_landed, 16)
                sp.wait_ge(out_landed, GROUPS * 16)

            @block.gpsimd
            def _(pool):
                with pool.Fori(0, GROUPS) as i:
                    ln.rstd_by_gpsimd(pool, i)

            @block.scalar
            def _(act):
                nc.scalar.preload_act_table_set("silu_and_others")
                with act.Fori(0, GROUPS) as i:
                    ln.xnT_by_scalar(act, i, bank[:, MISC, :])
                    act.wait_ge(best_ready, at(i, 1, 1))
                    nc.scalar.activation(score[:, :], best[:, :, 0], ACT.Tanh, scale=0.5).then_inc(tanh_ready, 1)
                    for c in range(SHARED):
                        act.wait_ge(shared_done, at(i, SHARED, c + 1))
                        act.wait_ge(shared_ready, at(i, SHARED, max(c - 1, 0)))
                        nc.scalar.activation(silu[:, c % 2, :], bank[:, GATE if c % 2 else MASK, :],
                                             ACT.Silu).then_inc(silu_ready, 1)
                    act.wait_ge(scaled_flipped, at(i, 1, 1))
                    nc.scalar.copy(scaledT[:, :], bank[:, MISC, :]).then_inc(scaledT_ready, 1)
                    for e in range(E6):
                        act.wait_ge(mask_done, at(i, E6, e + 1))
                        nc.scalar.copy(mask[:, e, :], bank[:, MASK + e % 2, :]).then_inc(mask_ready, 1)
                    act.wait_ge(masked_read, at(i, 2 * E6, E6))
                    nc.scalar.activation(silu[:, 0, :], bank[:, GATE, :], ACT.Silu).then_inc(silu_ready, 1)
                    act.wait_ge(masked_read, at(i, 2 * E6, 2 * E6))
                    nc.scalar.copy(yT[:, :], bank[:, SUM, :]).then_inc(yT_ready, 1)

            @block.vector
            def _(dve):
                with dve.Fori(0, GROUPS) as i:
                    chain = Chain(dve, chain_v, i, 5)
                    ln.norm_by_vector(dve, i, chain)

                    dve.wait_ge(logits_done, at(i, 1, 1))
                    chain.link(nc.vector.tensor_copy(
                        logits[:, :, :], bank[:, LOGITS, 0:G * E6].rearrange("p (n e) -> p n e", e=E6)))
                    core.hold_vector()
                    for n in range(G):
                        last = nc.vector.max(best[:, n, :], logits[:, n, :])
                    last.then_inc(best_ready, 1)
                    dve.wait_ge(best_ready, at(i, 1, 1))
                    core.hold_vector()
                    for n in range(G):
                        last = nc.vector.max_index(where[:, n, :], best[:, n, :], logits[:, n, :])
                    chain.link(last)
                    chain.link(nc.vector.tensor_copy(index[:, :], where[:, :, 0]))
                    for n in range(G):
                        last = nc.vector.tensor_scalar(chosen[:, n, :], w.s6_count[:, :], index[:, n:n + 1], None,
                                                       ALU.is_equal)
                    last.then_inc(chosen_ready, 1)
                    dve.wait_ge(tanh_ready, at(i, 1, 1))
                    chain.link(nc.vector.tensor_scalar(score[:, :], score[:, :], 0.5, 0.5, ALU.mult, ALU.add))
                    for n in range(G):
                        last = nc.vector.tensor_scalar(scaled[:, n, :], ln.xn[:, n, :], score[:, n:n + 1], None,
                                                       ALU.mult)
                    last.then_inc(scaled_ready, 1)

                    for c in range(SHARED):
                        dve.wait_ge(silu_ready, at(i, SHARED + 1, c + 1))
                        dve.wait_ge(shared_read, at(i, SHARED, max(c - 1, 0)))
                        nc.vector.tensor_tensor(shared[:, c % 2, :], bank[:, UP if c % 2 else MASK + 1, :],
                                                silu[:, c % 2, :], ALU.mult).then_inc(shared_ready, 1)

                    def mask_tokens(tokens, k):
                        e = k % E6
                        dve.wait_ge(mask_ready, at(i, E6, e + 1))
                        dve.wait_ge(masked_read, at(i, 2 * E6, max(k - 1, 0)))
                        nc.vector.tensor_tensor(masked[:, k % 2, :], tokens, mask[:, e, :],
                                                ALU.mult).then_inc(masked_ready, 1)

                    dve.wait_ge(scaledT_ready, at(i, 1, 1))
                    for e in range(E6):
                        mask_tokens(scaledT[:, :], e)
                    dve.wait_ge(masked_read, at(i, 2 * E6, E6))
                    dve.wait_ge(silu_ready, at(i, SHARED + 1, SHARED + 1))
                    nc.vector.tensor_tensor(hidden[:, :], bank[:, UP, :], silu[:, 0, :],
                                            ALU.mult).then_inc(hidden_ready, 1)
                    dve.wait_ge(hidden_ready, at(i, 1, 1))
                    for e in range(E6):
                        mask_tokens(hidden[:, :], E6 + e)
                    dve.wait_ge(y_flipped, at(i, 1, 1))
                    x = core.x[:, bass.ts(i, G), :]
                    nc.vector.tensor_tensor(x, bank[:, OUT, :].rearrange("p (n d) -> p n d", d=D), x,
                                            ALU.add).then_inc(x_ready, 1)
                    chain.end()

            @block.tensor
            def _(pe):
                with pe.Fori(0, GROUPS) as i:
                    pe.wait_ge(scaledT_ready, at(i, 1, 0))
                    ln.flip_by_tensor(pe, i, bank[:, MISC, :])
                    pe.wait_ge(ln.xnT_ready, at(i, 1, 1))
                    for n in range(G):
                        last = nc.tensor.matmul(bank[:, LOGITS, n * E6:(n + 1) * E6], ln.xnT[:, n * T:(n + 1) * T],
                                                w.s6_routerT[:, :], start=True, stop=True)
                    last.then_inc(logits_done, 1)

                    def shared_hidden(c):
                        if c >= 2:
                            pe.wait_ge(shared_ready, at(i, SHARED, c - 1))
                        nc.tensor.matmul(bank[:, GATE if c % 2 else MASK, :], w.s6_sgateT[:, c * P:(c + 1) * P],
                                         ln.xnT[:, :], start=True, stop=True)
                        nc.tensor.matmul(bank[:, UP if c % 2 else MASK + 1, :], w.s6_supT[:, c * P:(c + 1) * P],
                                         ln.xnT[:, :], start=True, stop=True).then_inc(shared_done, 1)

                    def shared_down(c):
                        pe.wait_ge(shared_ready, at(i, SHARED, c + 1))
                        if c == 0:
                            pe.wait_ge(yT_ready, at(i, 1, 0))
                        nc.tensor.matmul(bank[:, SUM, :], w.s6_sdownT[:, c, :], shared[:, c % 2, :], start=(c == 0),
                                         stop=False).then_inc(shared_read, 1)

                    shared_hidden(0)
                    shared_hidden(1)
                    for c in range(SHARED):
                        if c + 2 < SHARED:
                            shared_hidden(c + 2)
                        shared_down(c)

                    for n in range(G):
                        pe.wait_ge(scaled_ready, at(i, 1, 1))
                        last = nc.tensor.transpose(bank[:, MISC, n * T:(n + 1) * T], scaled[:, n, :], core.ident[:, :])
                    last.then_inc(scaled_flipped, 1)

                    def mask_of(e):
                        pe.wait_ge(chosen_ready, at(i, 1, 1))
                        pe.wait_ge(mask_ready, at(i, E6, max(e - 1, 0)))
                        for n in range(G):
                            last = nc.tensor.matmul(bank[:, MASK + e % 2, n * T:(n + 1) * T],
                                                    chosen[:, n, e:e + 1].to_broadcast([P, P]), core.ident_bf[:, :],
                                                    start=True, stop=True)
                        last.then_inc(mask_done, 1)

                    mask_of(0)
                    mask_of(1)
                    for e in range(E6):
                        pe.wait_ge(masked_ready, at(i, 2 * E6, e + 1))
                        nc.tensor.matmul(bank[:, GATE, :], w.s6_gateup[:, e, 0:P], masked[:, e % 2, :],
                                         start=(e == 0), stop=(e == E6 - 1))
                        nc.tensor.matmul(bank[:, UP, :], w.s6_gateup[:, e, P:EXP6], masked[:, e % 2, :],
                                         start=(e == 0), stop=(e == E6 - 1)).then_inc(masked_read, 1)
                        if e + 2 < E6:
                            mask_of(e + 2)
                    for e in range(E6):
                        pe.wait_ge(masked_ready, at(i, 2 * E6, E6 + e + 1))
                        nc.tensor.matmul(bank[:, SUM, :], w.s6_down[:, e, :], masked[:, e % 2, :], start=False,
                                         stop=(e == E6 - 1)).then_inc(masked_read, 1)
                    pe.wait_ge(yT_ready, at(i, 1, 1))
                    pe.wait_ge(x_ready, at(i, 1, 0))
                    for n in range(G):
                        last = nc.tensor.transpose(bank[:, OUT, n * T:(n + 1) * T], yT[:, n * T:(n + 1) * T],
                                                   core.ident[:, :])
                    last.then_inc(y_flipped, 1)



def laid_out(inputs):
    f = {k: np.asarray(v) for k, v in inputs.items()}
    band, upto, minus_after, own = level_constants()
    out = {"x": f["x"], "band": band, "upto": upto, "minus_after": minus_after, "own": own}
    out["s1_wq"], out["s1_wk"], out["s1_wv"] = f["L0_attn_Wq"], f["L0_attn_Wk"], f["L0_attn_Wv"]
    out["s1_woT"] = f["L0_attn_Wo"].T
    levels = f["L0_attn_Wdl"].reshape(H1, -1, D)[:, :LEVELS].transpose(1, 0, 2).reshape(LEVELS * H1, D)
    out["s1_small"] = np.concatenate([f["L0_attn_Wg"], levels]).T
    out["s1_bias"] = np.concatenate([f["L0_attn_bg"], f["L0_attn_Lparam"][:, :LEVELS].T.reshape(-1)])
    out["s1_g"], out["s1_b"] = f["L0_attn_ln_g"], f["L0_attn_ln_b"]
    out["flip"] = np.eye(P, dtype=np.float32)[::-1]
    out["ctxT"] = f["ctx_1024"].reshape(BATCH * M, D).T
    out["head_of"] = narrow_constants()
    for name in ("q", "k", "v", "o"):
        out[f"s2_w{name}T"] = f[f"L0_xattn_W{name}"].T
        out[f"s2_b{name}"] = f[f"L0_xattn_b{name}"]
    out["s3_norm"], out["s3_gateT"] = f["L0_ffn_norm_weight"], f["L0_ffn_gate_w"].T
    out["s3_w1T"] = f["L0_ffn_w1"].reshape(E3 * HID, D).T
    out["s3_b1T"] = f["L0_ffn_b1"].reshape(E3 * CHUNKS, P).T
    out["s3_w2T"] = f["L0_ffn_w2"].transpose(0, 2, 1).reshape(E3 * HID, D)
    out["s3_b2"] = f["L0_ffn_b2"]
    out["count"] = np.arange(16, dtype=np.float32)
    for k, name in enumerate(("q", "k", "v")):
        out[f"s4_w{name}T"] = f["L1_attn_Wqkv"][k * D:(k + 1) * D].T
    out["s4_woT"] = f["L1_attn_Wout"].T
    out["ramp"], out["s4_coeffsT"], out["s4_wposT"] = ramp_constants(), f["L1_attn_coeffs"].T, f["L1_attn_Wpos"].T
    out["s5_gamma"], out["s5_beta"] = f["L1_xattn_ln_gamma"], f["L1_xattn_ln_beta"]
    out["s5_wq"], out["s5_wkv"], out["s5_wo"] = f["L1_xattn_w_q"], f["L1_xattn_w_kv"], f["L1_xattn_w_out"]
    out["s5_bo"], out["s5_gate"] = f["L1_xattn_b_out"], f["L1_xattn_gate"]
    out["s6_routerT"], out["s6_gateup"] = f["L1_ffn_router_w"].T, f["L1_ffn_gate_up_proj"]
    out["s6_down"], out["s6_sgateT"] = f["L1_ffn_down_proj"], f["L1_ffn_shared_gate_w"].T
    out["s6_supT"], out["s6_sdownT"] = f["L1_ffn_shared_up_w"].T, f["L1_ffn_shared_down_w"].T
    return {k: np.ascontiguousarray(v) for k, v in out.items()}


def program(nc, a, out, stages=(1, 2, 3, 4, 5, 6)):
    scratch = nc.dram_tensor("lam_scratch", [P, LEVELS, G * H1], F32, kind="Internal").ap()
    bias_dram = nc.dram_tensor("bias_scratch", [H, SPAN], F32, kind="Internal").ap()
    with ExitStack() as ctx:
        core = Core(nc, ctx)
        w = Weights(core)
        stage1_weights(w, a)
        s2 = narrow_weights(w, a, "s2")
        stage3_weights(w, a)
        s4 = narrow_weights(w, a, "s4")
        bias_weights(w, a)
        stage5_weights(w, a)
        stage6_weights(w, a)

        x_landed = ctx.enter_context(nc.semaphore("x_landed"))
        setup_step = ctx.enter_context(nc.semaphore("setup_step"))
        out_landed = ctx.enter_context(nc.semaphore("out_landed"))
        with nc.Block() as block:
            @block.sync
            def _(sp):
                sp.dma_start(core.x[:, :, :], a["x"].rearrange("n t d -> t n d")).then_inc(x_landed, 16)
                for stage, tile, source in w.loads:
                    sp.dma_start(tile[tuple(slice(None) for _ in tile.shape)], source).then_inc(w.landed[stage], 16)
                sp.wait_ge(x_landed, 16)

            @block.gpsimd
            def _(pool):
                nc.gpsimd.memset(core.minus_half[:, :], -0.5)
                for eps, tile in core.eps.items():
                    nc.gpsimd.memset(tile[:, :], eps)
                nc.gpsimd.memset(core.ident[:, :], 0.0).then_inc(setup_step, 1)
                pool.wait_ge(setup_step, 1)
                nc.gpsimd.affine_select(out=core.ident[:, :], in_=core.ident[:, :], compare_op=ALU.not_equal, fill=1.0,
                                        base=0, pattern=[[-1, P]], channel_multiplier=1).then_inc(setup_step, 1)
                pool.wait_ge(setup_step, 2)
                nc.gpsimd.tensor_copy(core.ident_bf[:, :], core.ident[:, :])

        if 1 in stages:
            stage1(nc, core, w, scratch)
        if 2 in stages:
            narrow_attention(nc, core, w, "s2", s2, ctxT_dram=a["ctxT"])
        if 3 in stages:
            stage3(nc, core, w)
        if 4 in stages:
            make_bias(nc, core, w, bias_dram)
            narrow_attention(nc, core, w, "s4", s4, bias=w.bias)
        if 5 in stages:
            stage5(nc, core, w, a["ctxT"])
        if 6 in stages:
            stage6(nc, core, w, out)

        with nc.Block() as block:
            @block.sync
            def _(sp):
                if 6 not in stages:
                    sp.dma_start(out.rearrange("n t d -> t n d"), core.x[:, :, :]).then_inc(out_landed, 16)
                    sp.wait_ge(out_landed, 16)
                for stage in w.landed:
                    sp.wait_ge(w.landed[stage], w.count[stage])


def kernel(**inputs):
    import concourse.bacc as bacc
    from concourse.bass_utils import run_bass_kernel_spmd

    nc = bacc.Bacc("TRN2", target_bir_lowering=False, num_devices=1)
    arrays = laid_out(inputs)
    a = {name: nc.dram_tensor(name, v.shape, mybir.dt.from_np(v.dtype), kind="ExternalInput").ap()
         for name, v in arrays.items()}
    out = nc.dram_tensor("out", (BATCH, T, D), F32, kind="ExternalOutput").ap()
    program(nc, a, out)
    return run_bass_kernel_spmd(nc, [arrays], core_ids=[0]).results[0]["out"]
```

```python
from contextlib import ExitStack

import numpy as np
import concourse.bass as bass
from concourse import mybir

F32 = mybir.dt.float32
BF16 = mybir.dt.bfloat16
U32 = mybir.dt.uint32
ALU = mybir.AluOpType
ACT = mybir.ActivationFunctionType
AX = mybir.AxisListType

P = 128
BATCH = 32
T = 128
D = 128
M = 77
G = 4
GROUPS = BATCH // G
GT = G * T
GM = G * M
LN_EPS = 1e-5
RMS_EPS = 1e-6
CREDIT = 1


def at(i, per_group, k):
    if isinstance(i, int):
        return max(i * per_group + k, 0) + CREDIT
    return i * per_group + (k + CREDIT)


class Chain:

    def __init__(self, engine, semaphore, i, per_group):
        self.engine, self.semaphore, self.i, self.per_group, self.links = engine, semaphore, i, per_group, 0

    def link(self, instruction):
        self.links += 1
        instruction.then_inc(self.semaphore, 1)
        self.engine.wait_ge(self.semaphore, at(self.i, self.per_group, self.links))

    def end(self):
        assert self.links == self.per_group, (self.links, self.per_group)
class Core:

    def __init__(self, nc, ctx):
        self.nc, self.ctx = nc, ctx
        self.local = ctx
        self.fresh = []
        self.x = self.sbuf("x_all", [P, BATCH, D])
        self.ident = self.sbuf("ident", [P, P])
        self.ident_bf = self.sbuf("ident_bf", [P, P], BF16)
        self.minus_half = self.sbuf("minus_half", [P, G])
        self.eps = {LN_EPS: self.sbuf("ln_eps", [P, G]), RMS_EPS: self.sbuf("rms_eps", [P, G])}
        self.spare = self.sbuf("spare", [P, 1])
        self.bank = ctx.enter_context(nc.psum_tensor("bank", [P, 8, 512], F32))

    def sbuf(self, name, shape, dtype=F32):
        return self.ctx.enter_context(self.nc.sbuf_tensor(name, shape, dtype))

    def semaphore(self, name):
        s = self.local.enter_context(self.nc.semaphore(name))
        self.fresh.append((s, CREDIT))
        return s

    def plain_semaphore(self, name):
        s = self.local.enter_context(self.nc.semaphore(name))
        self.fresh.append((s, 0))
        return s

    def hold_vector(self):
        self.nc.vector.tensor_copy(self.spare[:, :], self.minus_half[:, 0:1])

    def start_stage(self, weights_landed, count):
        nc, fresh, self.fresh = self.nc, self.fresh, []
        with nc.Block() as block:
            @block.gpsimd
            def _(pool):
                for s, start in fresh:
                    pool.sem_clear(s)
                    if start:
                        pool.sem_inc(s, start)

            @block.sync
            def _(sp):
                sp.wait_ge(weights_landed, count)


class Moments:

    def __init__(self, core, sbuf, name, eps=LN_EPS):
        self.core, self.nc, self.eps = core, core.nc, eps
        self.stats = sbuf(name + "_stats", [P, G, 6])
        self.moments = sbuf(name + "_moments", [P, G, 2])
        self.variance = sbuf(name + "_variance", [P, G])
        self.rstd = sbuf(name + "_rstd", [P, G])
        self.moments_ready = core.semaphore(name + "_moments_ready")
        self.variance_ready = core.semaphore(name + "_variance_ready")
        self.rstd_ready = core.semaphore(name + "_rstd_ready")

    def moments_by_vector(self, chain, source):
        nc = self.nc
        for n in range(G):
            last = nc.vector.bn_stats(self.stats[:, n, :], source(n))
        chain.link(last)
        self.core.hold_vector()
        for n in range(G):
            last = nc.vector.bn_aggr(self.moments[:, n, :], self.stats[:, n, :])
        last.then_inc(self.moments_ready, 1)

    def rstd_by_gpsimd(self, pool, i):
        nc = self.nc
        pool.wait_ge(self.moments_ready, at(i, 1, 1))
        nc.gpsimd.tensor_tensor(self.variance[:, :], self.moments[:, :, 1], self.core.eps[self.eps][:, :],
                                ALU.add).then_inc(self.variance_ready, 1)
        pool.wait_ge(self.variance_ready, at(i, 1, 1))
        nc.gpsimd.tensor_tensor(self.rstd[:, :], self.variance[:, :], self.core.minus_half[:, :],
                                ALU.pow).then_inc(self.rstd_ready, 1)

    def scaled_by_vector(self, dve, i, out, source, ready):
        nc = self.nc
        dve.wait_ge(self.rstd_ready, at(i, 1, 1))
        for n in range(G):
            nc.vector.tensor_scalar(out[:, n, :], source(n), self.moments[:, n, 0:1], self.rstd[:, n:n + 1],
                                    ALU.subtract, ALU.mult).then_inc(ready, 1)


class Norm(Moments):

    def __init__(self, core, sbuf, name):
        super().__init__(core, sbuf, name)
        self.xn = sbuf(name + "_xn", [P, G, D])
        self.xnT = sbuf(name + "_xnT", [P, GT])
        self.xn_ready = core.semaphore(name + "_xn_ready")
        self.flipped = core.semaphore(name + "_flipped")
        self.xnT_ready = core.semaphore(name + "_xnT_ready")

    def source(self, i):
        return lambda n: self.core.x[:, bass.ds(i * G + n, 1), :]

    def norm_by_vector(self, dve, i, chain):
        self.moments_by_vector(chain, self.source(i))
        self.scaled_by_vector(dve, i, self.xn, self.source(i), self.xn_ready)

    def flip_by_tensor(self, pe, i, bank):
        nc = self.nc
        for n in range(G):
            pe.wait_ge(self.xn_ready, at(i, G, n + 1))
            last = nc.tensor.transpose(bank[:, n * T:(n + 1) * T], self.xn[:, n, :], self.core.ident[:, :])
        last.then_inc(self.flipped, 1)

    def xnT_by_scalar(self, act, i, bank):
        act.wait_ge(self.flipped, at(i, 1, 1))
        self.nc.scalar.copy(self.xnT[:, :], bank[:, :]).then_inc(self.xnT_ready, 1)


class Weights:

    def __init__(self, core):
        self.core, self.loads, self.landed, self.count = core, [], {}, {}

    def load(self, stage, name, shape, source, dtype=F32):
        if stage not in self.landed:
            self.landed[stage] = self.core.ctx.enter_context(self.core.nc.semaphore(f"{stage}_weights_landed"))
            self.count[stage] = 0
        tile = self.core.sbuf(name, shape, dtype)
        self.loads.append((stage, tile, source))
        self.count[stage] += 16
        return tile



H1 = 8
LEVELS = 8
TB = P // LEVELS
NB = T // TB
SMALL = H1 + LEVELS * H1
HALF = NB // 2 * H1 * TB


def level_constants():
    band = np.zeros((LEVELS, TB, 2 * T - TB), np.float32)
    for b in range(TB):
        for c in range(2 * T - TB):
            distance = b - (c - (T - TB))
            if 0 <= distance < T:
                band[0 if distance == 0 else int(np.log2(distance)) + 1, b, c] = 1.0
    u, t = np.arange(T)[:, None], np.arange(T)[None, :]
    upto = (u <= t).astype(np.float32)
    minus_after = -(u > t).astype(np.float32)
    own = np.tile(np.eye(TB, dtype=np.float32), (LEVELS, 1))
    return band.reshape(P, 2 * T - TB), upto, minus_after, own


def stage1_weights(w, a):
    heads = "(h s) d -> s h d"
    w.s1_wq = w.load("s1", "w_s1_q", [P, H1, D], a["s1_wq"].rearrange(heads, s=P))
    w.s1_wk = w.load("s1", "w_s1_k", [P, H1, D], a["s1_wk"].rearrange(heads, s=P))
    w.s1_wv = w.load("s1", "w_s1_v", [P, H1, D], a["s1_wv"].rearrange(heads, s=P))
    w.s1_woT = w.load("s1", "w_s1_oT", [P, H1, D], a["s1_woT"].rearrange(heads, s=P))
    w.s1_small = w.load("s1", "w_s1_small", [P, SMALL], a["s1_small"])
    w.s1_bias = w.load("s1", "w_s1_bias", [P, SMALL], a["s1_bias"].unsqueeze(0).to_broadcast([P, SMALL]))
    w.s1_g = w.load("s1", "w_s1_g", [P, D], a["s1_g"].unsqueeze(0).to_broadcast([P, D]))
    w.s1_b = w.load("s1", "w_s1_b", [P, D], a["s1_b"].unsqueeze(0).to_broadcast([P, D]))
    w.band = w.load("s1", "w_band", [P, 2 * T - TB], a["band"])
    w.upto = w.load("s1", "w_upto", [P, T], a["upto"])
    w.minus_after = w.load("s1", "w_minus_after", [P, T], a["minus_after"])
    w.own = w.load("s1", "w_own", [P, TB], a["own"])


def stage1(nc, core, w, scratch):
    with ExitStack() as local:
        core.local = local
        def sbuf(name, shape, dtype=F32):
            return local.enter_context(nc.sbuf_tensor(name, shape, dtype))

        ln = Norm(core, sbuf, "s1_ln")
        ln2 = Moments(core, sbuf, "s1_ln2")
        qk = sbuf("s1_qk", [P, H1, D])
        vo = sbuf("s1_vo", [P, H1, D])
        qT = sbuf("s1_qT", [P, G * NB, H1, TB])
        v = sbuf("s1_v", [P, G, H1 * D])
        pre = sbuf("s1_pre", [P, 1 + LEVELS, G, H1])
        log = sbuf("s1_log", [P, 1 + LEVELS, G, H1])
        soft = sbuf("s1_soft", [P, 1 + LEVELS, G, H1])
        lam = sbuf("s1_lam", [P, NB, G, H1])
        gate = sbuf("s1_gate", [P, 2, NB, H1, TB])
        level = sbuf("s1_level", [P, 2, NB, H1, TB])
        decay = sbuf("s1_decay", [P, 2, 2, HALF])
        weight = sbuf("s1_weight", [P, 2, HALF])
        aT = sbuf("s1_aT", [P, 2, H1, T])
        y = sbuf("s1_y", [P, G, D])
        z = sbuf("s1_z", [P, G, D])

        fold_done = core.plain_semaphore("s1_fold_done")
        fold_kept = core.plain_semaphore("s1_fold_kept")
        chain_v = core.semaphore("s1_chain_v")
        chain_p = core.semaphore("s1_chain_p")
        small_done = core.semaphore("s1_small_done")
        pre_kept = core.semaphore("s1_pre_kept")
        magnitude_ready = core.semaphore("s1_magnitude_ready")
        exp_ready = core.semaphore("s1_exp_ready")
        log_ready = core.semaphore("s1_log_ready")
        soft_ready = core.semaphore("s1_soft_ready")
        projected = core.semaphore("s1_projected")
        kept_by_scalar = core.semaphore("s1_kept_by_scalar")
        kept_by_vector = core.semaphore("s1_kept_by_vector")
        gate_ready = core.semaphore("s1_gate_ready")
        level_ready = core.semaphore("s1_level_ready")
        logdecay_done = core.semaphore("s1_logdecay_done")
        decay_ready = core.semaphore("s1_decay_ready")
        level_done = core.semaphore("s1_level_done")
        weight_ready = core.semaphore("s1_weight_ready")
        score_done = core.semaphore("s1_score_done")
        aT_ready = core.semaphore("s1_aT_ready")
        out_done = core.semaphore("s1_out_done")
        y_ready = core.semaphore("s1_y_ready")
        z_ready = core.semaphore("s1_z_ready")
        x_ready = core.semaphore("s1_x_ready")
        spilled = core.plain_semaphore("s1_spilled")
        lam_landed = core.plain_semaphore("s1_lam_landed")

        core.start_stage(w.landed["s1"], w.count["s1"])
        bank = core.bank
        LOGDECAY, LEVEL, SCORE, WORK = 0, 2, 4, 6
        PROJ = H1 + 2 * G

        with nc.Block() as block:
            @block.tensor
            def _(pe):
                for h in range(H1):
                    if h >= 2:
                        pe.wait_ge(fold_kept, h - 1)
                    nc.tensor.matmul(bank[:, h % 2, 0:D], w.s1_wq[:, h, :], w.s1_wk[:, h, :], start=True, stop=True)
                    nc.tensor.matmul(bank[:, h % 2, D:2 * D], w.s1_wv[:, h, :], w.s1_woT[:, h, :], start=True,
                                     stop=True).then_inc(fold_done, 1)

            @block.vector
            def _(dve):
                for h in range(H1):
                    dve.wait_ge(fold_done, h + 1)
                    nc.vector.tensor_scalar(qk[:, h, :], bank[:, h % 2, 0:D], float(D) ** -0.5, None, ALU.mult)
                    nc.vector.tensor_copy(vo[:, h, :], bank[:, h % 2, D:2 * D]).then_inc(fold_kept, 1)

        def keep(copy, k):
            source = bank[:, WORK + k % 2, :]
            if k < H1:
                return copy(qT[:, :, k, :], source.rearrange("p (a b) -> p a b", b=TB))
            n, c = (k - H1) // 2, (k - H1) % 2
            return copy(v[:, n, c * 512:(c + 1) * 512], source)

        with nc.Block() as block:
            @block.sync
            def _(sp):
                with sp.Fori(0, GROUPS) as i:
                    sp.wait_ge(soft_ready, at(i, 1, 1))
                    sp.dma_start(scratch[:, :, :],
                                 soft[:, 1:, :, :].rearrange("p l n h -> p l (n h)")).then_inc(spilled, 16)
                    sp.wait_ge(spilled, (i + 1) * 16)
                    for l in range(LEVELS):
                        sp.dma_start(lam[l * TB:(l + 1) * TB, :, :, :].rearrange("b a n h -> b a (n h)"),
                                     scratch[:, l, :].rearrange("(a b) c -> b a c", b=TB)).then_inc(lam_landed, 16)
                sp.wait_ge(lam_landed, GROUPS * 16 * LEVELS)

            @block.gpsimd
            def _(pool):
                with pool.Fori(0, GROUPS) as i:
                    chain = Chain(pool, chain_p, i, 2)
                    ln.rstd_by_gpsimd(pool, i)
                    for n in range(G):
                        free = 2 * max(n - 1, 0)
                        if n == 0:
                            pool.wait_ge(soft_ready, at(i, 1, 1))
                        pool.wait_ge(logdecay_done, at(i, 2 * G, free))
                        nc.gpsimd.tensor_tensor(
                            gate[:, n % 2, :, :, :],
                            w.upto[:, :].rearrange("p (a b) -> p a b", b=TB).unsqueeze(2).to_broadcast([P, NB, H1, TB]),
                            soft[:, 0, n, :].unsqueeze(1).unsqueeze(3).to_broadcast([P, NB, H1, TB]),
                            ALU.mult).then_inc(gate_ready, 1)
                        if n == 0:
                            pool.wait_ge(lam_landed, (i + 1) * (16 * LEVELS))
                        pool.wait_ge(level_done, at(i, 2 * G, free))
                        nc.gpsimd.tensor_tensor(
                            level[:, n % 2, :, :, :],
                            lam[:, :, n, :].unsqueeze(3).to_broadcast([P, NB, H1, TB]),
                            w.own[:, :].unsqueeze(1).unsqueeze(1).to_broadcast([P, NB, H1, TB]),
                            ALU.mult).then_inc(level_ready, 1)
                    ln2.rstd_by_gpsimd(pool, i)
                    pool.wait_ge(z_ready, at(i, G, G))
                    chain.link(nc.gpsimd.tensor_tensor(
                        z[:, :, :], z[:, :, :], w.s1_g[:, :].unsqueeze(1).to_broadcast([P, G, D]), ALU.mult))
                    chain.link(nc.gpsimd.tensor_tensor(
                        z[:, :, :], z[:, :, :], w.s1_b[:, :].unsqueeze(1).to_broadcast([P, G, D]), ALU.add))
                    x = core.x[:, bass.ts(i, G), :]
                    nc.gpsimd.tensor_tensor(x, x, z[:, :, :], ALU.add).then_inc(x_ready, 1)
                    chain.end()

            @block.scalar
            def _(act):
                nc.scalar.preload_act_table_set("natural_log_exp_and_others")
                with act.Fori(0, GROUPS) as i:
                    ln.xnT_by_scalar(act, i, bank[:, WORK, :])
                    act.wait_ge(magnitude_ready, at(i, 1, 1))
                    nc.scalar.activation(log[:, :, :, :], log[:, :, :, :], ACT.Exp).then_inc(exp_ready, 1)
                    act.wait_ge(exp_ready, at(i, 1, 1))
                    nc.scalar.activation(log[:, :, :, :], log[:, :, :, :], ACT.Ln, bias=1.0).then_inc(log_ready, 1)
                    for k in range(0, PROJ, 2):
                        act.wait_ge(projected, at(i, PROJ, k + 1))
                        keep(nc.scalar.copy, k).then_inc(kept_by_scalar, 1)
                    for n in range(G):
                        act.wait_ge(weight_ready, at(i, 2 * G, 2 * max(n - 1, 0)))
                        for j in range(2):
                            act.wait_ge(logdecay_done, at(i, 2 * G, 2 * n + j + 1))
                            nc.scalar.activation(decay[:, n % 2, j, :], bank[:, LOGDECAY + j, :],
                                                 ACT.Exp).then_inc(decay_ready, 1)

            @block.vector
            def _(dve):
                with dve.Fori(0, GROUPS) as i:
                    chain = Chain(dve, chain_v, i, 3)
                    ln.norm_by_vector(dve, i, chain)

                    dve.wait_ge(small_done, at(i, 1, 1))
                    chain.link(nc.vector.tensor_tensor(
                        pre[:, :, :, :].rearrange("p l n h -> p n l h"),
                        bank[:, WORK + 1, 0:G * SMALL].rearrange("p (n l h) -> p n l h", n=G, h=H1),
                        w.s1_bias[:, :].rearrange("p (l h) -> p l h", h=H1).unsqueeze(1).to_broadcast(
                            [P, G, 1 + LEVELS, H1]), ALU.add))
                    nc.vector.scalar_tensor_tensor(out=log[:, :, :, :], in0=pre[:, :, :, :], scalar=-1.0,
                                                   in1=pre[:, :, :, :], op0=ALU.mult,
                                                   op1=ALU.min).then_inc(magnitude_ready, 1)
                    for k in range(1, PROJ, 2):
                        dve.wait_ge(projected, at(i, PROJ, k + 1))
                        keep(nc.vector.tensor_copy, k).then_inc(kept_by_vector, 1)
                        if k == 1:
                            dve.wait_ge(log_ready, at(i, 1, 1))
                            nc.vector.scalar_tensor_tensor(out=soft[:, :, :, :], in0=pre[:, :, :, :], scalar=0.0,
                                                           in1=log[:, :, :, :], op0=ALU.max,
                                                           op1=ALU.add).then_inc(soft_ready, 1)

                    def y_of(n):
                        dve.wait_ge(out_done, at(i, G, n + 1))
                        nc.vector.tensor_tensor(y[:, n, :], bank[:, WORK + n % 2, 0:D], ln.xn[:, n, :],
                                                ALU.add).then_inc(y_ready, 1)

                    for n in range(G):
                        if n >= 1:
                            y_of(n - 1)
                        for j in range(2):
                            dve.wait_ge(decay_ready, at(i, 2 * G, 2 * n + j + 1))
                            dve.wait_ge(level_done, at(i, 2 * G, 2 * n + j + 1))
                            nc.vector.tensor_tensor(weight[:, j, :], bank[:, LEVEL + j, :], decay[:, n % 2, j, :],
                                                    ALU.mult).then_inc(weight_ready, 1)
                        dve.wait_ge(out_done, at(i, G, max(n - 1, 0)))
                        for j in range(2):
                            dve.wait_ge(weight_ready, at(i, 2 * G, 2 * n + j + 1))
                            dve.wait_ge(score_done, at(i, 2 * G, 2 * n + j + 1))
                            nc.vector.tensor_tensor(
                                aT[:, n % 2, :, j * (T // 2):(j + 1) * (T // 2)].rearrange("p h (a b) -> p a h b", b=TB),
                                bank[:, SCORE + j, :].rearrange("p (a h b) -> p a h b", h=H1, b=TB),
                                weight[:, j, :].rearrange("p (a h b) -> p a h b", h=H1, b=TB),
                                ALU.mult).then_inc(aT_ready, 1)
                    y_of(G - 1)
                    dve.wait_ge(y_ready, at(i, G, G))
                    ln2.moments_by_vector(chain, lambda n: y[:, n, :])
                    dve.wait_ge(x_ready, at(i, 1, 0))
                    ln2.scaled_by_vector(dve, i, z, lambda n: y[:, n, :], z_ready)
                    chain.end()

            @block.tensor
            def _(pe):
                with pe.Fori(0, GROUPS) as i:
                    pe.wait_ge(y_ready, at(i, G, 0))
                    ln.flip_by_tensor(pe, i, bank[:, WORK, :])
                    pe.wait_ge(ln.xnT_ready, at(i, 1, 1))
                    for n in range(G):
                        last = nc.tensor.matmul(bank[:, WORK + 1, n * SMALL:(n + 1) * SMALL],
                                                ln.xnT[:, n * T:(n + 1) * T], w.s1_small[:, :], start=True, stop=True)
                    last.then_inc(small_done, 1)
                    for k in range(PROJ):
                        if k == 1:
                            pe.wait_ge(magnitude_ready, at(i, 1, 1))
                        if k >= 2:
                            pe.wait_ge(kept_by_vector if k % 2 else kept_by_scalar, at(i, PROJ // 2, k // 2))
                        if k < H1:
                            nc.tensor.matmul(bank[:, WORK + k % 2, :], qk[:, k, :], ln.xnT[:, :], start=True,
                                             stop=True).then_inc(projected, 1)
                        else:
                            n, c = (k - H1) // 2, (k - H1) % 2
                            nc.tensor.matmul(bank[:, WORK + k % 2, :], ln.xnT[:, n * T:(n + 1) * T],
                                             vo[:, c * (H1 // 2):(c + 1) * (H1 // 2), :].rearrange("p h d -> p (h d)"),
                                             start=True, stop=True).then_inc(projected, 1)

                    def out_of(n):
                        pe.wait_ge(aT_ready, at(i, 2 * G, 2 * n + 2))
                        pe.wait_ge(y_ready, at(i, G, max(n - 1, 0)))
                        for h in range(H1):
                            last = nc.tensor.matmul(bank[:, WORK + n % 2, 0:D], aT[:, n % 2, h, :],
                                                    v[:, n, h * D:(h + 1) * D], start=(h == 0), stop=(h == H1 - 1))
                        last.then_inc(out_done, 1)

                    for n in range(G):
                        pe.wait_ge(gate_ready, at(i, G, n + 1))
                        for j in range(2):
                            pe.wait_ge(decay_ready, at(i, 2 * G, max(2 * n + j - 1, 0)))
                            nc.tensor.matmul(bank[:, LOGDECAY + j, :], w.minus_after[:, :],
                                             gate[:, n % 2, j * (NB // 2):(j + 1) * (NB // 2), :, :].rearrange(
                                                 "p a h b -> p (a h b)"), start=True,
                                             stop=True).then_inc(logdecay_done, 1)
                        if n == 0:
                            pe.wait_ge(kept_by_scalar, at(i, PROJ // 2, PROJ // 2))
                            pe.wait_ge(kept_by_vector, at(i, PROJ // 2, PROJ // 2))
                        if n >= 1:
                            out_of(n - 1)
                        pe.wait_ge(level_ready, at(i, G, n + 1))
                        for j in range(2):
                            pe.wait_ge(weight_ready, at(i, 2 * G, max(2 * n + j - 1, 0)))
                            for c in range(NB // 2):
                                a = j * (NB // 2) + c
                                start = T - TB - TB * a
                                last = nc.tensor.matmul(
                                    bank[:, LEVEL + j, c * H1 * TB:(c + 1) * H1 * TB], w.band[:, start:start + T],
                                    level[:, n % 2, a, :, :].rearrange("p h b -> p (h b)"), start=True, stop=True)
                            last.then_inc(level_done, 1)
                        for j in range(2):
                            pe.wait_ge(aT_ready, at(i, 2 * G, max(2 * n + j - 1, 0)))
                            first = n * NB + j * (NB // 2)
                            nc.tensor.matmul(bank[:, SCORE + j, :], ln.xnT[:, n * T:(n + 1) * T],
                                             qT[:, first:first + NB // 2, :, :].rearrange("p a h b -> p (a h b)"),
                                             start=True, stop=True).then_inc(score_done, 1)
                    out_of(G - 1)



H = 16
HU = 8
U = G * H // HU
QUADS = 2 * U
SCORE, FLIP, WORK = 0, 4, 6
NORM_FLIP = U - 2


def turns(engine, turn):
    with engine.Fori(0, GROUPS - 1) as i:
        turn(i, True)
    turn(GROUPS - 1, False)


class Softmax:

    def __init__(self, core, sbuf, name, keys, bias=None, shares=False):
        self.core, self.nc, self.keys, self.bias, self.shares = core, core.nc, keys, bias, shares
        self.p = sbuf(name + "_p", [P, 2, HU, keys])
        self.peak = sbuf(name + "_peak", [P, 2, HU])
        self.pT = sbuf(name + "_pT", [P, 2, HU, T])
        self.scored = core.semaphore(name + "_scored")
        self.biased = core.semaphore(name + "_biased")
        self.peak_ready = core.semaphore(name + "_peak_ready")
        self.lowered = core.semaphore(name + "_lowered")
        self.exp_ready = core.semaphore(name + "_exp_ready")
        self.p_flipped = core.semaphore(name + "_p_flipped")
        self.pT_ready = core.semaphore(name + "_pT_ready")
        self.weighed = core.semaphore(name + "_weighed")
        if shares:
            self.total = sbuf(name + "_total", [P, 2, HU])
            self.inverse = sbuf(name + "_inverse", [P, 2, HU])
            self.total_ready = core.semaphore(name + "_total_ready")
            self.inverse_ready = core.semaphore(name + "_inverse_ready")
            self.share_ready = core.semaphore(name + "_share_ready")

    def lower_by_vector(self, dve, i, u):
        nc = self.nc
        p = self.p[:, u % 2, :, :]
        p4 = p.rearrange("p (g j) m -> p g j m", j=4)
        peak = self.peak[:, u % 2, :]
        first = SCORE + 2 * (u % 2)
        scores = self.core.bank[:, first:first + 2, 0:4 * self.keys].rearrange("p g (j m) -> p g j m", m=self.keys)
        dve.wait_ge(self.scored, at(i, U, u + 1))
        dve.wait_ge(self.p_flipped, at(i, QUADS, max(2 * u - 2, 0)))
        if self.bias is None:
            nc.vector.tensor_reduce(peak.rearrange("p (g j) -> p g j", j=4), scores, AX.X,
                                    ALU.max).then_inc(self.peak_ready, 1)
            dve.wait_ge(self.peak_ready, at(i, U, u + 1))
            nc.vector.tensor_tensor(p4, scores, peak.rearrange("p (g j) -> p g j", j=4).unsqueeze(3).to_broadcast(
                [P, 2, 4, self.keys]), ALU.subtract).then_inc(self.lowered, 1)
        else:
            h = HU * (u % 2)
            nc.vector.tensor_tensor(p.rearrange("p h m -> p (h m)"), scores.rearrange("p g j m -> p (g j m)"),
                                    self.bias[:, h:h + HU, :].rearrange("p h m -> p (h m)"),
                                    ALU.add).then_inc(self.biased, 1)
            dve.wait_ge(self.biased, at(i, U, u + 1))
            nc.vector.tensor_reduce(peak, p, AX.X, ALU.max).then_inc(self.peak_ready, 1)
            dve.wait_ge(self.peak_ready, at(i, U, u + 1))
            nc.vector.tensor_tensor(p, p, peak.unsqueeze(2).to_broadcast([P, HU, self.keys]),
                                    ALU.subtract).then_inc(self.lowered, 1)

    def banks_read(self):
        return self.lowered if self.bias is None else self.biased

    def exp_by_scalar(self, act, i, u):
        p = self.p[:, u % 2, :, :]
        act.wait_ge(self.lowered, at(i, U, u + 1))
        self.nc.scalar.activation(p, p, ACT.Exp).then_inc(self.exp_ready, 1)

    def share_by_vector(self, dve, i, u):
        nc = self.nc
        p = self.p[:, u % 2, :, :]
        dve.wait_ge(self.exp_ready, at(i, U, u + 1))
        nc.vector.tensor_reduce(self.total[:, u % 2, :], p, AX.X, ALU.add).then_inc(self.total_ready, 1)
        dve.wait_ge(self.total_ready, at(i, U, u + 1))
        nc.vector.reciprocal(self.inverse[:, u % 2, :], self.total[:, u % 2, :]).then_inc(self.inverse_ready, 1)
        dve.wait_ge(self.inverse_ready, at(i, U, u + 1))
        nc.vector.tensor_tensor(p, p, self.inverse[:, u % 2, :].unsqueeze(2).to_broadcast([P, HU, self.keys]),
                                ALU.mult).then_inc(self.share_ready, 1)

    def flip_by_tensor(self, pe, i, u, norm=None):
        nc = self.nc
        pe.wait_ge(self.share_ready if self.shares else self.exp_ready, at(i, U, u + 1))
        for q in (2 * u, 2 * u + 1):
            pe.wait_ge(self.pT_ready, at(i, QUADS, max(q - 1, 0)))
            if norm is not None and q == 2 * NORM_FLIP:
                pe.wait_ge(norm.xnT_ready, at(i + 1, 1, 1))
            for j in range(4):
                last = nc.tensor.transpose(self.core.bank[0:self.keys, FLIP + q % 2, j * T:(j + 1) * T],
                                           self.p[:, u % 2, 4 * (q % 2) + j, :], self.core.ident[:, :])
            last.then_inc(self.p_flipped, 1)

    def pT_by_scalar(self, act, i, u):
        act.wait_ge(self.weighed, at(i, U, max(u - 1, 0)))
        for q in (2 * u, 2 * u + 1):
            h = 4 * (q % 2)
            act.wait_ge(self.p_flipped, at(i, QUADS, q + 1))
            self.nc.scalar.copy(self.pT[0:self.keys, u % 2, h:h + 4, :].rearrange("m h t -> m (h t)"),
                                self.core.bank[0:self.keys, FLIP + q % 2, :]).then_inc(self.pT_ready, 1)



DH = D // H


def narrow_constants():
    return (np.arange(D)[:, None] // DH == np.arange(H)[None, :]).astype(np.float32)


def narrow_weights(w, a, s):
    t = {}
    for name in ("q", "k", "v", "o"):
        t[name] = w.load(s, f"w_{s}_{name}", [P, D], a[f"{s}_w{name}T"])
    if s == "s2":
        t["bq"] = w.load(s, f"w_{s}_bq", [P, 1], a[f"{s}_bq"].unsqueeze(1))
        t["bk"] = w.load(s, f"w_{s}_bk", [P, 1], a[f"{s}_bk"].unsqueeze(1))
        t["bv"] = w.load(s, f"w_{s}_bv", [M, D], a[f"{s}_bv"].unsqueeze(0).to_broadcast([M, D]))
        t["bo"] = w.load(s, f"w_{s}_bo", [P, D], a[f"{s}_bo"].unsqueeze(0).to_broadcast([P, D]))
    t["head_of"] = w.load(s, f"w_{s}_head_of", [P, H], a["head_of"])
    return t


def narrow_attention(nc, core, w, s, t, ctxT_dram=None, bias=None):
    cross = ctxT_dram is not None
    keys = M if cross else T
    with ExitStack() as local:
        core.local = local
        def sbuf(name, shape, dtype=F32):
            return local.enter_context(nc.sbuf_tensor(name, shape, dtype))

        ln = Norm(core, sbuf, s + "_ln")
        sm = Softmax(core, sbuf, s, keys, bias)
        source = sbuf(s + "_ctxT", [P, GM]) if cross else ln.xnT
        qT = sbuf(s + "_qT", [P, GT])
        kT = sbuf(s + "_kT", [P, G, keys])
        own = sbuf(s + "_own", [P, 2, HU, keys])
        v = sbuf(s + "_v", [P, G, H, DH + 1])
        inverse = sbuf(s + "_inverse", [P, 2, H])
        o = sbuf(s + "_o", [P, 2, D])
        oT = sbuf(s + "_oT", [P, 2, T])

        chain_v = core.semaphore(s + "_chain_v")
        q_done = core.semaphore(s + "_q_done")
        k_done = core.semaphore(s + "_k_done")
        v_done = core.semaphore(s + "_v_done")
        q_kept = core.semaphore(s + "_q_kept")
        k_kept = core.semaphore(s + "_k_kept")
        v_kept = core.semaphore(s + "_v_kept")
        own_ready = core.semaphore(s + "_own_ready")
        inverse_ready = core.semaphore(s + "_inverse_ready")
        o_ready = core.semaphore(s + "_o_ready")
        o_flipped = core.semaphore(s + "_o_flipped")
        oT_ready = core.semaphore(s + "_oT_ready")
        out_done = core.semaphore(s + "_out_done")
        x_ready = core.semaphore(s + "_x_ready")
        x_biased = core.semaphore(s + "_x_biased")
        ones_ready = core.plain_semaphore(s + "_ones_ready")
        ctx_landed = core.plain_semaphore(s + "_ctx_landed")
        core.start_stage(w.landed[s], w.count[s])
        bank = core.bank
        Q, K, V = SCORE, SCORE + 1, SCORE + 2
        OT, OUT = 2 * D, 3 * D

        with nc.Block() as block:
            if cross:
                @block.sync
                def _(sp):
                    with sp.Fori(0, GROUPS) as i:
                        sp.wait_ge(v_done, at(i, 1, 0))
                        sp.dma_start(source[:, :], ctxT_dram[:, bass.ts(i, GM)]).then_inc(ctx_landed, 16)

            @block.gpsimd
            def _(pool):
                def own_of(i, u):
                    pool.wait_ge(k_kept, at(i, 1, 1))
                    pool.wait_ge(sm.scored, at(i, U, u - 1))
                    h = HU * (u % 2)
                    nc.gpsimd.tensor_tensor(own[:, u % 2, :, :],
                                            kT[:, u // 2, :].unsqueeze(1).to_broadcast([P, HU, keys]),
                                            t["head_of"][:, h:h + HU].unsqueeze(2).to_broadcast([P, HU, keys]),
                                            ALU.mult).then_inc(own_ready, 1)

                def bias_x(i):
                    if cross:
                        pool.wait_ge(ln.xn_ready, at(i, G, G))
                        x = core.x[:, bass.ts(i, G), :]
                        nc.gpsimd.tensor_tensor(x, x, t["bo"][:, :].unsqueeze(1).to_broadcast([P, G, D]),
                                                ALU.add).then_inc(x_biased, 1)

                def turn(i, more):
                    for u in range(2, U):
                        if u == 4 and more:
                            ln.rstd_by_gpsimd(pool, i + 1)
                        own_of(i, u)
                    if more:
                        own_of(i + 1, 0)
                        own_of(i + 1, 1)
                        bias_x(i + 1)

                nc.gpsimd.memset(v[:, :, :, :], 1.0).then_inc(ones_ready, 1)
                ln.rstd_by_gpsimd(pool, 0)
                own_of(0, 0)
                own_of(0, 1)
                bias_x(0)
                turns(pool, turn)

            @block.scalar
            def _(act):
                def turn(i, more):
                    for u in range(1, U + 3):
                        if u >= 4 and u % 2 == 0:
                            n = (u - 4) // 2
                            act.wait_ge(o_flipped, at(i, G, n + 1))
                            nc.scalar.copy(oT[:, n % 2, :], bank[:, WORK + n % 2, OT:OT + T]).then_inc(oT_ready, 1)
                        if u <= U:
                            sm.pT_by_scalar(act, i, u - 1)
                        if u == NORM_FLIP and more:
                            ln.xnT_by_scalar(act, i + 1, bank[:, FLIP, :])
                        if u < U:
                            sm.exp_by_scalar(act, i, u)
                    if more:
                        sm.exp_by_scalar(act, i + 1, 0)

                nc.scalar.preload_act_table_set("exp_and_others")
                ln.xnT_by_scalar(act, 0, bank[:, FLIP, :])
                sm.exp_by_scalar(act, 0, 0)
                turns(act, turn)

            @block.vector
            def _(dve):
                def keep_qk(i):
                    dve.wait_ge(q_done, at(i, 1, 1))
                    k_out = kT[:, :, :].rearrange("p n m -> p (n m)")
                    k_in = bank[:, K, 0:G * keys]
                    if cross:
                        dve.wait_ge(k_done, at(i, 1, 1))
                        nc.vector.tensor_scalar(k_out, k_in, t["bk"][:, 0:1], None, ALU.add).then_inc(k_kept, 1)
                        nc.vector.tensor_scalar(qT[:, :], bank[:, Q, :], t["bq"][:, 0:1], float(DH) ** -0.5,
                                                ALU.add, ALU.mult).then_inc(q_kept, 1)
                    else:
                        dve.wait_ge(k_done, at(i, 1, 1))
                        nc.vector.tensor_copy(k_out, k_in).then_inc(k_kept, 1)
                        nc.vector.tensor_scalar(qT[:, :], bank[:, Q, :], float(DH) ** -0.5, None,
                                                ALU.mult).then_inc(q_kept, 1)

                def keep_v(i):
                    dve.wait_ge(v_done, at(i, 1, 1))
                    v_in = bank[0:keys, V, :].rearrange("m (n h d) -> m n h d", h=H, d=DH)
                    v_out = v[0:keys, :, :, 0:DH]
                    if cross:
                        nc.vector.tensor_tensor(v_out, v_in, t["bv"][:, :].rearrange("m (h d) -> m h d", d=DH).unsqueeze(
                            1).to_broadcast([M, G, H, DH]), ALU.add).then_inc(v_kept, 1)
                    else:
                        nc.vector.tensor_copy(v_out, v_in).then_inc(v_kept, 1)

                def head_outputs(i, n):
                    out = bank[:, WORK + n % 2, 0:H * (DH + 1)].rearrange("p (h d) -> p h d", d=DH + 1)
                    dve.wait_ge(sm.weighed, at(i, U, 2 * n + 2))
                    nc.vector.reciprocal(inverse[:, n % 2, :], out[:, :, DH]).then_inc(inverse_ready, 1)
                    dve.wait_ge(inverse_ready, at(i, G, n + 1))
                    nc.vector.tensor_tensor(o[:, n % 2, :].rearrange("p (h d) -> p h d", d=DH), out[:, :, 0:DH],
                                            inverse[:, n % 2, :].unsqueeze(2).to_broadcast([P, H, DH]),
                                            ALU.mult).then_inc(o_ready, 1)

                def add_to_x(i, n):
                    dve.wait_ge(out_done, at(i, G, n + 1))
                    if cross:
                        dve.wait_ge(x_biased, at(i, 1, 1))
                    x = core.x[:, bass.ds(i * G + n, 1), :]
                    nc.vector.tensor_tensor(x, bank[:, WORK + n % 2, OUT:OUT + D].unsqueeze(1), x,
                                            ALU.add).then_inc(x_ready, 1)

                def turn(i, more):
                    chain = Chain(dve, chain_v, i + 1, 1)
                    for u in range(1, U + 2):
                        if u < U:
                            sm.lower_by_vector(dve, i, u)
                        elif u == U and more:
                            keep_qk(i + 1)
                        if u >= 5 and u % 2 == 1:
                            add_to_x(i, (u - 5) // 2)
                        if u >= 3 and u % 2 == 1:
                            head_outputs(i, (u - 3) // 2)
                        if u == 2 and more:
                            ln.moments_by_vector(chain, ln.source(i + 1))
                        if u == 4 and more:
                            ln.scaled_by_vector(dve, i + 1, ln.xn, ln.source(i + 1), ln.xn_ready)
                    if more:
                        keep_v(i + 1)
                        sm.lower_by_vector(dve, i + 1, 0)
                    add_to_x(i, G - 1)

                dve.wait_ge(ones_ready, 1)
                ln.norm_by_vector(dve, 0, Chain(dve, chain_v, 0, 1))
                keep_qk(0)
                keep_v(0)
                sm.lower_by_vector(dve, 0, 0)
                turns(dve, turn)

            @block.tensor
            def _(pe):
                def project_qk(i):
                    pe.wait_ge(ln.xnT_ready, at(i, 1, 1))
                    pe.wait_ge(sm.banks_read(), at(i, U, -1))
                    if cross:
                        pe.wait_ge(ctx_landed, (i + 1) * 16)
                    nc.tensor.matmul(bank[:, K, 0:G * keys], t["k"][:, :], source[:, :], start=True,
                                     stop=True).then_inc(k_done, 1)
                    nc.tensor.matmul(bank[:, Q, :], t["q"][:, :], ln.xnT[:, :], start=True,
                                     stop=True).then_inc(q_done, 1)

                def project_v(i):
                    pe.wait_ge(sm.banks_read(), at(i, U, 0))
                    for n in range(G):
                        last = nc.tensor.matmul(bank[0:keys, V, n * D:(n + 1) * D],
                                                source[:, n * keys:(n + 1) * keys], t["v"][:, :], start=True, stop=True)
                    last.then_inc(v_done, 1)

                def scores_of(i, u):
                    if u == 0:
                        pe.wait_ge(q_kept, at(i, 1, 1))
                    else:
                        pe.wait_ge(v_kept, at(i, 1, 1))
                        pe.wait_ge(sm.banks_read(), at(i, U, u - 1))
                    pe.wait_ge(own_ready, at(i, U, u + 1))
                    n = u // 2
                    for g in range(2):
                        last = nc.tensor.matmul(bank[:, SCORE + 2 * (u % 2) + g, 0:4 * keys], qT[:, n * T:(n + 1) * T],
                                                own[:, u % 2, 4 * g:4 * g + 4, :].rearrange("p h m -> p (h m)"),
                                                start=True, stop=True)
                    last.then_inc(sm.scored, 1)

                def weigh(i, u):
                    n = u // 2
                    pe.wait_ge(x_ready, at(i, G, max(n - 1, 0)))
                    pe.wait_ge(sm.pT_ready, at(i, QUADS, 2 * u + 2))
                    for j in range(HU):
                        h = HU * (u % 2) + j
                        last = nc.tensor.matmul(bank[:, WORK + n % 2, h * (DH + 1):(h + 1) * (DH + 1)],
                                                sm.pT[0:keys, u % 2, j, :], v[0:keys, n, h, :], start=True, stop=True)
                    last.then_inc(sm.weighed, 1)

                def flip_outputs(i, n):
                    pe.wait_ge(o_ready, at(i, G, n + 1))
                    nc.tensor.transpose(bank[:, WORK + n % 2, OT:OT + T], o[:, n % 2, :],
                                        core.ident[:, :]).then_inc(o_flipped, 1)

                def output_of(i, n):
                    pe.wait_ge(oT_ready, at(i, G, n + 1))
                    nc.tensor.matmul(bank[:, WORK + n % 2, OUT:OUT + D], oT[:, n % 2, :], t["o"][:, :],
                                     start=True, stop=True).then_inc(out_done, 1)

                def turn(i, more):
                    for u in range(1, U + 2):
                        output = u >= 4 and u % 2 == 0
                        if u < U:
                            scores_of(i, u)
                        elif u == U and more:
                            project_qk(i + 1)
                        if output:
                            flip_outputs(i, (u - 4) // 2)
                        if u <= U:
                            sm.flip_by_tensor(pe, i, u - 1, ln if more else None)
                        if u == NORM_FLIP and more:
                            pe.wait_ge(sm.pT_ready, at(i, QUADS, 2 * u - 1))
                            ln.flip_by_tensor(pe, i + 1, bank[:, FLIP, :])
                        if output:
                            output_of(i, (u - 4) // 2)
                        if u >= 2:
                            weigh(i, u - 2)
                    if more:
                        project_v(i + 1)
                        scores_of(i + 1, 0)
                    flip_outputs(i, G - 1)
                    output_of(i, G - 1)

                ln.flip_by_tensor(pe, 0, bank[:, FLIP, :])
                project_qk(0)
                project_v(0)
                scores_of(0, 0)
                turns(pe, turn)



E3, HID = 8, 256
CHUNKS = HID // P


def stage3_weights(w, a):
    w.s3_norm = w.load("s3", "w_s3_norm", [P, 1], a["s3_norm"].unsqueeze(1))
    w.s3_gateT = w.load("s3", "w_s3_gateT", [P, E3], a["s3_gateT"])
    w.s3_w1T = w.load("s3", "w_s3_w1T", [P, E3 * HID], a["s3_w1T"])
    w.s3_b1 = w.load("s3", "w_s3_b1", [P, E3 * CHUNKS], a["s3_b1T"])
    w.s3_w2T = w.load("s3", "w_s3_w2T", [P, E3 * CHUNKS, D], a["s3_w2T"].rearrange("(c p) d -> p c d", p=P))
    w.s3_b2 = w.load("s3", "w_s3_b2", [E3, D], a["s3_b2"])
    w.s3_count = w.load("s3", "w_s3_count", [P, E3], a["count"][0:E3].unsqueeze(0).to_broadcast([P, E3]))


def stage3(nc, core, w):
    with ExitStack() as local:
        core.local = local
        def sbuf(name, shape, dtype=F32):
            return local.enter_context(nc.sbuf_tensor(name, shape, dtype))

        ln = Norm(core, sbuf, "s3_ln")
        rms = Moments(core, sbuf, "s3_rms", RMS_EPS)
        tokens = sbuf("s3_tokens", [P, G, D])
        square = sbuf("s3_square", [P, G])
        hT = sbuf("s3_hT", [P, 2, CHUNKS, GT])
        best = sbuf("s3_best", [P, G, 8])
        where = sbuf("s3_where", [P, G, 8], U32)
        index = sbuf("s3_index", [P, G, 2])
        logits = sbuf("s3_logits", [P, G, E3])
        gap = sbuf("s3_gap", [P, G])
        share = sbuf("s3_share", [P, G, 2])
        combine = sbuf("s3_combine", [P, G, E3])
        second = sbuf("s3_second", [P, G, E3])
        combineT = sbuf("s3_combineT", [E3, GT])
        total = sbuf("s3_total", [P, G, D])

        sem = core.semaphore
        chain_v = sem("s3_chain_v")
        square_ready = sem("s3_square_ready")
        tokens_ready = sem("s3_tokens_ready")
        logits_done = sem("s3_logits_done")
        gap_ready = sem("s3_gap_ready")
        tanh_ready = sem("s3_tanh_ready")
        combine_ready = sem("s3_combine_ready")
        combine_flipped = sem("s3_combine_flipped")
        combineT_ready = sem("s3_combineT_ready")
        offset_done = sem("s3_offset_done")
        total_started = sem("s3_total_started")
        hidden_done = sem("s3_hidden_done")
        hT_ready = sem("s3_hT_ready")
        expert_done = sem("s3_expert_done")
        added = sem("s3_added")
        x_ready = sem("s3_x_ready")
        core.start_stage(w.landed["s3"], w.count["s3"])
        bank = core.bank
        MISC, LOGITS, HIDDEN, OUT = 0, 1, 2, 6

        with nc.Block() as block:
            @block.gpsimd
            def _(pool):
                with pool.Fori(0, GROUPS) as i:
                    ln.rstd_by_gpsimd(pool, i)
                    rms.rstd_by_gpsimd(pool, i)
                    pool.wait_ge(total_started, at(i, 1, 1))
                    pool.wait_ge(added, at(i, E3 * G, E3 * G))
                    x = core.x[:, bass.ts(i, G), :]
                    nc.gpsimd.tensor_tensor(x, x, total[:, :, :], ALU.add).then_inc(x_ready, 1)

            @block.scalar
            def _(act):
                nc.scalar.preload_act_table_set("gelu_and_others")
                with act.Fori(0, GROUPS) as i:
                    act.wait_ge(ln.flipped, at(i, 1, 1))
                    nc.scalar.activation(ln.xnT[:, :], bank[:, MISC, :], ACT.Copy,
                                         scale=w.s3_norm[:, 0:1]).then_inc(ln.xnT_ready, 1)
                    act.wait_ge(gap_ready, at(i, 1, 1))
                    nc.scalar.activation(gap[:, :], gap[:, :], ACT.Tanh, scale=0.5).then_inc(tanh_ready, 1)
                    act.wait_ge(combine_flipped, at(i, 1, 1))
                    nc.scalar.copy(combineT[:, :], bank[0:E3, MISC, :]).then_inc(combineT_ready, 1)
                    for e in range(E3):
                        act.wait_ge(expert_done, at(i, E3, max(e - 1, 0)))
                        for c in range(CHUNKS):
                            k = e * CHUNKS + c
                            act.wait_ge(hidden_done, at(i, E3 * CHUNKS, k + 1))
                            nc.scalar.activation(hT[:, e % 2, c, :], bank[:, HIDDEN + k % 4, :], ACT.Gelu,
                                                 bias=w.s3_b1[:, k:k + 1]).then_inc(hT_ready, 1)

            @block.vector
            def _(dve):
                with dve.Fori(0, GROUPS) as i:
                    chain = Chain(dve, chain_v, i, 9)
                    ln.norm_by_vector(dve, i, chain)
                    dve.wait_ge(ln.xn_ready, at(i, G, G))
                    for n in range(G):
                        last = nc.vector.bn_stats(rms.stats[:, n, :], ln.xn[:, n, :])
                    chain.link(last)
                    core.hold_vector()
                    for n in range(G):
                        last = nc.vector.bn_aggr(rms.moments[:, n, :], rms.stats[:, n, :])
                    chain.link(last)
                    chain.link(nc.vector.tensor_tensor(square[:, :], rms.moments[:, :, 0], rms.moments[:, :, 0], ALU.mult))
                    nc.vector.tensor_tensor(rms.moments[:, :, 1], rms.moments[:, :, 1], square[:, :],
                                            ALU.add).then_inc(rms.moments_ready, 1)
                    dve.wait_ge(rms.rstd_ready, at(i, 1, 1))
                    for n in range(G):
                        nc.vector.tensor_scalar(tokens[:, n, :], ln.xn[:, n, :], rms.rstd[:, n:n + 1], None,
                                                ALU.mult).then_inc(tokens_ready, 1)

                    dve.wait_ge(logits_done, at(i, 1, 1))
                    chain.link(nc.vector.tensor_copy(
                        logits[:, :, :], bank[:, LOGITS, 0:G * E3].rearrange("p (n e) -> p n e", e=E3)))
                    core.hold_vector()
                    for n in range(G):
                        last = nc.vector.max(best[:, n, :], logits[:, n, :])
                    chain.link(last)
                    nc.vector.tensor_tensor(gap[:, :], best[:, :, 0], best[:, :, 1], ALU.subtract).then_inc(gap_ready, 1)
                    core.hold_vector()
                    for n in range(G):
                        last = nc.vector.max_index(where[:, n, :], best[:, n, :], logits[:, n, :])
                    chain.link(last)
                    nc.vector.tensor_copy(index[:, :, :], where[:, :, 0:2])
                    dve.wait_ge(tanh_ready, at(i, 1, 1))
                    nc.vector.tensor_scalar(share[:, :, 0], gap[:, :], 0.5, 0.5, ALU.mult, ALU.add)
                    chain.link(nc.vector.tensor_scalar(share[:, :, 1], gap[:, :], -0.5, 0.5, ALU.mult, ALU.add))
                    for n in range(G):
                        last = nc.vector.tensor_scalar(second[:, n, :], w.s3_count[:, :], index[:, n, 1:2],
                                                       share[:, n, 1:2], ALU.is_equal, ALU.mult)
                        last = nc.vector.tensor_scalar(combine[:, n, :], w.s3_count[:, :], index[:, n, 0:1],
                                                       share[:, n, 0:1], ALU.is_equal, ALU.mult)
                    chain.link(last)
                    nc.vector.tensor_tensor(combine[:, :, :], combine[:, :, :], second[:, :, :],
                                            ALU.add).then_inc(combine_ready, 1)

                    dve.wait_ge(offset_done, at(i, 1, 1))
                    dve.wait_ge(x_ready, at(i, 1, 0))
                    nc.vector.tensor_tensor(total[:, :, :], bank[:, LOGITS, :].rearrange("p (n d) -> p n d", d=D),
                                            ln.xn[:, :, :], ALU.add).then_inc(total_started, 1)
                    dve.wait_ge(total_started, at(i, 1, 1))
                    for e in range(E3):
                        dve.wait_ge(expert_done, at(i, E3, e + 1))
                        if e > 0:
                            dve.wait_ge(added, at(i, E3 * G, e * G))
                        for n in range(G):
                            nc.vector.scalar_tensor_tensor(
                                out=total[:, n, :], in0=bank[:, OUT + e % 2, n * D:(n + 1) * D],
                                scalar=combine[:, n, e:e + 1], in1=total[:, n, :], op0=ALU.mult,
                                op1=ALU.add).then_inc(added, 1)
                    chain.end()

            @block.tensor
            def _(pe):
                with pe.Fori(0, GROUPS) as i:
                    pe.wait_ge(combineT_ready, at(i, 1, 0))
                    for n in range(G):
                        pe.wait_ge(tokens_ready, at(i, G, n + 1))
                        last = nc.tensor.transpose(bank[:, MISC, n * T:(n + 1) * T], tokens[:, n, :], core.ident[:, :])
                    last.then_inc(ln.flipped, 1)
                    pe.wait_ge(ln.xnT_ready, at(i, 1, 1))
                    pe.wait_ge(total_started, at(i, 1, 0))
                    for n in range(G):
                        last = nc.tensor.matmul(bank[:, LOGITS, n * E3:(n + 1) * E3], ln.xnT[:, n * T:(n + 1) * T],
                                                w.s3_gateT[:, :], start=True, stop=True)
                    last.then_inc(logits_done, 1)

                    def hidden_of(e):
                        for c in range(CHUNKS):
                            k = e * CHUNKS + c
                            pe.wait_ge(hT_ready, at(i, E3 * CHUNKS, max(k - 3, 0)))
                            nc.tensor.matmul(bank[:, HIDDEN + k % 4, :], w.s3_w1T[:, k * P:(k + 1) * P], ln.xnT[:, :],
                                             start=True, stop=True).then_inc(hidden_done, 1)

                    def output_of(e):
                        pe.wait_ge(hT_ready, at(i, E3 * CHUNKS, (e + 1) * CHUNKS))
                        pe.wait_ge(added, at(i, E3 * G, max(e - 1, 0) * G))
                        for n in range(G):
                            for c in range(CHUNKS):
                                last = nc.tensor.matmul(bank[:, OUT + e % 2, n * D:(n + 1) * D],
                                                        hT[:, e % 2, c, n * T:(n + 1) * T],
                                                        w.s3_w2T[:, e * CHUNKS + c, :], start=(c == 0),
                                                        stop=(c == CHUNKS - 1))
                        last.then_inc(expert_done, 1)

                    hidden_of(0)
                    hidden_of(1)
                    for n in range(G):
                        pe.wait_ge(combine_ready, at(i, 1, 1))
                        last = nc.tensor.transpose(bank[0:E3, MISC, n * T:(n + 1) * T], combine[:, n, :],
                                                   core.ident[:, :])
                    last.then_inc(combine_flipped, 1)
                    pe.wait_ge(combineT_ready, at(i, 1, 1))
                    for n in range(G):
                        last = nc.tensor.matmul(bank[:, LOGITS, n * D:(n + 1) * D], combineT[:, n * T:(n + 1) * T],
                                                w.s3_b2[:, :], start=True, stop=True)
                    last.then_inc(offset_done, 1)
                    for e in range(E3):
                        if e >= 1 and e + 1 < E3:
                            hidden_of(e + 1)
                        output_of(e)



FILTERS, TAPS, RES = 4, 101, 64
SPAN = 2 * T - 1


def ramp_constants():
    signal = np.linspace(0.0, 1.0, RES).astype(np.float32)
    distance = np.abs(np.arange(SPAN) - (T - 1)).astype(np.float32) / np.float32(T - 1)
    row = np.clip(np.round(distance * (RES - 1)).astype(np.int64), 0, RES - 1)
    before = row[None, :] - np.arange(TAPS)[:, None]
    return np.where(before >= 0, signal[np.maximum(before, 0)], 0.0).astype(np.float32)


def bias_weights(w, a):
    w.ramp = w.load("s4", "w_ramp", [TAPS, SPAN], a["ramp"])
    w.coeffsT = w.load("s4", "w_coeffsT", [TAPS, FILTERS], a["s4_coeffsT"])
    w.wposT = w.load("s4", "w_wposT", [FILTERS, H], a["s4_wposT"])
    w.flip = w.load("s4", "w_flip", [P, P], a["flip"])
    w.bias = w.core.sbuf("pos_bias", [P, H, T])


def make_bias(nc, core, w, bias_dram):
    with ExitStack() as local:
        core.local = local
        filtered = local.enter_context(nc.sbuf_tensor("filtered", [FILTERS, SPAN], F32))
        by_head = local.enter_context(nc.sbuf_tensor("by_head", [H, SPAN], F32))
        reversed_bias = local.enter_context(nc.sbuf_tensor("reversed_bias", [P, H, T], F32))
        made = core.plain_semaphore("bias_made")
        kept = core.plain_semaphore("bias_kept")
        spilled = core.plain_semaphore("bias_spilled")
        landed = core.plain_semaphore("bias_landed")
        core.start_stage(w.landed["s4"], w.count["s4"])
        with nc.Block() as block:
            @block.tensor
            def _(pe):
                nc.tensor.matmul(core.bank[0:FILTERS, 0, 0:SPAN], w.coeffsT[:, :], w.ramp[:, :], start=True,
                                 stop=True).then_inc(made, 1)
                pe.wait_ge(kept, 1)
                nc.tensor.matmul(core.bank[0:H, 1, 0:SPAN], w.wposT[:, :], filtered[:, :], start=True,
                                 stop=True).then_inc(made, 1)
                pe.wait_ge(landed, 16)
                for g in range(4):
                    nc.tensor.matmul(core.bank[:, 2 + g, :], w.flip[:, :],
                                     reversed_bias[:, 4 * g:4 * g + 4, :].rearrange("p h t -> p (h t)"), start=True,
                                     stop=True).then_inc(made, 1)

            @block.vector
            def _(dve):
                dve.wait_ge(made, 1)
                nc.vector.tensor_copy(filtered[:, :], core.bank[0:FILTERS, 0, 0:SPAN]).then_inc(kept, 1)
                dve.wait_ge(made, 2)
                nc.vector.tensor_copy(by_head[:, :], core.bank[0:H, 1, 0:SPAN]).then_inc(kept, 1)
                for g in range(4):
                    dve.wait_ge(made, 3 + g)
                    nc.vector.tensor_copy(w.bias[:, 4 * g:4 * g + 4, :].rearrange("p h t -> p (h t)"),
                                          core.bank[:, 2 + g, :])

            @block.sync
            def _(sp):
                sp.wait_ge(kept, 2)
                sp.dma_start(bias_dram[:, :], by_head[:, :]).then_inc(spilled, 16)
                sp.wait_ge(spilled, 16)
                runs = bass.AP(bias_dram.tensor, 0, [[1, P], [SPAN, H], [1, T]])
                sp.dma_start(reversed_bias[:, :, :], runs).then_inc(landed, 16)



DH5 = 64
PAIRS = H * DH5 // P


def stage5_weights(w, a):
    w.s5_gamma = w.load("s5", "w_s5_gamma", [P, 1], a["s5_gamma"].unsqueeze(1))
    w.s5_beta = w.load("s5", "w_s5_beta", [P, 1], a["s5_beta"].unsqueeze(1))
    pairs = "(c p) d -> p c d"
    w.s5_wqT = w.load("s5", "w_s5_qT", [P, PAIRS, D], a["s5_wqT"].rearrange(pairs, p=P))
    w.s5_wkT = w.load("s5", "w_s5_kT", [P, PAIRS, D], a["s5_wkT"].rearrange(pairs, p=P))
    w.s5_wvT = w.load("s5", "w_s5_vT", [P, PAIRS, D], a["s5_wvT"].rearrange(pairs, p=P))
    w.s5_wo = w.load("s5", "w_s5_o", [P, PAIRS, D], a["s5_wo"].rearrange(pairs, p=P))
    w.s5_bo = w.load("s5", "w_s5_bo", [P, D], a["s5_bo"].unsqueeze(0).to_broadcast([P, D]))
    w.s5_gate = w.load("s5", "w_s5_gate", [P, 1], a["s5_gate"].unsqueeze(0).to_broadcast([P, 1]))


def stage5(nc, core, w, ctxT_dram):
    with ExitStack() as local:
        core.local = local
        def sbuf(name, shape, dtype=F32):
            return local.enter_context(nc.sbuf_tensor(name, shape, dtype))

        ln = Norm(core, sbuf, "s5_ln")
        ln2 = Moments(core, sbuf, "s5_ln2")
        sm = Softmax(core, sbuf, "s5", M, shares=True)
        xn2 = sbuf("s5_xn2", [P, G, D])
        kq = sbuf("s5_kq", [P, H, D])
        vo = sbuf("s5_vo", [P, H, D])
        ctxT = sbuf("s5_ctxT", [P, GM])
        kT = sbuf("s5_kT", [P, H, GM])
        v = sbuf("s5_v", [P, G, H * D])

        sem = core.semaphore
        chain_v = sem("s5_chain_v")
        xn2_ready = sem("s5_xn2_ready")
        keys_done = sem("s5_keys_done")
        keys_by_scalar = sem("s5_keys_by_scalar")
        keys_by_vector = sem("s5_keys_by_vector")
        values_done = sem("s5_values_done")
        values_kept = sem("s5_values_kept")
        x_ready = sem("s5_x_ready")
        x_biased = sem("s5_x_biased")
        ctx_landed = core.plain_semaphore("s5_ctx_landed")
        tanh_ready = core.plain_semaphore("s5_tanh_ready")
        wo_scaled = core.plain_semaphore("s5_wo_scaled")
        fold_done = core.plain_semaphore("s5_fold_done")
        fold_kept = core.plain_semaphore("s5_fold_kept")
        core.start_stage(w.landed["s5"], w.count["s5"])
        bank = core.bank
        VALUES, OUT = WORK, WORK + 1
        KEYS = H // 2
        QUARTERS = 4

        with nc.Block() as block:
            @block.scalar
            def _(act):
                nc.scalar.activation(w.s5_gate[:, :], w.s5_gate[:, :], ACT.Tanh).then_inc(tanh_ready, 1)

            @block.vector
            def _(dve):
                dve.wait_ge(tanh_ready, 1)
                nc.vector.tensor_scalar(w.s5_wo[:, :, :], w.s5_wo[:, :, :], w.s5_gate[:, 0:1], None,
                                        ALU.mult).then_inc(wo_scaled, 1)
                nc.vector.tensor_scalar(w.s5_bo[:, :], w.s5_bo[:, :], w.s5_gate[:, 0:1], None, ALU.mult)
                for h in range(H):
                    dve.wait_ge(fold_done, h + 1)
                    nc.vector.tensor_scalar(kq[:, h, :], bank[:, h % 8, 0:D], float(DH5) ** -0.5, None, ALU.mult)
                    nc.vector.tensor_copy(vo[:, h, :], bank[:, h % 8, D:2 * D]).then_inc(fold_kept, 1)

            @block.tensor
            def _(pe):
                pe.wait_ge(wo_scaled, 1)
                for h in range(H):
                    c, rows = h // 2, slice(DH5 * (h % 2), DH5 * (h % 2) + DH5)
                    if h >= 8:
                        pe.wait_ge(fold_kept, h - 7)
                    nc.tensor.matmul(bank[:, h % 8, 0:D], w.s5_wkT[rows, c, :], w.s5_wqT[rows, c, :], start=True,
                                     stop=True)
                    nc.tensor.matmul(bank[:, h % 8, D:2 * D], w.s5_wvT[rows, c, :], w.s5_wo[rows, c, :], start=True,
                                     stop=True).then_inc(fold_done, 1)

        def keep_keys(copy, h):
            return copy(kT[:, h, :], bank[:, SCORE + h % 4, 0:GM])

        with nc.Block() as block:
            @block.sync
            def _(sp):
                with sp.Fori(0, GROUPS) as i:
                    sp.wait_ge(values_done, at(i, G * QUARTERS, 0))
                    sp.dma_start(ctxT[:, :], ctxT_dram[:, bass.ts(i, GM)]).then_inc(ctx_landed, 16)

            @block.gpsimd
            def _(pool):
                def norm(i):
                    ln.rstd_by_gpsimd(pool, i)
                    ln2.rstd_by_gpsimd(pool, i)
                    pool.wait_ge(ln.xn_ready, at(i, G, G))
                    x = core.x[:, bass.ts(i, G), :]
                    nc.gpsimd.tensor_tensor(x, x, w.s5_bo[:, :].unsqueeze(1).to_broadcast([P, G, D]),
                                            ALU.add).then_inc(x_biased, 1)

                norm(0)
                turns(pool, lambda i, more: norm(i + 1) if more else None)

            @block.scalar
            def _(act):
                def xnT_of(i):
                    act.wait_ge(ln.flipped, at(i, 1, 1))
                    nc.scalar.activation(ln.xnT[:, :], bank[:, FLIP, :], ACT.Identity, bias=w.s5_beta[:, 0:1],
                                         scale=w.s5_gamma[:, 0:1]).then_inc(ln.xnT_ready, 1)

                def keys_of(i):
                    for h in range(0, H, 2):
                        act.wait_ge(keys_done, at(i, H, h + 1))
                        keep_keys(nc.scalar.copy, h).then_inc(keys_by_scalar, 1)

                def values_of(i, k):
                    act.wait_ge(values_done, at(i, G * QUARTERS, k + 1))
                    n, c = k // QUARTERS, k % QUARTERS
                    nc.scalar.copy(v[0:M, n, c * 512:(c + 1) * 512], bank[0:M, VALUES, :]).then_inc(values_kept, 1)

                def turn(i, more):
                    for u in range(U + 1):
                        if u < U:
                            values_of(i, 2 * u)
                        if u >= 1:
                            sm.pT_by_scalar(act, i, u - 1)
                        if u < U:
                            values_of(i, 2 * u + 1)
                            sm.exp_by_scalar(act, i, u)
                    if more:
                        xnT_of(i + 1)
                        keys_of(i + 1)

                nc.scalar.preload_act_table_set("exp_and_others")
                xnT_of(0)
                keys_of(0)
                turns(act, turn)

            @block.vector
            def _(dve):
                def norm(i):
                    chain = Chain(dve, chain_v, i, 2)

                    def part(u):
                        if u == 2:
                            ln.moments_by_vector(chain, ln.source(i))
                        if u == 3:
                            ln.scaled_by_vector(dve, i, ln.xn, ln.source(i), ln.xn_ready)
                        if u == 4:
                            dve.wait_ge(ln.xn_ready, at(i, G, G))
                            ln2.moments_by_vector(chain, lambda n: ln.xn[:, n, :])
                        if u == 5:
                            ln2.scaled_by_vector(dve, i, xn2, lambda n: ln.xn[:, n, :], xn2_ready)
                    return part

                def keys_of(i):
                    for h in range(1, H, 2):
                        dve.wait_ge(keys_done, at(i, H, h + 1))
                        keep_keys(nc.vector.tensor_copy, h).then_inc(keys_by_vector, 1)

                def add_to_x(i, n):
                    dve.wait_ge(sm.weighed, at(i, U, 2 * n + 2))
                    dve.wait_ge(x_biased, at(i, 1, 1))
                    x = core.x[:, bass.ds(i * G + n, 1), :]
                    nc.vector.tensor_tensor(x, bank[:, OUT, 0:D].unsqueeze(1), x,
                                            ALU.add).then_inc(x_ready, 1)

                def turn(i, more):
                    part = norm(i + 1)
                    sm.lower_by_vector(dve, i, 0)
                    for u in range(1, U + 1):
                        sm.share_by_vector(dve, i, u - 1)
                        if u < U:
                            sm.lower_by_vector(dve, i, u)
                        if more:
                            part(u)
                        if u >= 4 and u % 2 == 0:
                            add_to_x(i, (u - 4) // 2)
                    if more:
                        keys_of(i + 1)
                    add_to_x(i, G - 1)

                first = norm(0)
                for u in range(2, 6):
                    first(u)
                keys_of(0)
                turns(dve, turn)

            @block.tensor
            def _(pe):
                def flip_norm(i):
                    pe.wait_ge(xn2_ready, at(i, G, G))
                    pe.wait_ge(sm.pT_ready, at(i, QUADS, 0))
                    for n in range(G):
                        last = nc.tensor.transpose(bank[:, FLIP, n * T:(n + 1) * T], xn2[:, n, :],
                                                   core.ident[:, :])
                    last.then_inc(ln.flipped, 1)

                def keys_of(i, heads):
                    for h in heads:
                        if h < 4:
                            pe.wait_ge(sm.lowered, at(i, U, 0))
                        else:
                            pe.wait_ge(keys_by_vector if h % 2 else keys_by_scalar, at(i, KEYS, (h - 4) // 2 + 1))
                        if h == 0:
                            pe.wait_ge(ctx_landed, (i + 1) * 16)
                        nc.tensor.matmul(bank[:, SCORE + h % 4, 0:GM], kq[:, h, :], ctxT[:, :], start=True,
                                         stop=True).then_inc(keys_done, 1)

                def values_of(i, k):
                    pe.wait_ge(values_kept, at(i, G * QUARTERS, k))
                    n, c = k // QUARTERS, k % QUARTERS
                    nc.tensor.matmul(bank[0:M, VALUES, :], ctxT[:, n * M:(n + 1) * M],
                                     vo[:, 4 * c:4 * c + 4, :].rearrange("p h d -> p (h d)"), start=True,
                                     stop=True).then_inc(values_done, 1)

                def scores_of(i, u):
                    if u == 0:
                        pe.wait_ge(ln.xnT_ready, at(i, 1, 1))
                        pe.wait_ge(keys_by_scalar, at(i, KEYS, KEYS))
                        pe.wait_ge(keys_by_vector, at(i, KEYS, KEYS))
                    else:
                        pe.wait_ge(sm.lowered, at(i, U, u - 1))
                    n = u // 2
                    for g in range(2):
                        h = HU * (u % 2) + 4 * g
                        last = nc.tensor.matmul(bank[:, SCORE + 2 * (u % 2) + g, 0:4 * M].rearrange(
                            "p (h m) -> p h m", m=M), ln.xnT[:, n * T:(n + 1) * T],
                            kT[:, h:h + 4, n * M:(n + 1) * M], start=True, stop=True)
                    last.then_inc(sm.scored, 1)

                def weigh(i, u):
                    n = u // 2
                    pe.wait_ge(x_ready, at(i, G, n))
                    pe.wait_ge(sm.pT_ready, at(i, QUADS, 2 * u + 2))
                    pe.wait_ge(values_kept, at(i, G * QUARTERS, (n + 1) * QUARTERS))
                    for j in range(HU):
                        h = HU * (u % 2) + j
                        last = nc.tensor.matmul(bank[:, OUT, 0:D], sm.pT[0:M, u % 2, j, :],
                                                v[0:M, n, h * D:(h + 1) * D], start=(h == 0), stop=(h == H - 1))
                    last.then_inc(sm.weighed, 1)

                def turn(i, more):
                    for u in range(U + 2):
                        if u < U:
                            scores_of(i, u)
                            values_of(i, 2 * u)
                        if 1 <= u <= U:
                            sm.flip_by_tensor(pe, i, u - 1)
                        if u < U:
                            values_of(i, 2 * u + 1)
                        elif more and u == U:
                            keys_of(i + 1, range(4))
                            flip_norm(i + 1)
                            keys_of(i + 1, range(4, 8))
                        elif more:
                            keys_of(i + 1, range(8, H))
                        if u >= 2:
                            weigh(i, u - 2)

                flip_norm(0)
                keys_of(0, range(H))
                turns(pe, turn)



E6 = 16
SHARED = 4
EXP6 = 2 * P


def stage6_weights(w, a):
    w.s6_routerT = w.load("s6", "w_s6_routerT", [P, E6], a["s6_routerT"])
    w.s6_count = w.load("s6", "w_s6_count", [P, E6], a["count"].unsqueeze(0).to_broadcast([P, E6]))
    w.s6_gateup = w.load("s6", "w_s6_gateup", [P, E6, EXP6], a["s6_gateup"].rearrange("e d f -> d e f"))
    w.s6_down = w.load("s6", "w_s6_down", [P, E6, D], a["s6_down"].rearrange("e f d -> f e d"))
    w.s6_sgateT = w.load("s6", "w_s6_sgateT", [P, SHARED * P], a["s6_sgateT"])
    w.s6_supT = w.load("s6", "w_s6_supT", [P, SHARED * P], a["s6_supT"])
    w.s6_sdownT = w.load("s6", "w_s6_sdownT", [P, SHARED, D], a["s6_sdownT"].rearrange("(c p) d -> p c d", p=P))


def stage6(nc, core, w, out):
    with ExitStack() as local:
        core.local = local
        def sbuf(name, shape, dtype=F32):
            return local.enter_context(nc.sbuf_tensor(name, shape, dtype))

        ln = Norm(core, sbuf, "s6_ln")
        logits = sbuf("s6_logits", [P, G, E6])
        best = sbuf("s6_best", [P, G, 8])
        where = sbuf("s6_where", [P, G, 8], U32)
        index = sbuf("s6_index", [P, G])
        chosen = sbuf("s6_chosen", [P, G, E6], BF16)
        score = sbuf("s6_score", [P, G])
        scaled = sbuf("s6_scaled", [P, G, D])
        scaledT = sbuf("s6_scaledT", [P, GT])
        silu = sbuf("s6_silu", [P, 2, GT])
        shared = sbuf("s6_shared", [P, 2, GT])
        mask = sbuf("s6_mask", [P, E6, GT], BF16)
        masked = sbuf("s6_masked", [P, 2, GT])
        hidden = sbuf("s6_hidden", [P, GT])
        yT = sbuf("s6_yT", [P, GT])

        sem = core.semaphore
        chain_v = sem("s6_chain_v")
        logits_done = sem("s6_logits_done")
        best_ready = sem("s6_best_ready")
        tanh_ready = sem("s6_tanh_ready")
        chosen_ready = sem("s6_chosen_ready")
        scaled_ready = sem("s6_scaled_ready")
        scaled_flipped = sem("s6_scaled_flipped")
        scaledT_ready = sem("s6_scaledT_ready")
        shared_done = sem("s6_shared_done")
        silu_ready = sem("s6_silu_ready")
        shared_ready = sem("s6_shared_ready")
        shared_read = sem("s6_shared_read")
        mask_done = sem("s6_mask_done")
        mask_ready = sem("s6_mask_ready")
        masked_ready = sem("s6_masked_ready")
        masked_read = sem("s6_masked_read")
        hidden_ready = sem("s6_hidden_ready")
        yT_ready = sem("s6_yT_ready")
        y_flipped = sem("s6_y_flipped")
        x_ready = sem("s6_x_ready")
        out_landed = core.plain_semaphore("s6_out_landed")
        core.start_stage(w.landed["s6"], w.count["s6"])
        bank = core.bank
        MISC, LOGITS, MASK, GATE, UP, SUM, OUT = 0, 1, 2, 4, 5, 6, 7

        with nc.Block() as block:
            @block.sync
            def _(sp):
                with sp.Fori(0, GROUPS) as i:
                    sp.wait_ge(x_ready, at(i, 1, 1))
                    sp.dma_start(out.rearrange("n t d -> t n d")[:, bass.ts(i, G), :],
                                 core.x[:, bass.ts(i, G), :]).then_inc(out_landed, 16)
                sp.wait_ge(out_landed, GROUPS * 16)

            @block.gpsimd
            def _(pool):
                with pool.Fori(0, GROUPS) as i:
                    ln.rstd_by_gpsimd(pool, i)

            @block.scalar
            def _(act):
                nc.scalar.preload_act_table_set("silu_and_others")
                with act.Fori(0, GROUPS) as i:
                    ln.xnT_by_scalar(act, i, bank[:, MISC, :])
                    act.wait_ge(best_ready, at(i, 1, 1))
                    nc.scalar.activation(score[:, :], best[:, :, 0], ACT.Tanh, scale=0.5).then_inc(tanh_ready, 1)
                    for c in range(SHARED):
                        act.wait_ge(shared_done, at(i, SHARED, c + 1))
                        act.wait_ge(shared_ready, at(i, SHARED, max(c - 1, 0)))
                        nc.scalar.activation(silu[:, c % 2, :], bank[:, GATE if c % 2 else MASK, :],
                                             ACT.Silu).then_inc(silu_ready, 1)
                    act.wait_ge(scaled_flipped, at(i, 1, 1))
                    nc.scalar.copy(scaledT[:, :], bank[:, MISC, :]).then_inc(scaledT_ready, 1)
                    for e in range(E6):
                        act.wait_ge(mask_done, at(i, E6, e + 1))
                        nc.scalar.copy(mask[:, e, :], bank[:, MASK + e % 2, :]).then_inc(mask_ready, 1)
                    act.wait_ge(masked_read, at(i, 2 * E6, E6))
                    nc.scalar.activation(silu[:, 0, :], bank[:, GATE, :], ACT.Silu).then_inc(silu_ready, 1)
                    act.wait_ge(masked_read, at(i, 2 * E6, 2 * E6))
                    nc.scalar.copy(yT[:, :], bank[:, SUM, :]).then_inc(yT_ready, 1)

            @block.vector
            def _(dve):
                with dve.Fori(0, GROUPS) as i:
                    chain = Chain(dve, chain_v, i, 5)
                    ln.norm_by_vector(dve, i, chain)

                    dve.wait_ge(logits_done, at(i, 1, 1))
                    chain.link(nc.vector.tensor_copy(
                        logits[:, :, :], bank[:, LOGITS, 0:G * E6].rearrange("p (n e) -> p n e", e=E6)))
                    core.hold_vector()
                    for n in range(G):
                        last = nc.vector.max(best[:, n, :], logits[:, n, :])
                    last.then_inc(best_ready, 1)
                    dve.wait_ge(best_ready, at(i, 1, 1))
                    core.hold_vector()
                    for n in range(G):
                        last = nc.vector.max_index(where[:, n, :], best[:, n, :], logits[:, n, :])
                    chain.link(last)
                    chain.link(nc.vector.tensor_copy(index[:, :], where[:, :, 0]))
                    for n in range(G):
                        last = nc.vector.tensor_scalar(chosen[:, n, :], w.s6_count[:, :], index[:, n:n + 1], None,
                                                       ALU.is_equal)
                    last.then_inc(chosen_ready, 1)
                    dve.wait_ge(tanh_ready, at(i, 1, 1))
                    chain.link(nc.vector.tensor_scalar(score[:, :], score[:, :], 0.5, 0.5, ALU.mult, ALU.add))
                    for n in range(G):
                        last = nc.vector.tensor_scalar(scaled[:, n, :], ln.xn[:, n, :], score[:, n:n + 1], None,
                                                       ALU.mult)
                    last.then_inc(scaled_ready, 1)

                    for c in range(SHARED):
                        dve.wait_ge(silu_ready, at(i, SHARED + 1, c + 1))
                        dve.wait_ge(shared_read, at(i, SHARED, max(c - 1, 0)))
                        nc.vector.tensor_tensor(shared[:, c % 2, :], bank[:, UP if c % 2 else MASK + 1, :],
                                                silu[:, c % 2, :], ALU.mult).then_inc(shared_ready, 1)

                    def mask_tokens(tokens, k):
                        e = k % E6
                        dve.wait_ge(mask_ready, at(i, E6, e + 1))
                        dve.wait_ge(masked_read, at(i, 2 * E6, max(k - 1, 0)))
                        nc.vector.tensor_tensor(masked[:, k % 2, :], tokens, mask[:, e, :],
                                                ALU.mult).then_inc(masked_ready, 1)

                    dve.wait_ge(scaledT_ready, at(i, 1, 1))
                    for e in range(E6):
                        mask_tokens(scaledT[:, :], e)
                    dve.wait_ge(masked_read, at(i, 2 * E6, E6))
                    dve.wait_ge(silu_ready, at(i, SHARED + 1, SHARED + 1))
                    nc.vector.tensor_tensor(hidden[:, :], bank[:, UP, :], silu[:, 0, :],
                                            ALU.mult).then_inc(hidden_ready, 1)
                    dve.wait_ge(hidden_ready, at(i, 1, 1))
                    for e in range(E6):
                        mask_tokens(hidden[:, :], E6 + e)
                    dve.wait_ge(y_flipped, at(i, 1, 1))
                    x = core.x[:, bass.ts(i, G), :]
                    nc.vector.tensor_tensor(x, bank[:, OUT, :].rearrange("p (n d) -> p n d", d=D), x,
                                            ALU.add).then_inc(x_ready, 1)
                    chain.end()

            @block.tensor
            def _(pe):
                with pe.Fori(0, GROUPS) as i:
                    pe.wait_ge(scaledT_ready, at(i, 1, 0))
                    ln.flip_by_tensor(pe, i, bank[:, MISC, :])
                    pe.wait_ge(ln.xnT_ready, at(i, 1, 1))
                    for n in range(G):
                        last = nc.tensor.matmul(bank[:, LOGITS, n * E6:(n + 1) * E6], ln.xnT[:, n * T:(n + 1) * T],
                                                w.s6_routerT[:, :], start=True, stop=True)
                    last.then_inc(logits_done, 1)

                    def shared_hidden(c):
                        if c >= 2:
                            pe.wait_ge(shared_ready, at(i, SHARED, c - 1))
                        nc.tensor.matmul(bank[:, GATE if c % 2 else MASK, :], w.s6_sgateT[:, c * P:(c + 1) * P],
                                         ln.xnT[:, :], start=True, stop=True)
                        nc.tensor.matmul(bank[:, UP if c % 2 else MASK + 1, :], w.s6_supT[:, c * P:(c + 1) * P],
                                         ln.xnT[:, :], start=True, stop=True).then_inc(shared_done, 1)

                    def shared_down(c):
                        pe.wait_ge(shared_ready, at(i, SHARED, c + 1))
                        if c == 0:
                            pe.wait_ge(yT_ready, at(i, 1, 0))
                        nc.tensor.matmul(bank[:, SUM, :], w.s6_sdownT[:, c, :], shared[:, c % 2, :], start=(c == 0),
                                         stop=False).then_inc(shared_read, 1)

                    shared_hidden(0)
                    shared_hidden(1)
                    for c in range(SHARED):
                        if c + 2 < SHARED:
                            shared_hidden(c + 2)
                        shared_down(c)

                    for n in range(G):
                        pe.wait_ge(scaled_ready, at(i, 1, 1))
                        last = nc.tensor.transpose(bank[:, MISC, n * T:(n + 1) * T], scaled[:, n, :], core.ident[:, :])
                    last.then_inc(scaled_flipped, 1)

                    def mask_of(e):
                        pe.wait_ge(chosen_ready, at(i, 1, 1))
                        pe.wait_ge(mask_ready, at(i, E6, max(e - 1, 0)))
                        for n in range(G):
                            last = nc.tensor.matmul(bank[:, MASK + e % 2, n * T:(n + 1) * T],
                                                    chosen[:, n, e:e + 1].to_broadcast([P, P]), core.ident_bf[:, :],
                                                    start=True, stop=True)
                        last.then_inc(mask_done, 1)

                    mask_of(0)
                    mask_of(1)
                    for e in range(E6):
                        pe.wait_ge(masked_ready, at(i, 2 * E6, e + 1))
                        nc.tensor.matmul(bank[:, GATE, :], w.s6_gateup[:, e, 0:P], masked[:, e % 2, :],
                                         start=(e == 0), stop=(e == E6 - 1))
                        nc.tensor.matmul(bank[:, UP, :], w.s6_gateup[:, e, P:EXP6], masked[:, e % 2, :],
                                         start=(e == 0), stop=(e == E6 - 1)).then_inc(masked_read, 1)
                        if e + 2 < E6:
                            mask_of(e + 2)
                    for e in range(E6):
                        pe.wait_ge(masked_ready, at(i, 2 * E6, E6 + e + 1))
                        nc.tensor.matmul(bank[:, SUM, :], w.s6_down[:, e, :], masked[:, e % 2, :], start=False,
                                         stop=(e == E6 - 1)).then_inc(masked_read, 1)
                    pe.wait_ge(yT_ready, at(i, 1, 1))
                    pe.wait_ge(x_ready, at(i, 1, 0))
                    for n in range(G):
                        last = nc.tensor.transpose(bank[:, OUT, n * T:(n + 1) * T], yT[:, n * T:(n + 1) * T],
                                                   core.ident[:, :])
                    last.then_inc(y_flipped, 1)



def laid_out(inputs):
    f = {k: np.asarray(v) for k, v in inputs.items()}
    band, upto, minus_after, own = level_constants()
    out = {"x": f["x"], "band": band, "upto": upto, "minus_after": minus_after, "own": own}
    out["s1_wq"], out["s1_wk"], out["s1_wv"] = f["L0_attn_Wq"], f["L0_attn_Wk"], f["L0_attn_Wv"]
    out["s1_woT"] = f["L0_attn_Wo"].T
    levels = f["L0_attn_Wdl"].reshape(H1, -1, D)[:, :LEVELS].transpose(1, 0, 2).reshape(LEVELS * H1, D)
    out["s1_small"] = np.concatenate([f["L0_attn_Wg"], levels]).T
    out["s1_bias"] = np.concatenate([f["L0_attn_bg"], f["L0_attn_Lparam"][:, :LEVELS].T.reshape(-1)])
    out["s1_g"], out["s1_b"] = f["L0_attn_ln_g"], f["L0_attn_ln_b"]
    out["flip"] = np.eye(P, dtype=np.float32)[::-1]
    out["ctxT"] = f["ctx_1024"].reshape(BATCH * M, D).T
    out["head_of"] = narrow_constants()
    for name in ("q", "k", "v", "o"):
        out[f"s2_w{name}T"] = f[f"L0_xattn_W{name}"].T
        out[f"s2_b{name}"] = f[f"L0_xattn_b{name}"]
    out["s3_norm"], out["s3_gateT"] = f["L0_ffn_norm_weight"], f["L0_ffn_gate_w"].T
    out["s3_w1T"] = f["L0_ffn_w1"].reshape(E3 * HID, D).T
    out["s3_b1T"] = f["L0_ffn_b1"].reshape(E3 * CHUNKS, P).T
    out["s3_w2T"] = f["L0_ffn_w2"].transpose(0, 2, 1).reshape(E3 * HID, D)
    out["s3_b2"] = f["L0_ffn_b2"]
    out["count"] = np.arange(16, dtype=np.float32)
    for k, name in enumerate(("q", "k", "v")):
        out[f"s4_w{name}T"] = f["L1_attn_Wqkv"][k * D:(k + 1) * D].T
    out["s4_woT"] = f["L1_attn_Wout"].T
    out["ramp"], out["s4_coeffsT"], out["s4_wposT"] = ramp_constants(), f["L1_attn_coeffs"].T, f["L1_attn_Wpos"].T
    out["s5_gamma"], out["s5_beta"] = f["L1_xattn_ln_gamma"], f["L1_xattn_ln_beta"]
    out["s5_wqT"], out["s5_wo"] = f["L1_xattn_w_q"].T, f["L1_xattn_w_out"]
    out["s5_wkT"], out["s5_wvT"] = f["L1_xattn_w_kv"][:, :H * DH5].T, f["L1_xattn_w_kv"][:, H * DH5:].T
    out["s5_bo"], out["s5_gate"] = f["L1_xattn_b_out"], f["L1_xattn_gate"]
    out["s6_routerT"], out["s6_gateup"] = f["L1_ffn_router_w"].T, f["L1_ffn_gate_up_proj"]
    out["s6_down"], out["s6_sgateT"] = f["L1_ffn_down_proj"], f["L1_ffn_shared_gate_w"].T
    out["s6_supT"], out["s6_sdownT"] = f["L1_ffn_shared_up_w"].T, f["L1_ffn_shared_down_w"].T
    return {k: np.ascontiguousarray(v) for k, v in out.items()}


def program(nc, a, out, stages=(1, 2, 3, 4, 5, 6)):
    scratch = nc.dram_tensor("lam_scratch", [P, LEVELS, G * H1], F32, kind="Internal").ap()
    bias_dram = nc.dram_tensor("bias_scratch", [H, SPAN], F32, kind="Internal").ap()
    with ExitStack() as ctx:
        core = Core(nc, ctx)
        w = Weights(core)
        stage1_weights(w, a)
        s2 = narrow_weights(w, a, "s2")
        stage3_weights(w, a)
        s4 = narrow_weights(w, a, "s4")
        bias_weights(w, a)
        stage5_weights(w, a)
        stage6_weights(w, a)

        x_landed = ctx.enter_context(nc.semaphore("x_landed"))
        setup_step = ctx.enter_context(nc.semaphore("setup_step"))
        out_landed = ctx.enter_context(nc.semaphore("out_landed"))
        with nc.Block() as block:
            @block.sync
            def _(sp):
                sp.dma_start(core.x[:, :, :], a["x"].rearrange("n t d -> t n d")).then_inc(x_landed, 16)
                for stage, tile, source in w.loads:
                    sp.dma_start(tile[tuple(slice(None) for _ in tile.shape)], source).then_inc(w.landed[stage], 16)
                sp.wait_ge(x_landed, 16)

            @block.gpsimd
            def _(pool):
                nc.gpsimd.memset(core.minus_half[:, :], -0.5)
                for eps, tile in core.eps.items():
                    nc.gpsimd.memset(tile[:, :], eps)
                nc.gpsimd.memset(core.ident[:, :], 0.0).then_inc(setup_step, 1)
                pool.wait_ge(setup_step, 1)
                nc.gpsimd.affine_select(out=core.ident[:, :], in_=core.ident[:, :], compare_op=ALU.not_equal, fill=1.0,
                                        base=0, pattern=[[-1, P]], channel_multiplier=1).then_inc(setup_step, 1)
                pool.wait_ge(setup_step, 2)
                nc.gpsimd.tensor_copy(core.ident_bf[:, :], core.ident[:, :])

        if 1 in stages:
            stage1(nc, core, w, scratch)
        if 2 in stages:
            narrow_attention(nc, core, w, "s2", s2, ctxT_dram=a["ctxT"])
        if 3 in stages:
            stage3(nc, core, w)
        if 4 in stages:
            make_bias(nc, core, w, bias_dram)
            narrow_attention(nc, core, w, "s4", s4, bias=w.bias)
        if 5 in stages:
            stage5(nc, core, w, a["ctxT"])
        if 6 in stages:
            stage6(nc, core, w, out)

        with nc.Block() as block:
            @block.sync
            def _(sp):
                if 6 not in stages:
                    sp.dma_start(out.rearrange("n t d -> t n d"), core.x[:, :, :]).then_inc(out_landed, 16)
                    sp.wait_ge(out_landed, 16)
                for stage in w.landed:
                    sp.wait_ge(w.landed[stage], w.count[stage])


def kernel(**inputs):
    import concourse.bacc as bacc
    from concourse.bass_utils import run_bass_kernel_spmd

    nc = bacc.Bacc("TRN2", target_bir_lowering=False, num_devices=1)
    arrays = laid_out(inputs)
    a = {name: nc.dram_tensor(name, v.shape, mybir.dt.from_np(v.dtype), kind="ExternalInput").ap()
         for name, v in arrays.items()}
    out = nc.dram_tensor("out", (BATCH, T, D), F32, kind="ExternalOutput").ap()
    program(nc, a, out)
    return run_bass_kernel_spmd(nc, [arrays], core_ids=[0]).results[0]["out"]
```

```python
from contextlib import ExitStack

import numpy as np
import concourse.bass as bass
from concourse import mybir

F32 = mybir.dt.float32
BF16 = mybir.dt.bfloat16
U32 = mybir.dt.uint32
ALU = mybir.AluOpType
ACT = mybir.ActivationFunctionType
AX = mybir.AxisListType

P = 128
BATCH = 32
T = 128
D = 128
M = 77
G = 4
GROUPS = BATCH // G
GT = G * T
GM = G * M
LN_EPS = 1e-5
RMS_EPS = 1e-6
CREDIT = 1


def at(i, per_group, k):
    if isinstance(i, int):
        return max(i * per_group + k, 0) + CREDIT
    return i * per_group + (k + CREDIT)


def turns(engine, turn):
    with engine.Fori(0, GROUPS - 1) as i:
        turn(i, True)
    turn(GROUPS - 1, False)


class Chain:

    def __init__(self, engine, semaphore, i, per_group):
        self.engine, self.semaphore, self.i, self.per_group, self.links = engine, semaphore, i, per_group, 0

    def link(self, instruction):
        self.links += 1
        instruction.then_inc(self.semaphore, 1)
        self.engine.wait_ge(self.semaphore, at(self.i, self.per_group, self.links))

    def end(self):
        assert self.links == self.per_group, (self.links, self.per_group)
class Core:

    def __init__(self, nc, ctx):
        self.nc, self.ctx = nc, ctx
        self.local = ctx
        self.fresh = []
        self.x = self.sbuf("x_all", [P, BATCH, D])
        self.ident = self.sbuf("ident", [P, P])
        self.ident_bf = self.sbuf("ident_bf", [P, P], BF16)
        self.minus_half = self.sbuf("minus_half", [P, G])
        self.eps = {LN_EPS: self.sbuf("ln_eps", [P, G]), RMS_EPS: self.sbuf("rms_eps", [P, G])}
        self.spare = self.sbuf("spare", [P, 1])
        self.bank = ctx.enter_context(nc.psum_tensor("bank", [P, 8, 512], F32))

    def sbuf(self, name, shape, dtype=F32):
        return self.ctx.enter_context(self.nc.sbuf_tensor(name, shape, dtype))

    def semaphore(self, name):
        s = self.local.enter_context(self.nc.semaphore(name))
        self.fresh.append((s, CREDIT))
        return s

    def plain_semaphore(self, name):
        s = self.local.enter_context(self.nc.semaphore(name))
        self.fresh.append((s, 0))
        return s

    def hold_vector(self):
        self.nc.vector.tensor_copy(self.spare[:, :], self.minus_half[:, 0:1])

    def start_stage(self, weights_landed, count):
        nc, fresh, self.fresh = self.nc, self.fresh, []
        with nc.Block() as block:
            @block.gpsimd
            def _(pool):
                for s, start in fresh:
                    pool.sem_clear(s)
                    if start:
                        pool.sem_inc(s, start)

            @block.sync
            def _(sp):
                sp.wait_ge(weights_landed, count)


class Moments:

    def __init__(self, core, sbuf, name, eps=LN_EPS):
        self.core, self.nc, self.eps = core, core.nc, eps
        self.stats = sbuf(name + "_stats", [P, G, 6])
        self.moments = sbuf(name + "_moments", [P, G, 2])
        self.variance = sbuf(name + "_variance", [P, G])
        self.rstd = sbuf(name + "_rstd", [P, G])
        self.moments_ready = core.semaphore(name + "_moments_ready")
        self.variance_ready = core.semaphore(name + "_variance_ready")
        self.rstd_ready = core.semaphore(name + "_rstd_ready")

    def moments_by_vector(self, chain, source):
        nc = self.nc
        for n in range(G):
            last = nc.vector.bn_stats(self.stats[:, n, :], source(n))
        chain.link(last)
        self.core.hold_vector()
        for n in range(G):
            last = nc.vector.bn_aggr(self.moments[:, n, :], self.stats[:, n, :])
        last.then_inc(self.moments_ready, 1)

    def rstd_by_gpsimd(self, pool, i):
        nc = self.nc
        pool.wait_ge(self.moments_ready, at(i, 1, 1))
        nc.gpsimd.tensor_tensor(self.variance[:, :], self.moments[:, :, 1], self.core.eps[self.eps][:, :],
                                ALU.add).then_inc(self.variance_ready, 1)
        pool.wait_ge(self.variance_ready, at(i, 1, 1))
        nc.gpsimd.tensor_tensor(self.rstd[:, :], self.variance[:, :], self.core.minus_half[:, :],
                                ALU.pow).then_inc(self.rstd_ready, 1)

    def scaled_by_vector(self, dve, i, out, source, ready):
        nc = self.nc
        dve.wait_ge(self.rstd_ready, at(i, 1, 1))
        for n in range(G):
            nc.vector.tensor_scalar(out[:, n, :], source(n), self.moments[:, n, 0:1], self.rstd[:, n:n + 1],
                                    ALU.subtract, ALU.mult).then_inc(ready, 1)


class Norm(Moments):

    def __init__(self, core, sbuf, name):
        super().__init__(core, sbuf, name)
        self.xn = sbuf(name + "_xn", [P, G, D])
        self.xnT = sbuf(name + "_xnT", [P, GT])
        self.xn_ready = core.semaphore(name + "_xn_ready")
        self.flipped = core.semaphore(name + "_flipped")
        self.xnT_ready = core.semaphore(name + "_xnT_ready")

    def source(self, i):
        return lambda n: self.core.x[:, bass.ds(i * G + n, 1), :]

    def norm_by_vector(self, dve, i, chain):
        self.moments_by_vector(chain, self.source(i))
        self.scaled_by_vector(dve, i, self.xn, self.source(i), self.xn_ready)

    def flip_by_tensor(self, pe, i, bank):
        nc = self.nc
        for n in range(G):
            pe.wait_ge(self.xn_ready, at(i, G, n + 1))
            last = nc.tensor.transpose(bank[:, n * T:(n + 1) * T], self.xn[:, n, :], self.core.ident[:, :])
        last.then_inc(self.flipped, 1)

    def xnT_by_scalar(self, act, i, bank):
        act.wait_ge(self.flipped, at(i, 1, 1))
        self.nc.scalar.copy(self.xnT[:, :], bank[:, :]).then_inc(self.xnT_ready, 1)


class Weights:

    def __init__(self, core):
        self.core, self.loads, self.landed, self.count = core, [], {}, {}

    def load(self, stage, name, shape, source, dtype=F32):
        if stage not in self.landed:
            self.landed[stage] = self.core.ctx.enter_context(self.core.nc.semaphore(f"{stage}_weights_landed"))
            self.count[stage] = 0
        tile = self.core.sbuf(name, shape, dtype)
        self.loads.append((stage, tile, source))
        self.count[stage] += 16
        return tile

    def start_loads(self, sp, wanted):
        for stage, tile, source in self.loads:
            if wanted(stage):
                sp.dma_start(tile[tuple(slice(None) for _ in tile.shape)], source).then_inc(self.landed[stage], 16)



H1 = 8
LEVELS = 8
TB = P // LEVELS
NB = T // TB
SMALL = H1 + LEVELS * H1
HALF = NB // 2 * H1 * TB


def level_constants():
    band = np.zeros((LEVELS, TB, 2 * T - TB), np.float32)
    for b in range(TB):
        for c in range(2 * T - TB):
            distance = b - (c - (T - TB))
            if 0 <= distance < T:
                band[0 if distance == 0 else int(np.log2(distance)) + 1, b, c] = 1.0
    u, t = np.arange(T)[:, None], np.arange(T)[None, :]
    upto = (u <= t).astype(np.float32)
    minus_after = -(u > t).astype(np.float32)
    own = np.tile(np.eye(TB, dtype=np.float32), (LEVELS, 1))
    return band.reshape(P, 2 * T - TB), upto, minus_after, own


def stage1_weights(w, a):
    heads = "(h s) d -> s h d"
    w.s1_wq = w.load("s1", "w_s1_q", [P, H1, D], a["s1_wq"].rearrange(heads, s=P))
    w.s1_wk = w.load("s1", "w_s1_k", [P, H1, D], a["s1_wk"].rearrange(heads, s=P))
    w.s1_wv = w.load("s1", "w_s1_v", [P, H1, D], a["s1_wv"].rearrange(heads, s=P))
    w.s1_woT = w.load("s1", "w_s1_oT", [P, H1, D], a["s1_woT"].rearrange(heads, s=P))
    w.s1_small = w.load("s1", "w_s1_small", [P, SMALL], a["s1_small"])
    w.s1_bias = w.load("s1", "w_s1_bias", [P, SMALL], a["s1_bias"].unsqueeze(0).to_broadcast([P, SMALL]))
    w.s1_g = w.load("s1", "w_s1_g", [P, D], a["s1_g"].unsqueeze(0).to_broadcast([P, D]))
    w.s1_b = w.load("s1", "w_s1_b", [P, D], a["s1_b"].unsqueeze(0).to_broadcast([P, D]))
    w.band = w.load("s1", "w_band", [P, 2 * T - TB], a["band"])
    w.upto = w.load("s1", "w_upto", [P, T], a["upto"])
    w.minus_after = w.load("s1", "w_minus_after", [P, T], a["minus_after"])
    w.own = w.load("s1", "w_own", [P, TB], a["own"])


def stage1(nc, core, w, scratch):
    with ExitStack() as local:
        core.local = local
        def sbuf(name, shape, dtype=F32):
            return local.enter_context(nc.sbuf_tensor(name, shape, dtype))

        ln = Norm(core, sbuf, "s1_ln")
        ln2 = Moments(core, sbuf, "s1_ln2")
        qk = sbuf("s1_qk", [P, H1, D])
        vo = sbuf("s1_vo", [P, H1, D])
        qT = sbuf("s1_qT", [P, G * NB, H1, TB])
        v = sbuf("s1_v", [P, G, H1 * D])
        pre = sbuf("s1_pre", [P, 1 + LEVELS, G, H1])
        log = sbuf("s1_log", [P, 1 + LEVELS, G, H1])
        soft = sbuf("s1_soft", [P, 1 + LEVELS, G, H1])
        lam = sbuf("s1_lam", [P, NB, G, H1])
        gate = sbuf("s1_gate", [P, 2, NB, H1, TB])
        level = sbuf("s1_level", [P, 2, NB, H1, TB])
        decay = sbuf("s1_decay", [P, 2, 2, HALF])
        weight = sbuf("s1_weight", [P, 2, HALF])
        aT = sbuf("s1_aT", [P, 2, H1, T])
        xnT = sbuf("s1_xnT", [P, GT])
        y = sbuf("s1_y", [P, G, D])
        z = sbuf("s1_z", [P, G, D])

        fold_done = core.plain_semaphore("s1_fold_done")
        fold_kept = core.plain_semaphore("s1_fold_kept")
        chain_v = core.semaphore("s1_chain_v")
        tail_v = core.semaphore("s1_tail_v")
        xnT_ready = core.semaphore("s1_xnT_ready")
        y_started = core.semaphore("s1_y_started")
        chain_p = core.semaphore("s1_chain_p")
        small_done = core.semaphore("s1_small_done")
        pre_kept = core.semaphore("s1_pre_kept")
        magnitude_ready = core.semaphore("s1_magnitude_ready")
        exp_ready = core.semaphore("s1_exp_ready")
        log_ready = core.semaphore("s1_log_ready")
        soft_ready = core.semaphore("s1_soft_ready")
        projected = core.semaphore("s1_projected")
        kept_by_scalar = core.semaphore("s1_kept_by_scalar")
        kept_by_vector = core.semaphore("s1_kept_by_vector")
        gate_ready = core.semaphore("s1_gate_ready")
        level_ready = core.semaphore("s1_level_ready")
        logdecay_done = core.semaphore("s1_logdecay_done")
        decay_ready = core.semaphore("s1_decay_ready")
        level_done = core.semaphore("s1_level_done")
        weight_ready = core.semaphore("s1_weight_ready")
        score_done = core.semaphore("s1_score_done")
        aT_ready = core.semaphore("s1_aT_ready")
        out_done = core.semaphore("s1_out_done")
        y_ready = core.semaphore("s1_y_ready")
        z_ready = core.semaphore("s1_z_ready")
        x_ready = core.semaphore("s1_x_ready")
        spilled = core.plain_semaphore("s1_spilled")
        lam_landed = core.plain_semaphore("s1_lam_landed")

        core.start_stage(w.landed["s1"], w.count["s1"])
        bank = core.bank
        LOGDECAY, LEVEL, SCORE, WORK = 0, 2, 4, 6
        PROJ = H1 + 2 * G

        with nc.Block() as block:
            @block.tensor
            def _(pe):
                for h in range(H1):
                    if h >= 2:
                        pe.wait_ge(fold_kept, h - 1)
                    nc.tensor.matmul(bank[:, h % 2, 0:D], w.s1_wq[:, h, :], w.s1_wk[:, h, :], start=True, stop=True)
                    nc.tensor.matmul(bank[:, h % 2, D:2 * D], w.s1_wv[:, h, :], w.s1_woT[:, h, :], start=True,
                                     stop=True).then_inc(fold_done, 1)

            @block.vector
            def _(dve):
                for h in range(H1):
                    dve.wait_ge(fold_done, h + 1)
                    nc.vector.tensor_scalar(qk[:, h, :], bank[:, h % 2, 0:D], float(D) ** -0.5, None, ALU.mult)
                    nc.vector.tensor_copy(vo[:, h, :], bank[:, h % 2, D:2 * D]).then_inc(fold_kept, 1)

        def keep(copy, k):
            source = bank[:, LOGDECAY + k % 2, :]
            if k < H1:
                return copy(qT[:, :, k, :], source.rearrange("p (a b) -> p a b", b=TB))
            n, c = (k - H1) // 2, (k - H1) % 2
            return copy(v[:, n, c * 512:(c + 1) * 512], source)

        with nc.Block() as block:
            @block.sync
            def _(sp):
                def rearrange_levels(i):
                    sp.wait_ge(soft_ready, at(i, 1, 1))
                    sp.dma_start(scratch[:, :, :],
                                 soft[:, 1:, :, :].rearrange("p l n h -> p l (n h)")).then_inc(spilled, 16)
                    sp.wait_ge(spilled, (i + 1) * 16)
                    for l in range(LEVELS):
                        sp.dma_start(lam[l * TB:(l + 1) * TB, :, :, :].rearrange("b a n h -> b a (n h)"),
                                     scratch[:, l, :].rearrange("(a b) c -> b a c", b=TB)).then_inc(lam_landed, 16)

                rearrange_levels(0)
                w.start_loads(sp, lambda stage: stage != "s1")
                with sp.Fori(1, GROUPS) as i:
                    rearrange_levels(i)
                sp.wait_ge(lam_landed, GROUPS * 16 * LEVELS)

            @block.gpsimd
            def _(pool):
                def gate_and_level(i, n):
                    free = 2 * max(n - 1, 0)
                    if n == 0:
                        pool.wait_ge(soft_ready, at(i, 1, 1))
                    pool.wait_ge(logdecay_done, at(i, 2 * G, free))
                    nc.gpsimd.tensor_tensor(
                        gate[:, n % 2, :, :, :],
                        w.upto[:, :].rearrange("p (a b) -> p a b", b=TB).unsqueeze(2).to_broadcast([P, NB, H1, TB]),
                        soft[:, 0, n, :].unsqueeze(1).unsqueeze(3).to_broadcast([P, NB, H1, TB]),
                        ALU.mult).then_inc(gate_ready, 1)
                    if n == 0:
                        pool.wait_ge(lam_landed, (i + 1) * (16 * LEVELS))
                    pool.wait_ge(level_done, at(i, 2 * G, free))
                    nc.gpsimd.tensor_tensor(
                        level[:, n % 2, :, :, :],
                        lam[:, :, n, :].unsqueeze(3).to_broadcast([P, NB, H1, TB]),
                        w.own[:, :].unsqueeze(1).unsqueeze(1).to_broadcast([P, NB, H1, TB]),
                        ALU.mult).then_inc(level_ready, 1)

                def turn(i, more):
                    chain = Chain(pool, chain_p, i, 2)
                    for n in range(1, G):
                        gate_and_level(i, n)
                        if n == 1 and more:
                            ln.rstd_by_gpsimd(pool, i + 1)
                    if more:
                        gate_and_level(i + 1, 0)
                    ln2.rstd_by_gpsimd(pool, i)
                    pool.wait_ge(z_ready, at(i, G, G))
                    chain.link(nc.gpsimd.tensor_tensor(
                        z[:, :, :], z[:, :, :], w.s1_g[:, :].unsqueeze(1).to_broadcast([P, G, D]), ALU.mult))
                    chain.link(nc.gpsimd.tensor_tensor(
                        z[:, :, :], z[:, :, :], w.s1_b[:, :].unsqueeze(1).to_broadcast([P, G, D]), ALU.add))
                    x = core.x[:, bass.ts(i, G), :]
                    nc.gpsimd.tensor_tensor(x, x, z[:, :, :], ALU.add).then_inc(x_ready, 1)
                    chain.end()

                ln.rstd_by_gpsimd(pool, 0)
                gate_and_level(0, 0)
                turns(pool, turn)

            @block.scalar
            def _(act):
                def exponentials(i):
                    act.wait_ge(magnitude_ready, at(i, 1, 1))
                    nc.scalar.activation(log[:, :, :, :], log[:, :, :, :], ACT.Exp).then_inc(exp_ready, 1)
                    act.wait_ge(exp_ready, at(i, 1, 1))
                    nc.scalar.activation(log[:, :, :, :], log[:, :, :, :], ACT.Ln, bias=1.0).then_inc(log_ready, 1)

                def keep_projections(i):
                    for k in range(0, PROJ, 2):
                        act.wait_ge(projected, at(i, PROJ, k + 1))
                        keep(nc.scalar.copy, k).then_inc(kept_by_scalar, 1)
                        if k == 2:
                            act.wait_ge(score_done, at(i, 2 * G, 0))
                            nc.scalar.copy(xnT[:, :], ln.xnT[:, :]).then_inc(xnT_ready, 1)

                def turn(i, more):
                    for n in range(G):
                        act.wait_ge(weight_ready, at(i, 2 * G, 2 * max(n - 1, 0)))
                        for j in range(2):
                            act.wait_ge(logdecay_done, at(i, 2 * G, 2 * n + j + 1))
                            nc.scalar.activation(decay[:, n % 2, j, :], bank[:, LOGDECAY + j, :],
                                                 ACT.Exp).then_inc(decay_ready, 1)
                        if n == 2 and more:
                            ln.xnT_by_scalar(act, i + 1, bank[:, WORK, :])
                    if more:
                        exponentials(i + 1)
                        keep_projections(i + 1)

                nc.scalar.preload_act_table_set("natural_log_exp_and_others")
                ln.xnT_by_scalar(act, 0, bank[:, WORK, :])
                exponentials(0)
                keep_projections(0)
                turns(act, turn)

            @block.vector
            def _(dve):
                def magnitudes(i, chain):
                    dve.wait_ge(small_done, at(i, 1, 1))
                    chain.link(nc.vector.tensor_tensor(
                        pre[:, :, :, :].rearrange("p l n h -> p n l h"),
                        bank[:, WORK + 1, 0:G * SMALL].rearrange("p (n l h) -> p n l h", n=G, h=H1),
                        w.s1_bias[:, :].rearrange("p (l h) -> p l h", h=H1).unsqueeze(1).to_broadcast(
                            [P, G, 1 + LEVELS, H1]), ALU.add))
                    nc.vector.scalar_tensor_tensor(out=log[:, :, :, :], in0=pre[:, :, :, :], scalar=-1.0,
                                                   in1=pre[:, :, :, :], op0=ALU.mult,
                                                   op1=ALU.min).then_inc(magnitude_ready, 1)

                def softplus(i):
                    dve.wait_ge(log_ready, at(i, 1, 1))
                    nc.vector.scalar_tensor_tensor(out=soft[:, :, :, :], in0=pre[:, :, :, :], scalar=0.0,
                                                   in1=log[:, :, :, :], op0=ALU.max, op1=ALU.add).then_inc(soft_ready, 1)

                def keep_projections(i, banks):
                    for k in banks:
                        dve.wait_ge(projected, at(i, PROJ, k + 1))
                        keep(nc.vector.tensor_copy, k).then_inc(kept_by_vector, 1)

                def y_of(i, n):
                    dve.wait_ge(out_done, at(i, G, n + 1))
                    dve.wait_ge(y_started, at(i, 1, 1))
                    nc.vector.tensor_tensor(y[:, n, :], bank[:, WORK + n % 2, 0:D], y[:, n, :],
                                            ALU.add).then_inc(y_ready, 1)

                def turn(i, more):
                    chain = Chain(dve, chain_v, i + 1, 2)
                    dve.wait_ge(ln.xn_ready, at(i, G, G))
                    dve.wait_ge(z_ready, at(i, G, 0))
                    nc.vector.tensor_copy(y[:, :, :], ln.xn[:, :, :]).then_inc(y_started, 1)
                    for n in range(G):
                        if n >= 1:
                            y_of(i, n - 1)
                        if n == 1 and more:
                            ln.moments_by_vector(chain, ln.source(i + 1))
                        if n == G - 1 and more:
                            magnitudes(i + 1, chain)
                        for j in range(2):
                            dve.wait_ge(decay_ready, at(i, 2 * G, 2 * n + j + 1))
                            dve.wait_ge(level_done, at(i, 2 * G, 2 * n + j + 1))
                            nc.vector.tensor_tensor(weight[:, j, :], bank[:, LEVEL + j, :], decay[:, n % 2, j, :],
                                                    ALU.mult).then_inc(weight_ready, 1)
                        dve.wait_ge(out_done, at(i, G, max(n - 1, 0)))
                        for j in range(2):
                            dve.wait_ge(weight_ready, at(i, 2 * G, 2 * n + j + 1))
                            dve.wait_ge(score_done, at(i, 2 * G, 2 * n + j + 1))
                            nc.vector.tensor_tensor(
                                aT[:, n % 2, :, j * (T // 2):(j + 1) * (T // 2)].rearrange("p h (a b) -> p a h b", b=TB),
                                bank[:, SCORE + j, :].rearrange("p (a h b) -> p a h b", h=H1, b=TB),
                                weight[:, j, :].rearrange("p (a h b) -> p a h b", h=H1, b=TB),
                                ALU.mult).then_inc(aT_ready, 1)
                        if n == 1 and more:
                            ln.scaled_by_vector(dve, i + 1, ln.xn, ln.source(i + 1), ln.xn_ready)
                    if more:
                        softplus(i + 1)
                        keep_projections(i + 1, (1, 3))
                    y_of(i, G - 1)
                    if more:
                        keep_projections(i + 1, (5,))
                    dve.wait_ge(y_ready, at(i, G, G))
                    tail = Chain(dve, tail_v, i, 1)
                    ln2.moments_by_vector(tail, lambda n: y[:, n, :])
                    if more:
                        keep_projections(i + 1, (7,))
                    dve.wait_ge(x_ready, at(i, 1, 0))
                    ln2.scaled_by_vector(dve, i, z, lambda n: y[:, n, :], z_ready)
                    if more:
                        keep_projections(i + 1, range(9, PROJ, 2))

                chain = Chain(dve, chain_v, 0, 2)
                ln.norm_by_vector(dve, 0, chain)
                magnitudes(0, chain)
                softplus(0)
                keep_projections(0, range(1, PROJ, 2))
                turns(dve, turn)

            @block.tensor
            def _(pe):
                def small_projections(i):
                    pe.wait_ge(ln.xnT_ready, at(i, 1, 1))
                    for n in range(G):
                        last = nc.tensor.matmul(bank[:, WORK + 1, n * SMALL:(n + 1) * SMALL],
                                                ln.xnT[:, n * T:(n + 1) * T], w.s1_small[:, :], start=True, stop=True)
                    last.then_inc(small_done, 1)

                def project(i, banks):
                    for k in banks:
                        if k < 2:
                            pe.wait_ge(decay_ready, at(i, 2 * G, k - 1))
                        else:
                            pe.wait_ge(kept_by_vector if k % 2 else kept_by_scalar, at(i, PROJ // 2, k // 2))
                        if k < H1:
                            nc.tensor.matmul(bank[:, LOGDECAY + k % 2, :], qk[:, k, :], ln.xnT[:, :], start=True,
                                             stop=True).then_inc(projected, 1)
                        else:
                            n, c = (k - H1) // 2, (k - H1) % 2
                            nc.tensor.matmul(bank[:, LOGDECAY + k % 2, :], ln.xnT[:, n * T:(n + 1) * T],
                                             vo[:, c * (H1 // 2):(c + 1) * (H1 // 2), :].rearrange("p h d -> p (h d)"),
                                             start=True, stop=True).then_inc(projected, 1)

                def logdecay_of(i, n):
                    pe.wait_ge(gate_ready, at(i, G, n + 1))
                    for j in range(2):
                        if n >= 1:
                            pe.wait_ge(decay_ready, at(i, 2 * G, 2 * n + j - 1))
                        nc.tensor.matmul(bank[:, LOGDECAY + j, :], w.minus_after[:, :],
                                         gate[:, n % 2, j * (NB // 2):(j + 1) * (NB // 2), :, :].rearrange(
                                             "p a h b -> p (a h b)"), start=True, stop=True).then_inc(logdecay_done, 1)

                def level_of(i, n):
                    pe.wait_ge(level_ready, at(i, G, n + 1))
                    for j in range(2):
                        pe.wait_ge(weight_ready, at(i, 2 * G, max(2 * n + j - 1, 0)))
                        for c in range(NB // 2):
                            a = j * (NB // 2) + c
                            start = T - TB - TB * a
                            last = nc.tensor.matmul(
                                bank[:, LEVEL + j, c * H1 * TB:(c + 1) * H1 * TB], w.band[:, start:start + T],
                                level[:, n % 2, a, :, :].rearrange("p h b -> p (h b)"), start=True, stop=True)
                        last.then_inc(level_done, 1)

                def scores_of(i, n):
                    pe.wait_ge(xnT_ready, at(i, 1, 1))
                    for j in range(2):
                        pe.wait_ge(aT_ready, at(i, 2 * G, max(2 * n + j - 1, 0)))
                        first = n * NB + j * (NB // 2)
                        nc.tensor.matmul(bank[:, SCORE + j, :], xnT[:, n * T:(n + 1) * T],
                                         qT[:, first:first + NB // 2, :, :].rearrange("p a h b -> p (a h b)"),
                                         start=True, stop=True).then_inc(score_done, 1)

                def out_of(i, n):
                    pe.wait_ge(aT_ready, at(i, 2 * G, 2 * n + 2))
                    pe.wait_ge(y_ready, at(i, G, max(n - 1, 0)))
                    for h in range(H1):
                        last = nc.tensor.matmul(bank[:, WORK + n % 2, 0:D], aT[:, n % 2, h, :],
                                                v[:, n, h * D:(h + 1) * D], start=(h == 0), stop=(h == H1 - 1))
                    last.then_inc(out_done, 1)

                def turn(i, more):
                    level_of(i, 0)
                    pe.wait_ge(kept_by_scalar, at(i, PROJ // 2, PROJ // 2))
                    pe.wait_ge(kept_by_vector, at(i, PROJ // 2, PROJ // 2))
                    logdecay_of(i, 0)
                    scores_of(i, 0)
                    for n in range(1, G):
                        logdecay_of(i, n)
                        if n == G - 1 and more:
                            pe.wait_ge(y_ready, at(i, G, n - 1))
                            small_projections(i + 1)
                        out_of(i, n - 1)
                        if n == G - 2 and more:
                            pe.wait_ge(y_ready, at(i, G, n - 1))
                            ln.flip_by_tensor(pe, i + 1, bank[:, WORK, :])
                        level_of(i, n)
                        scores_of(i, n)
                    if more:
                        project(i + 1, range(4))
                        pe.wait_ge(magnitude_ready, at(i + 1, 1, 1))
                    out_of(i, G - 1)
                    if more:
                        project(i + 1, range(4, PROJ))

                ln.flip_by_tensor(pe, 0, bank[:, WORK, :])
                small_projections(0)
                project(0, range(PROJ))
                turns(pe, turn)



H = 16
HU = 8
U = G * H // HU
QUADS = 2 * U
SCORE, FLIP, WORK = 0, 4, 6
NORM_FLIP = U - 2


class Softmax:

    def __init__(self, core, sbuf, name, keys, bias=None, shares=False):
        self.core, self.nc, self.keys, self.bias, self.shares = core, core.nc, keys, bias, shares
        self.p = sbuf(name + "_p", [P, 2, HU, keys])
        self.peak = sbuf(name + "_peak", [P, 2, HU])
        self.pT = sbuf(name + "_pT", [P, 2, HU, T])
        self.scored = core.semaphore(name + "_scored")
        self.biased = core.semaphore(name + "_biased")
        self.peak_ready = core.semaphore(name + "_peak_ready")
        self.lowered = core.semaphore(name + "_lowered")
        self.exp_ready = core.semaphore(name + "_exp_ready")
        self.p_flipped = core.semaphore(name + "_p_flipped")
        self.pT_ready = core.semaphore(name + "_pT_ready")
        self.weighed = core.semaphore(name + "_weighed")
        if shares:
            self.total = sbuf(name + "_total", [P, 2, HU])
            self.inverse = sbuf(name + "_inverse", [P, 2, HU])
            self.total_ready = core.semaphore(name + "_total_ready")
            self.inverse_ready = core.semaphore(name + "_inverse_ready")
            self.share_ready = core.semaphore(name + "_share_ready")

    def lower_by_vector(self, dve, i, u):
        nc = self.nc
        p = self.p[:, u % 2, :, :]
        p4 = p.rearrange("p (g j) m -> p g j m", j=4)
        peak = self.peak[:, u % 2, :]
        first = SCORE + 2 * (u % 2)
        scores = self.core.bank[:, first:first + 2, 0:4 * self.keys].rearrange("p g (j m) -> p g j m", m=self.keys)
        dve.wait_ge(self.scored, at(i, U, u + 1))
        dve.wait_ge(self.p_flipped, at(i, QUADS, max(2 * u - 2, 0)))
        if self.bias is None:
            nc.vector.tensor_reduce(peak.rearrange("p (g j) -> p g j", j=4), scores, AX.X,
                                    ALU.max).then_inc(self.peak_ready, 1)
            dve.wait_ge(self.peak_ready, at(i, U, u + 1))
            nc.vector.tensor_tensor(p4, scores, peak.rearrange("p (g j) -> p g j", j=4).unsqueeze(3).to_broadcast(
                [P, 2, 4, self.keys]), ALU.subtract).then_inc(self.lowered, 1)
        else:
            h = HU * (u % 2)
            nc.vector.tensor_tensor(p.rearrange("p h m -> p (h m)"), scores.rearrange("p g j m -> p (g j m)"),
                                    self.bias[:, h:h + HU, :].rearrange("p h m -> p (h m)"),
                                    ALU.add).then_inc(self.biased, 1)
            dve.wait_ge(self.biased, at(i, U, u + 1))
            nc.vector.tensor_reduce(peak, p, AX.X, ALU.max).then_inc(self.peak_ready, 1)
            dve.wait_ge(self.peak_ready, at(i, U, u + 1))
            nc.vector.tensor_tensor(p, p, peak.unsqueeze(2).to_broadcast([P, HU, self.keys]),
                                    ALU.subtract).then_inc(self.lowered, 1)

    def banks_read(self):
        return self.lowered if self.bias is None else self.biased

    def exp_by_scalar(self, act, i, u):
        p = self.p[:, u % 2, :, :]
        act.wait_ge(self.lowered, at(i, U, u + 1))
        self.nc.scalar.activation(p, p, ACT.Exp).then_inc(self.exp_ready, 1)

    def share_by_vector(self, dve, i, u):
        nc = self.nc
        p = self.p[:, u % 2, :, :]
        dve.wait_ge(self.exp_ready, at(i, U, u + 1))
        nc.vector.tensor_reduce(self.total[:, u % 2, :], p, AX.X, ALU.add).then_inc(self.total_ready, 1)
        dve.wait_ge(self.total_ready, at(i, U, u + 1))
        nc.vector.reciprocal(self.inverse[:, u % 2, :], self.total[:, u % 2, :]).then_inc(self.inverse_ready, 1)
        dve.wait_ge(self.inverse_ready, at(i, U, u + 1))
        nc.vector.tensor_tensor(p, p, self.inverse[:, u % 2, :].unsqueeze(2).to_broadcast([P, HU, self.keys]),
                                ALU.mult).then_inc(self.share_ready, 1)

    def flip_by_tensor(self, pe, i, u, norm=None):
        nc = self.nc
        pe.wait_ge(self.share_ready if self.shares else self.exp_ready, at(i, U, u + 1))
        for q in (2 * u, 2 * u + 1):
            pe.wait_ge(self.pT_ready, at(i, QUADS, max(q - 1, 0)))
            if norm is not None and q == 2 * NORM_FLIP:
                pe.wait_ge(norm.xnT_ready, at(i + 1, 1, 1))
            for j in range(4):
                last = nc.tensor.transpose(self.core.bank[0:self.keys, FLIP + q % 2, j * T:(j + 1) * T],
                                           self.p[:, u % 2, 4 * (q % 2) + j, :], self.core.ident[:, :])
            last.then_inc(self.p_flipped, 1)

    def pT_by_scalar(self, act, i, u):
        act.wait_ge(self.weighed, at(i, U, max(u - 1, 0)))
        for q in (2 * u, 2 * u + 1):
            h = 4 * (q % 2)
            act.wait_ge(self.p_flipped, at(i, QUADS, q + 1))
            self.nc.scalar.copy(self.pT[0:self.keys, u % 2, h:h + 4, :].rearrange("m h t -> m (h t)"),
                                self.core.bank[0:self.keys, FLIP + q % 2, :]).then_inc(self.pT_ready, 1)



DH = D // H
LANE = P // 4


def narrow_constants():
    return (np.arange(D)[:, None] // DH == np.arange(H)[None, :]).astype(np.float32)


def narrow_weights(w, a, s):
    t = {}
    for name in ("q", "k", "v", "o"):
        t[name] = w.load(s, f"w_{s}_{name}", [P, D], a[f"{s}_w{name}T"])
    if s == "s2":
        t["bq"] = w.load(s, f"w_{s}_bq", [P, 1], a[f"{s}_bq"].unsqueeze(1))
        t["bk"] = w.load(s, f"w_{s}_bk", [P, 1], a[f"{s}_bk"].unsqueeze(1))
        t["bv"] = w.load(s, f"w_{s}_bv", [M, D], a[f"{s}_bv"].unsqueeze(0).to_broadcast([M, D]))
        t["bo"] = w.load(s, f"w_{s}_bo", [P, D], a[f"{s}_bo"].unsqueeze(0).to_broadcast([P, D]))
    t["head_of"] = w.load(s, f"w_{s}_head_of", [P, H], a["head_of"])
    return t


def narrow_attention(nc, core, w, s, t, ctxT_dram=None, bias=None):
    cross = ctxT_dram is not None
    keys = M if cross else T
    with ExitStack() as local:
        core.local = local
        def sbuf(name, shape, dtype=F32):
            return local.enter_context(nc.sbuf_tensor(name, shape, dtype))

        ln = Norm(core, sbuf, s + "_ln")
        sm = Softmax(core, sbuf, s, keys, bias)
        source = sbuf(s + "_ctxT", [P, GM]) if cross else ln.xnT
        qT = sbuf(s + "_qT", [P, GT])
        kT = sbuf(s + "_kT", [P, G, keys])
        own = sbuf(s + "_own", [P, 2, HU, keys])
        v = sbuf(s + "_v", [P, G, H, LANE])
        weighedT = sbuf(s + "_weighedT", [P, H // 4, T])
        inverse = sbuf(s + "_inverse", [P, 2, H])
        o = sbuf(s + "_o", [P, 2, D])
        oT = sbuf(s + "_oT", [P, 2, T])

        chain_v = core.semaphore(s + "_chain_v")
        q_done = core.semaphore(s + "_q_done")
        k_done = core.semaphore(s + "_k_done")
        v_done = core.semaphore(s + "_v_done")
        q_kept = core.semaphore(s + "_q_kept")
        k_kept = core.semaphore(s + "_k_kept")
        v_kept = core.semaphore(s + "_v_kept")
        own_ready = core.semaphore(s + "_own_ready")
        weighedT_ready = core.semaphore(s + "_weighedT_ready")
        weighed_flipped = core.semaphore(s + "_weighed_flipped")
        inverse_ready = core.semaphore(s + "_inverse_ready")
        o_ready = core.semaphore(s + "_o_ready")
        o_flipped = core.semaphore(s + "_o_flipped")
        oT_ready = core.semaphore(s + "_oT_ready")
        out_done = core.semaphore(s + "_out_done")
        x_ready = core.semaphore(s + "_x_ready")
        x_biased = core.semaphore(s + "_x_biased")
        ones_ready = core.plain_semaphore(s + "_ones_ready")
        ctx_landed = core.plain_semaphore(s + "_ctx_landed")
        core.start_stage(w.landed[s], w.count[s])
        bank = core.bank
        Q, K, V = SCORE, SCORE + 1, SCORE + 2
        WEIGHED, TAIL = WORK, WORK + 1
        OT, OUT = 0, D

        with nc.Block() as block:
            if cross:
                @block.sync
                def _(sp):
                    with sp.Fori(0, GROUPS) as i:
                        sp.wait_ge(v_done, at(i, 1, 0))
                        sp.dma_start(source[:, :], ctxT_dram[:, bass.ts(i, GM)]).then_inc(ctx_landed, 16)

            @block.gpsimd
            def _(pool):
                def own_of(i, u):
                    pool.wait_ge(k_kept, at(i, 1, 1))
                    pool.wait_ge(sm.scored, at(i, U, u - 1))
                    h = HU * (u % 2)
                    nc.gpsimd.tensor_tensor(own[:, u % 2, :, :],
                                            kT[:, u // 2, :].unsqueeze(1).to_broadcast([P, HU, keys]),
                                            t["head_of"][:, h:h + HU].unsqueeze(2).to_broadcast([P, HU, keys]),
                                            ALU.mult).then_inc(own_ready, 1)

                def bias_x(i):
                    if cross:
                        pool.wait_ge(ln.xn_ready, at(i, G, G))
                        x = core.x[:, bass.ts(i, G), :]
                        nc.gpsimd.tensor_tensor(x, x, t["bo"][:, :].unsqueeze(1).to_broadcast([P, G, D]),
                                                ALU.add).then_inc(x_biased, 1)

                def turn(i, more):
                    for u in range(2, U):
                        if u == 4 and more:
                            ln.rstd_by_gpsimd(pool, i + 1)
                        own_of(i, u)
                    if more:
                        own_of(i + 1, 0)
                        own_of(i + 1, 1)
                        bias_x(i + 1)

                nc.gpsimd.memset(v[:, :, :, :], 0.0).then_inc(ones_ready, 1)
                pool.wait_ge(ones_ready, 1)
                nc.gpsimd.memset(v[:, :, :, DH:DH + 1], 1.0).then_inc(ones_ready, 1)
                ln.rstd_by_gpsimd(pool, 0)
                own_of(0, 0)
                own_of(0, 1)
                bias_x(0)
                turns(pool, turn)

            @block.scalar
            def _(act):
                def oT_of(i, n):
                    act.wait_ge(o_flipped, at(i, G, n + 1))
                    nc.scalar.copy(oT[:, n % 2, :], bank[:, TAIL, OT:OT + T]).then_inc(oT_ready, 1)

                def turn(i, more):
                    for u in range(1, U + 2):
                        if u >= 4 and u % 2 == 0:
                            oT_of(i, (u - 4) // 2)
                        if u >= 3 and u % 2 == 1:
                            act.wait_ge(sm.weighed, at(i, U, u - 1))
                            nc.scalar.copy(weighedT[:, :, :].rearrange("p g t -> p (g t)"),
                                           bank[:, WEIGHED, :]).then_inc(weighedT_ready, 1)
                        if u <= U:
                            sm.pT_by_scalar(act, i, u - 1)
                        if u == NORM_FLIP and more:
                            ln.xnT_by_scalar(act, i + 1, bank[:, FLIP, :])
                        if u < U:
                            sm.exp_by_scalar(act, i, u)
                    oT_of(i, G - 1)
                    if more:
                        sm.exp_by_scalar(act, i + 1, 0)

                nc.scalar.preload_act_table_set("exp_and_others")
                ln.xnT_by_scalar(act, 0, bank[:, FLIP, :])
                sm.exp_by_scalar(act, 0, 0)
                turns(act, turn)

            @block.vector
            def _(dve):
                def keep_qk(i):
                    dve.wait_ge(q_done, at(i, 1, 1))
                    k_out = kT[:, :, :].rearrange("p n m -> p (n m)")
                    k_in = bank[:, K, 0:G * keys]
                    if cross:
                        dve.wait_ge(k_done, at(i, 1, 1))
                        nc.vector.tensor_scalar(k_out, k_in, t["bk"][:, 0:1], None, ALU.add).then_inc(k_kept, 1)
                        nc.vector.tensor_scalar(qT[:, :], bank[:, Q, :], t["bq"][:, 0:1], float(DH) ** -0.5,
                                                ALU.add, ALU.mult).then_inc(q_kept, 1)
                    else:
                        dve.wait_ge(k_done, at(i, 1, 1))
                        nc.vector.tensor_copy(k_out, k_in).then_inc(k_kept, 1)
                        nc.vector.tensor_scalar(qT[:, :], bank[:, Q, :], float(DH) ** -0.5, None,
                                                ALU.mult).then_inc(q_kept, 1)

                def keep_v(i):
                    dve.wait_ge(v_done, at(i, 1, 1))
                    dve.wait_ge(sm.weighed, at(i, U, 0))
                    v_in = bank[0:keys, V, :].rearrange("m (n h d) -> m n h d", h=H, d=DH)
                    v_out = v[0:keys, :, :, 0:DH]
                    if cross:
                        nc.vector.tensor_tensor(v_out, v_in, t["bv"][:, :].rearrange("m (h d) -> m h d", d=DH).unsqueeze(
                            1).to_broadcast([M, G, H, DH]), ALU.add).then_inc(v_kept, 1)
                    else:
                        nc.vector.tensor_copy(v_out, v_in).then_inc(v_kept, 1)

                def head_outputs(i, n):
                    out = bank[:, TAIL, :].rearrange("p (h d) -> p h d", d=LANE)
                    dve.wait_ge(weighed_flipped, at(i, G, n + 1))
                    nc.vector.reciprocal(inverse[:, n % 2, :], out[:, :, DH]).then_inc(inverse_ready, 1)
                    dve.wait_ge(inverse_ready, at(i, G, n + 1))
                    nc.vector.tensor_tensor(o[:, n % 2, :].rearrange("p (h d) -> p h d", d=DH), out[:, :, 0:DH],
                                            inverse[:, n % 2, :].unsqueeze(2).to_broadcast([P, H, DH]),
                                            ALU.mult).then_inc(o_ready, 1)

                def add_to_x(i, n):
                    dve.wait_ge(out_done, at(i, G, n + 1))
                    if cross:
                        dve.wait_ge(x_biased, at(i, 1, 1))
                    x = core.x[:, bass.ds(i * G + n, 1), :]
                    nc.vector.tensor_tensor(x, bank[:, TAIL, OUT:OUT + D].unsqueeze(1), x,
                                            ALU.add).then_inc(x_ready, 1)

                def turn(i, more):
                    chain = Chain(dve, chain_v, i + 1, 1)
                    for u in range(1, U + 1):
                        if u >= 4 and u % 2 == 0:
                            head_outputs(i, (u - 4) // 2)
                        if u < U:
                            sm.lower_by_vector(dve, i, u)
                        elif more:
                            keep_qk(i + 1)
                        if u >= 4 and u % 2 == 0:
                            add_to_x(i, (u - 4) // 2)
                        if u == 2 and more:
                            ln.moments_by_vector(chain, ln.source(i + 1))
                        if u == 4 and more:
                            ln.scaled_by_vector(dve, i + 1, ln.xn, ln.source(i + 1), ln.xn_ready)
                    if more:
                        keep_v(i + 1)
                    head_outputs(i, G - 1)
                    if more:
                        sm.lower_by_vector(dve, i + 1, 0)
                    add_to_x(i, G - 1)

                dve.wait_ge(ones_ready, 2)
                ln.norm_by_vector(dve, 0, Chain(dve, chain_v, 0, 1))
                keep_qk(0)
                keep_v(0)
                sm.lower_by_vector(dve, 0, 0)
                turns(dve, turn)

            @block.tensor
            def _(pe):
                def project_qk(i):
                    pe.wait_ge(ln.xnT_ready, at(i, 1, 1))
                    pe.wait_ge(sm.banks_read(), at(i, U, -1))
                    if cross:
                        pe.wait_ge(ctx_landed, (i + 1) * 16)
                    nc.tensor.matmul(bank[:, K, 0:G * keys], t["k"][:, :], source[:, :], start=True,
                                     stop=True).then_inc(k_done, 1)
                    nc.tensor.matmul(bank[:, Q, :], t["q"][:, :], ln.xnT[:, :], start=True,
                                     stop=True).then_inc(q_done, 1)

                def project_v(i):
                    pe.wait_ge(sm.banks_read(), at(i, U, 0))
                    for n in range(G):
                        last = nc.tensor.matmul(bank[0:keys, V, n * D:(n + 1) * D],
                                                source[:, n * keys:(n + 1) * keys], t["v"][:, :], start=True, stop=True)
                    last.then_inc(v_done, 1)

                def scores_of(i, u):
                    if u == 0:
                        pe.wait_ge(q_kept, at(i, 1, 1))
                    else:
                        pe.wait_ge(v_kept, at(i, 1, 1))
                        pe.wait_ge(sm.banks_read(), at(i, U, u - 1))
                    pe.wait_ge(own_ready, at(i, U, u + 1))
                    n = u // 2
                    for g in range(2):
                        last = nc.tensor.matmul(bank[:, SCORE + 2 * (u % 2) + g, 0:4 * keys], qT[:, n * T:(n + 1) * T],
                                                own[:, u % 2, 4 * g:4 * g + 4, :].rearrange("p h m -> p (h m)"),
                                                start=True, stop=True)
                    last.then_inc(sm.scored, 1)

                def weigh(i, u):
                    n = u // 2
                    pe.wait_ge(weighedT_ready, at(i, G, n))
                    pe.wait_ge(sm.pT_ready, at(i, QUADS, 2 * u + 2))
                    for j in range(HU):
                        h = HU * (u % 2) + j
                        last = nc.tensor.matmul(bank[h % 4 * LANE:(h % 4 + 1) * LANE, WEIGHED, h // 4 * T:(h // 4 + 1) * T],
                                                v[0:keys, n, h, :], sm.pT[0:keys, u % 2, j, :], start=True, stop=True,
                                                tile_position=(0, h % 4 * LANE))
                    last.then_inc(sm.weighed, 1)

                def flip_weighed(i, n):
                    pe.wait_ge(weighedT_ready, at(i, G, n + 1))
                    pe.wait_ge(x_ready, at(i, G, n))
                    for g in range(H // 4):
                        last = nc.tensor.transpose(bank[:, TAIL, g * T:(g + 1) * T], weighedT[:, g, :],
                                                   core.ident[:, :])
                    last.then_inc(weighed_flipped, 1)

                def flip_outputs(i, n):
                    pe.wait_ge(o_ready, at(i, G, n + 1))
                    nc.tensor.transpose(bank[:, TAIL, OT:OT + T], o[:, n % 2, :],
                                        core.ident[:, :]).then_inc(o_flipped, 1)

                def output_of(i, n):
                    pe.wait_ge(oT_ready, at(i, G, n + 1))
                    nc.tensor.matmul(bank[:, TAIL, OUT:OUT + D], oT[:, n % 2, :], t["o"][:, :],
                                     start=True, stop=True).then_inc(out_done, 1)

                def turn(i, more):
                    for u in range(1, U + 2):
                        output = u >= 4 and u % 2 == 0
                        if u < U:
                            scores_of(i, u)
                        elif more and u == U:
                            project_qk(i + 1)
                        elif more:
                            project_v(i + 1)
                        if output:
                            flip_outputs(i, (u - 4) // 2)
                        if u >= 2:
                            weigh(i, u - 2)
                        if output:
                            output_of(i, (u - 4) // 2)
                        if u <= U:
                            sm.flip_by_tensor(pe, i, u - 1, ln if more else None)
                        if u == NORM_FLIP and more:
                            pe.wait_ge(sm.pT_ready, at(i, QUADS, 2 * u - 1))
                            ln.flip_by_tensor(pe, i + 1, bank[:, FLIP, :])
                        if u >= 3 and u % 2 == 1:
                            flip_weighed(i, (u - 3) // 2)
                    if more:
                        scores_of(i + 1, 0)
                    flip_outputs(i, G - 1)
                    output_of(i, G - 1)

                ln.flip_by_tensor(pe, 0, bank[:, FLIP, :])
                project_qk(0)
                project_v(0)
                scores_of(0, 0)
                turns(pe, turn)



E3, HID = 8, 256
CHUNKS = HID // P


def stage3_weights(w, a):
    w.s3_norm = w.load("s3", "w_s3_norm", [P, 1], a["s3_norm"].unsqueeze(1))
    w.s3_gateT = w.load("s3", "w_s3_gateT", [P, E3], a["s3_gateT"])
    w.s3_w1T = w.load("s3", "w_s3_w1T", [P, E3 * HID], a["s3_w1T"])
    w.s3_b1 = w.load("s3", "w_s3_b1", [P, E3 * CHUNKS], a["s3_b1T"])
    w.s3_w2T = w.load("s3", "w_s3_w2T", [P, E3 * CHUNKS, D], a["s3_w2T"].rearrange("(c p) d -> p c d", p=P))
    w.s3_b2 = w.load("s3", "w_s3_b2", [E3, D], a["s3_b2"])
    w.s3_count = w.load("s3", "w_s3_count", [P, E3], a["count"][0:E3].unsqueeze(0).to_broadcast([P, E3]))


def stage3(nc, core, w):
    with ExitStack() as local:
        core.local = local
        def sbuf(name, shape, dtype=F32):
            return local.enter_context(nc.sbuf_tensor(name, shape, dtype))

        ln = Norm(core, sbuf, "s3_ln")
        rms = Moments(core, sbuf, "s3_rms", RMS_EPS)
        tokens = sbuf("s3_tokens", [P, G, D])
        square = sbuf("s3_square", [P, G])
        hT = sbuf("s3_hT", [P, 2, CHUNKS, GT])
        best = sbuf("s3_best", [P, G, 8])
        where = sbuf("s3_where", [P, G, 8], U32)
        index = sbuf("s3_index", [P, G, 2])
        logits = sbuf("s3_logits", [P, G, E3])
        gap = sbuf("s3_gap", [P, G])
        share = sbuf("s3_share", [P, G, 2])
        combine = sbuf("s3_combine", [P, G, E3])
        second = sbuf("s3_second", [P, G, E3])
        combineT = sbuf("s3_combineT", [E3, GT])
        total = sbuf("s3_total", [P, G, D])

        sem = core.semaphore
        chain_v = sem("s3_chain_v")
        routing_v = sem("s3_routing_v")
        square_ready = sem("s3_square_ready")
        tokens_ready = sem("s3_tokens_ready")
        logits_done = sem("s3_logits_done")
        gap_ready = sem("s3_gap_ready")
        tanh_ready = sem("s3_tanh_ready")
        combine_ready = sem("s3_combine_ready")
        combine_flipped = sem("s3_combine_flipped")
        combineT_ready = sem("s3_combineT_ready")
        offset_done = sem("s3_offset_done")
        total_started = sem("s3_total_started")
        hidden_done = sem("s3_hidden_done")
        hT_ready = sem("s3_hT_ready")
        expert_done = sem("s3_expert_done")
        added = sem("s3_added")
        x_ready = sem("s3_x_ready")
        core.start_stage(w.landed["s3"], w.count["s3"])
        bank = core.bank
        MISC, LOGITS, HIDDEN, OUT = 0, 1, 2, 6

        with nc.Block() as block:
            @block.gpsimd
            def _(pool):
                def norm(i):
                    ln.rstd_by_gpsimd(pool, i)
                    rms.rstd_by_gpsimd(pool, i)

                def turn(i, more):
                    if more:
                        norm(i + 1)
                    pool.wait_ge(total_started, at(i, 1, 1))
                    pool.wait_ge(added, at(i, E3 * G, E3 * G))
                    x = core.x[:, bass.ts(i, G), :]
                    nc.gpsimd.tensor_tensor(x, x, total[:, :, :], ALU.add).then_inc(x_ready, 1)

                norm(0)
                turns(pool, turn)

            @block.scalar
            def _(act):
                def xnT_of(i):
                    act.wait_ge(ln.flipped, at(i, 1, 1))
                    nc.scalar.activation(ln.xnT[:, :], bank[:, MISC, :], ACT.Copy,
                                         scale=w.s3_norm[:, 0:1]).then_inc(ln.xnT_ready, 1)

                def turn(i, more):
                    for e in range(E3):
                        if e == 1:
                            act.wait_ge(gap_ready, at(i, 1, 1))
                            nc.scalar.activation(gap[:, :], gap[:, :], ACT.Tanh, scale=0.5).then_inc(tanh_ready, 1)
                        if e == 2:
                            act.wait_ge(combine_flipped, at(i, 1, 1))
                            nc.scalar.copy(combineT[:, :], bank[0:E3, MISC, :]).then_inc(combineT_ready, 1)
                        act.wait_ge(expert_done, at(i, E3, max(e - 1, 0)))
                        for c in range(CHUNKS):
                            k = e * CHUNKS + c
                            act.wait_ge(hidden_done, at(i, E3 * CHUNKS, k + 1))
                            nc.scalar.activation(hT[:, e % 2, c, :], bank[:, HIDDEN + k % 4, :], ACT.Gelu,
                                                 bias=w.s3_b1[:, k:k + 1]).then_inc(hT_ready, 1)
                    if more:
                        xnT_of(i + 1)

                nc.scalar.preload_act_table_set("gelu_and_others")
                xnT_of(0)
                turns(act, turn)

            @block.vector
            def _(dve):
                def norm(i, chain, part):
                    if part == 1:
                        ln.moments_by_vector(chain, ln.source(i))
                    if part == 2:
                        ln.scaled_by_vector(dve, i, ln.xn, ln.source(i), ln.xn_ready)
                    if part == 3:
                        dve.wait_ge(ln.xn_ready, at(i, G, G))
                        for n in range(G):
                            last = nc.vector.bn_stats(rms.stats[:, n, :], ln.xn[:, n, :])
                        chain.link(last)
                        core.hold_vector()
                        for n in range(G):
                            last = nc.vector.bn_aggr(rms.moments[:, n, :], rms.stats[:, n, :])
                        chain.link(last)
                        chain.link(nc.vector.tensor_tensor(square[:, :], rms.moments[:, :, 0], rms.moments[:, :, 0],
                                                           ALU.mult))
                        nc.vector.tensor_tensor(rms.moments[:, :, 1], rms.moments[:, :, 1], square[:, :],
                                                ALU.add).then_inc(rms.moments_ready, 1)
                    if part == 4:
                        dve.wait_ge(rms.rstd_ready, at(i, 1, 1))
                        for n in range(G):
                            nc.vector.tensor_scalar(tokens[:, n, :], ln.xn[:, n, :], rms.rstd[:, n:n + 1], None,
                                                    ALU.mult).then_inc(tokens_ready, 1)

                def route(i, chain):
                    dve.wait_ge(logits_done, at(i, 1, 1))
                    chain.link(nc.vector.tensor_copy(
                        logits[:, :, :], bank[:, LOGITS, 0:G * E3].rearrange("p (n e) -> p n e", e=E3)))
                    core.hold_vector()
                    for n in range(G):
                        last = nc.vector.max(best[:, n, :], logits[:, n, :])
                    chain.link(last)
                    nc.vector.tensor_tensor(gap[:, :], best[:, :, 0], best[:, :, 1], ALU.subtract).then_inc(gap_ready, 1)
                    core.hold_vector()
                    for n in range(G):
                        last = nc.vector.max_index(where[:, n, :], best[:, n, :], logits[:, n, :])
                    chain.link(last)
                    nc.vector.tensor_copy(index[:, :, :], where[:, :, 0:2])
                    dve.wait_ge(tanh_ready, at(i, 1, 1))
                    nc.vector.tensor_scalar(share[:, :, 0], gap[:, :], 0.5, 0.5, ALU.mult, ALU.add)
                    chain.link(nc.vector.tensor_scalar(share[:, :, 1], gap[:, :], -0.5, 0.5, ALU.mult, ALU.add))
                    for n in range(G):
                        last = nc.vector.tensor_scalar(second[:, n, :], w.s3_count[:, :], index[:, n, 1:2],
                                                       share[:, n, 1:2], ALU.is_equal, ALU.mult)
                        last = nc.vector.tensor_scalar(combine[:, n, :], w.s3_count[:, :], index[:, n, 0:1],
                                                       share[:, n, 0:1], ALU.is_equal, ALU.mult)
                    chain.link(last)
                    nc.vector.tensor_tensor(combine[:, :, :], combine[:, :, :], second[:, :, :],
                                            ALU.add).then_inc(combine_ready, 1)

                def turn(i, more):
                    chain = Chain(dve, routing_v, i, 5)
                    route(i, chain)
                    chain.end()
                    chain = Chain(dve, chain_v, i + 1, 4)
                    dve.wait_ge(offset_done, at(i, 1, 1))
                    dve.wait_ge(x_ready, at(i, 1, 0))
                    nc.vector.tensor_tensor(total[:, :, :], bank[:, LOGITS, :].rearrange("p (n d) -> p n d", d=D),
                                            ln.xn[:, :, :], ALU.add).then_inc(total_started, 1)
                    dve.wait_ge(total_started, at(i, 1, 1))
                    for e in range(E3):
                        dve.wait_ge(expert_done, at(i, E3, e + 1))
                        if e > 0:
                            dve.wait_ge(added, at(i, E3 * G, e * G))
                        for n in range(G):
                            nc.vector.scalar_tensor_tensor(
                                out=total[:, n, :], in0=bank[:, OUT + e % 2, n * D:(n + 1) * D],
                                scalar=combine[:, n, e:e + 1], in1=total[:, n, :], op0=ALU.mult,
                                op1=ALU.add).then_inc(added, 1)
                        if more:
                            norm(i + 1, chain, e)

                chain = Chain(dve, chain_v, 0, 4)
                for part in range(1, 5):
                    norm(0, chain, part)
                chain.end()
                turns(dve, turn)

            @block.tensor
            def _(pe):
                def flip_tokens(i):
                    pe.wait_ge(combineT_ready, at(i, 1, 0))
                    for n in range(G):
                        pe.wait_ge(tokens_ready, at(i, G, n + 1))
                        last = nc.tensor.transpose(bank[:, MISC, n * T:(n + 1) * T], tokens[:, n, :], core.ident[:, :])
                    last.then_inc(ln.flipped, 1)

                def logits_of(i):
                    pe.wait_ge(ln.xnT_ready, at(i, 1, 1))
                    pe.wait_ge(total_started, at(i, 1, 0))
                    for n in range(G):
                        last = nc.tensor.matmul(bank[:, LOGITS, n * E3:(n + 1) * E3], ln.xnT[:, n * T:(n + 1) * T],
                                                w.s3_gateT[:, :], start=True, stop=True)
                    last.then_inc(logits_done, 1)

                def hidden_of(i, e):
                    for c in range(CHUNKS):
                        k = e * CHUNKS + c
                        pe.wait_ge(hT_ready, at(i, E3 * CHUNKS, max(k - 3, 0)))
                        nc.tensor.matmul(bank[:, HIDDEN + k % 4, :], w.s3_w1T[:, k * P:(k + 1) * P], ln.xnT[:, :],
                                         start=True, stop=True).then_inc(hidden_done, 1)

                def output_of(i, e):
                    pe.wait_ge(hT_ready, at(i, E3 * CHUNKS, (e + 1) * CHUNKS))
                    pe.wait_ge(added, at(i, E3 * G, max(e - 1, 0) * G))
                    for n in range(G):
                        for c in range(CHUNKS):
                            last = nc.tensor.matmul(bank[:, OUT + e % 2, n * D:(n + 1) * D],
                                                    hT[:, e % 2, c, n * T:(n + 1) * T],
                                                    w.s3_w2T[:, e * CHUNKS + c, :], start=(c == 0),
                                                    stop=(c == CHUNKS - 1))
                    last.then_inc(expert_done, 1)

                def offset_of(i):
                    pe.wait_ge(combineT_ready, at(i, 1, 1))
                    for n in range(G):
                        last = nc.tensor.matmul(bank[:, LOGITS, n * D:(n + 1) * D], combineT[:, n * T:(n + 1) * T],
                                                w.s3_b2[:, :], start=True, stop=True)
                    last.then_inc(offset_done, 1)

                def flip_combine(i):
                    for n in range(G):
                        pe.wait_ge(combine_ready, at(i, 1, 1))
                        last = nc.tensor.transpose(bank[0:E3, MISC, n * T:(n + 1) * T], combine[:, n, :],
                                                   core.ident[:, :])
                    last.then_inc(combine_flipped, 1)

                def turn(i, more):
                    logits_of(i)
                    hidden_of(i, 0)
                    hidden_of(i, 1)
                    output_of(i, 0)
                    flip_combine(i)
                    hidden_of(i, 2)
                    offset_of(i)
                    for e in range(1, E3):
                        output_of(i, e)
                        if e == E3 - 3 and more:
                            flip_tokens(i + 1)
                        if e + 2 < E3:
                            hidden_of(i, e + 2)

                flip_tokens(0)
                turns(pe, turn)



FILTERS, TAPS, RES = 4, 101, 64
SPAN = 2 * T - 1


def ramp_constants():
    signal = np.linspace(0.0, 1.0, RES).astype(np.float32)
    distance = np.abs(np.arange(SPAN) - (T - 1)).astype(np.float32) / np.float32(T - 1)
    row = np.clip(np.round(distance * (RES - 1)).astype(np.int64), 0, RES - 1)
    before = row[None, :] - np.arange(TAPS)[:, None]
    return np.where(before >= 0, signal[np.maximum(before, 0)], 0.0).astype(np.float32)


def bias_weights(w, a):
    w.ramp = w.load("s4", "w_ramp", [TAPS, SPAN], a["ramp"])
    w.coeffsT = w.load("s4", "w_coeffsT", [TAPS, FILTERS], a["s4_coeffsT"])
    w.wposT = w.load("s4", "w_wposT", [FILTERS, H], a["s4_wposT"])
    w.flip = w.load("s4", "w_flip", [P, P], a["flip"])
    w.bias = w.core.sbuf("pos_bias", [P, H, T])


def make_bias(nc, core, w, bias_dram):
    with ExitStack() as local:
        core.local = local
        filtered = local.enter_context(nc.sbuf_tensor("filtered", [FILTERS, SPAN], F32))
        by_head = local.enter_context(nc.sbuf_tensor("by_head", [H, SPAN], F32))
        reversed_bias = local.enter_context(nc.sbuf_tensor("reversed_bias", [P, H, T], F32))
        made = core.plain_semaphore("bias_made")
        kept = core.plain_semaphore("bias_kept")
        spilled = core.plain_semaphore("bias_spilled")
        landed = core.plain_semaphore("bias_landed")
        core.start_stage(w.landed["s4"], w.count["s4"])
        with nc.Block() as block:
            @block.tensor
            def _(pe):
                nc.tensor.matmul(core.bank[0:FILTERS, 0, 0:SPAN], w.coeffsT[:, :], w.ramp[:, :], start=True,
                                 stop=True).then_inc(made, 1)
                pe.wait_ge(kept, 1)
                nc.tensor.matmul(core.bank[0:H, 1, 0:SPAN], w.wposT[:, :], filtered[:, :], start=True,
                                 stop=True).then_inc(made, 1)
                pe.wait_ge(landed, 16)
                for g in range(4):
                    nc.tensor.matmul(core.bank[:, 2 + g, :], w.flip[:, :],
                                     reversed_bias[:, 4 * g:4 * g + 4, :].rearrange("p h t -> p (h t)"), start=True,
                                     stop=True).then_inc(made, 1)

            @block.vector
            def _(dve):
                dve.wait_ge(made, 1)
                nc.vector.tensor_copy(filtered[:, :], core.bank[0:FILTERS, 0, 0:SPAN]).then_inc(kept, 1)
                dve.wait_ge(made, 2)
                nc.vector.tensor_copy(by_head[:, :], core.bank[0:H, 1, 0:SPAN]).then_inc(kept, 1)
                for g in range(4):
                    dve.wait_ge(made, 3 + g)
                    nc.vector.tensor_copy(w.bias[:, 4 * g:4 * g + 4, :].rearrange("p h t -> p (h t)"),
                                          core.bank[:, 2 + g, :])

            @block.sync
            def _(sp):
                sp.wait_ge(kept, 2)
                sp.dma_start(bias_dram[:, :], by_head[:, :]).then_inc(spilled, 16)
                sp.wait_ge(spilled, 16)
                runs = bass.AP(bias_dram.tensor, 0, [[1, P], [SPAN, H], [1, T]])
                sp.dma_start(reversed_bias[:, :, :], runs).then_inc(landed, 16)



DH5 = 64
PAIRS = H * DH5 // P


def stage5_weights(w, a):
    w.s5_gamma = w.load("s5", "w_s5_gamma", [P, 1], a["s5_gamma"].unsqueeze(1))
    w.s5_beta = w.load("s5", "w_s5_beta", [P, 1], a["s5_beta"].unsqueeze(1))
    pairs = "(c p) d -> p c d"
    w.s5_wqT = w.load("s5", "w_s5_qT", [P, PAIRS, D], a["s5_wqT"].rearrange(pairs, p=P))
    w.s5_wkT = w.load("s5", "w_s5_kT", [P, PAIRS, D], a["s5_wkT"].rearrange(pairs, p=P))
    w.s5_wvT = w.load("s5", "w_s5_vT", [P, PAIRS, D], a["s5_wvT"].rearrange(pairs, p=P))
    w.s5_wo = w.load("s5", "w_s5_o", [P, PAIRS, D], a["s5_wo"].rearrange(pairs, p=P))
    w.s5_bo = w.load("s5", "w_s5_bo", [P, D], a["s5_bo"].unsqueeze(0).to_broadcast([P, D]))
    w.s5_gate = w.load("s5", "w_s5_gate", [P, 1], a["s5_gate"].unsqueeze(0).to_broadcast([P, 1]))


def stage5(nc, core, w, ctxT_dram):
    with ExitStack() as local:
        core.local = local
        def sbuf(name, shape, dtype=F32):
            return local.enter_context(nc.sbuf_tensor(name, shape, dtype))

        ln = Norm(core, sbuf, "s5_ln")
        ln2 = Moments(core, sbuf, "s5_ln2")
        sm = Softmax(core, sbuf, "s5", M, shares=True)
        xn2 = sbuf("s5_xn2", [P, G, D])
        kq = sbuf("s5_kq", [P, H, D])
        vo = sbuf("s5_vo", [P, H, D])
        ctxT = sbuf("s5_ctxT", [P, GM])
        kT = sbuf("s5_kT", [P, H, GM])
        v = sbuf("s5_v", [P, G, H * D])

        sem = core.semaphore
        chain_v = sem("s5_chain_v")
        xn2_ready = sem("s5_xn2_ready")
        keys_done = sem("s5_keys_done")
        keys_by_scalar = sem("s5_keys_by_scalar")
        keys_by_vector = sem("s5_keys_by_vector")
        values_done = sem("s5_values_done")
        values_kept = sem("s5_values_kept")
        x_ready = sem("s5_x_ready")
        x_biased = sem("s5_x_biased")
        ctx_landed = core.plain_semaphore("s5_ctx_landed")
        tanh_ready = core.plain_semaphore("s5_tanh_ready")
        wo_scaled = core.plain_semaphore("s5_wo_scaled")
        fold_done = core.plain_semaphore("s5_fold_done")
        fold_kept = core.plain_semaphore("s5_fold_kept")
        core.start_stage(w.landed["s5"], w.count["s5"])
        bank = core.bank
        VALUES, OUT = WORK, WORK + 1
        KEYS = H // 2
        QUARTERS = 4

        with nc.Block() as block:
            @block.scalar
            def _(act):
                nc.scalar.activation(w.s5_gate[:, :], w.s5_gate[:, :], ACT.Tanh).then_inc(tanh_ready, 1)

            @block.vector
            def _(dve):
                dve.wait_ge(tanh_ready, 1)
                nc.vector.tensor_scalar(w.s5_wo[:, :, :], w.s5_wo[:, :, :], w.s5_gate[:, 0:1], None,
                                        ALU.mult).then_inc(wo_scaled, 1)
                nc.vector.tensor_scalar(w.s5_bo[:, :], w.s5_bo[:, :], w.s5_gate[:, 0:1], None, ALU.mult)
                for h in range(H):
                    dve.wait_ge(fold_done, h + 1)
                    nc.vector.tensor_scalar(kq[:, h, :], bank[:, h % 8, 0:D], float(DH5) ** -0.5, None, ALU.mult)
                    nc.vector.tensor_copy(vo[:, h, :], bank[:, h % 8, D:2 * D]).then_inc(fold_kept, 1)

            @block.tensor
            def _(pe):
                pe.wait_ge(wo_scaled, 1)
                for h in range(H):
                    c, rows = h // 2, slice(DH5 * (h % 2), DH5 * (h % 2) + DH5)
                    if h >= 8:
                        pe.wait_ge(fold_kept, h - 7)
                    nc.tensor.matmul(bank[:, h % 8, 0:D], w.s5_wkT[rows, c, :], w.s5_wqT[rows, c, :], start=True,
                                     stop=True)
                    nc.tensor.matmul(bank[:, h % 8, D:2 * D], w.s5_wvT[rows, c, :], w.s5_wo[rows, c, :], start=True,
                                     stop=True).then_inc(fold_done, 1)

        def keep_keys(copy, h):
            return copy(kT[:, h, :], bank[:, SCORE + h % 4, 0:GM])

        with nc.Block() as block:
            @block.sync
            def _(sp):
                with sp.Fori(0, GROUPS) as i:
                    sp.wait_ge(values_done, at(i, G * QUARTERS, 0))
                    sp.dma_start(ctxT[:, :], ctxT_dram[:, bass.ts(i, GM)]).then_inc(ctx_landed, 16)

            @block.gpsimd
            def _(pool):
                def norm(i):
                    ln.rstd_by_gpsimd(pool, i)
                    ln2.rstd_by_gpsimd(pool, i)
                    pool.wait_ge(ln.xn_ready, at(i, G, G))
                    x = core.x[:, bass.ts(i, G), :]
                    nc.gpsimd.tensor_tensor(x, x, w.s5_bo[:, :].unsqueeze(1).to_broadcast([P, G, D]),
                                            ALU.add).then_inc(x_biased, 1)

                norm(0)
                turns(pool, lambda i, more: norm(i + 1) if more else None)

            @block.scalar
            def _(act):
                def xnT_of(i):
                    act.wait_ge(ln.flipped, at(i, 1, 1))
                    nc.scalar.activation(ln.xnT[:, :], bank[:, FLIP, :], ACT.Identity, bias=w.s5_beta[:, 0:1],
                                         scale=w.s5_gamma[:, 0:1]).then_inc(ln.xnT_ready, 1)

                def keys_of(i):
                    for h in range(0, H, 2):
                        act.wait_ge(keys_done, at(i, H, h + 1))
                        keep_keys(nc.scalar.copy, h).then_inc(keys_by_scalar, 1)

                def values_of(i, k):
                    act.wait_ge(values_done, at(i, G * QUARTERS, k + 1))
                    n, c = k // QUARTERS, k % QUARTERS
                    nc.scalar.copy(v[0:M, n, c * 512:(c + 1) * 512], bank[0:M, VALUES, :]).then_inc(values_kept, 1)

                def turn(i, more):
                    for u in range(U + 1):
                        if u < U:
                            values_of(i, 2 * u)
                        if u >= 1:
                            sm.pT_by_scalar(act, i, u - 1)
                        if u < U:
                            values_of(i, 2 * u + 1)
                            sm.exp_by_scalar(act, i, u)
                    if more:
                        xnT_of(i + 1)
                        keys_of(i + 1)

                nc.scalar.preload_act_table_set("exp_and_others")
                xnT_of(0)
                keys_of(0)
                turns(act, turn)

            @block.vector
            def _(dve):
                def norm(i):
                    chain = Chain(dve, chain_v, i, 2)

                    def part(u):
                        if u == 2:
                            ln.moments_by_vector(chain, ln.source(i))
                        if u == 3:
                            ln.scaled_by_vector(dve, i, ln.xn, ln.source(i), ln.xn_ready)
                        if u == 4:
                            dve.wait_ge(ln.xn_ready, at(i, G, G))
                            ln2.moments_by_vector(chain, lambda n: ln.xn[:, n, :])
                        if u == 5:
                            ln2.scaled_by_vector(dve, i, xn2, lambda n: ln.xn[:, n, :], xn2_ready)
                    return part

                def keys_of(i):
                    for h in range(1, H, 2):
                        dve.wait_ge(keys_done, at(i, H, h + 1))
                        keep_keys(nc.vector.tensor_copy, h).then_inc(keys_by_vector, 1)

                def add_to_x(i, n):
                    dve.wait_ge(sm.weighed, at(i, U, 2 * n + 2))
                    dve.wait_ge(x_biased, at(i, 1, 1))
                    x = core.x[:, bass.ds(i * G + n, 1), :]
                    nc.vector.tensor_tensor(x, bank[:, OUT, 0:D].unsqueeze(1), x,
                                            ALU.add).then_inc(x_ready, 1)

                def turn(i, more):
                    part = norm(i + 1)
                    sm.lower_by_vector(dve, i, 0)
                    for u in range(1, U + 1):
                        sm.share_by_vector(dve, i, u - 1)
                        if u < U:
                            sm.lower_by_vector(dve, i, u)
                        if more:
                            part(u)
                        if u >= 4 and u % 2 == 0:
                            add_to_x(i, (u - 4) // 2)
                    if more:
                        keys_of(i + 1)
                    add_to_x(i, G - 1)

                first = norm(0)
                for u in range(2, 6):
                    first(u)
                keys_of(0)
                turns(dve, turn)

            @block.tensor
            def _(pe):
                def flip_norm(i):
                    pe.wait_ge(xn2_ready, at(i, G, G))
                    pe.wait_ge(sm.pT_ready, at(i, QUADS, 0))
                    for n in range(G):
                        last = nc.tensor.transpose(bank[:, FLIP, n * T:(n + 1) * T], xn2[:, n, :],
                                                   core.ident[:, :])
                    last.then_inc(ln.flipped, 1)

                def keys_of(i, heads):
                    for h in heads:
                        if h < 4:
                            pe.wait_ge(sm.lowered, at(i, U, 0))
                        else:
                            pe.wait_ge(keys_by_vector if h % 2 else keys_by_scalar, at(i, KEYS, (h - 4) // 2 + 1))
                        if h == 0:
                            pe.wait_ge(ctx_landed, (i + 1) * 16)
                        nc.tensor.matmul(bank[:, SCORE + h % 4, 0:GM], kq[:, h, :], ctxT[:, :], start=True,
                                         stop=True).then_inc(keys_done, 1)

                def values_of(i, k):
                    pe.wait_ge(values_kept, at(i, G * QUARTERS, k))
                    n, c = k // QUARTERS, k % QUARTERS
                    nc.tensor.matmul(bank[0:M, VALUES, :], ctxT[:, n * M:(n + 1) * M],
                                     vo[:, 4 * c:4 * c + 4, :].rearrange("p h d -> p (h d)"), start=True,
                                     stop=True).then_inc(values_done, 1)

                def scores_of(i, u):
                    if u == 0:
                        pe.wait_ge(ln.xnT_ready, at(i, 1, 1))
                        pe.wait_ge(keys_by_scalar, at(i, KEYS, KEYS))
                        pe.wait_ge(keys_by_vector, at(i, KEYS, KEYS))
                    else:
                        pe.wait_ge(sm.lowered, at(i, U, u - 1))
                    n = u // 2
                    for g in range(2):
                        h = HU * (u % 2) + 4 * g
                        last = nc.tensor.matmul(bank[:, SCORE + 2 * (u % 2) + g, 0:4 * M].rearrange(
                            "p (h m) -> p h m", m=M), ln.xnT[:, n * T:(n + 1) * T],
                            kT[:, h:h + 4, n * M:(n + 1) * M], start=True, stop=True)
                    last.then_inc(sm.scored, 1)

                def weigh(i, u):
                    n = u // 2
                    pe.wait_ge(x_ready, at(i, G, n))
                    pe.wait_ge(sm.pT_ready, at(i, QUADS, 2 * u + 2))
                    pe.wait_ge(values_kept, at(i, G * QUARTERS, (n + 1) * QUARTERS))
                    for j in range(HU):
                        h = HU * (u % 2) + j
                        last = nc.tensor.matmul(bank[:, OUT, 0:D], sm.pT[0:M, u % 2, j, :],
                                                v[0:M, n, h * D:(h + 1) * D], start=(h == 0), stop=(h == H - 1))
                    last.then_inc(sm.weighed, 1)

                def turn(i, more):
                    for u in range(U + 2):
                        if u < U:
                            scores_of(i, u)
                            values_of(i, 2 * u)
                        if 1 <= u <= U:
                            sm.flip_by_tensor(pe, i, u - 1)
                        if u < U:
                            values_of(i, 2 * u + 1)
                        elif more and u == U:
                            keys_of(i + 1, range(4))
                            flip_norm(i + 1)
                            keys_of(i + 1, range(4, 8))
                        elif more:
                            keys_of(i + 1, range(8, H))
                        if u >= 2:
                            weigh(i, u - 2)

                flip_norm(0)
                keys_of(0, range(H))
                turns(pe, turn)



E6 = 16
SHARED = 4
EXP6 = 2 * P


def stage6_weights(w, a):
    w.s6_routerT = w.load("s6", "w_s6_routerT", [P, E6], a["s6_routerT"])
    w.s6_count = w.load("s6", "w_s6_count", [P, E6], a["count"].unsqueeze(0).to_broadcast([P, E6]))
    w.s6_gateup = w.load("s6", "w_s6_gateup", [P, E6, EXP6], a["s6_gateup"].rearrange("e d f -> d e f"))
    w.s6_down = w.load("s6", "w_s6_down", [P, E6, D], a["s6_down"].rearrange("e f d -> f e d"))
    w.s6_sgateT = w.load("s6", "w_s6_sgateT", [P, SHARED * P], a["s6_sgateT"])
    w.s6_supT = w.load("s6", "w_s6_supT", [P, SHARED * P], a["s6_supT"])
    w.s6_sdownT = w.load("s6", "w_s6_sdownT", [P, SHARED, D], a["s6_sdownT"].rearrange("(c p) d -> p c d", p=P))


def stage6(nc, core, w, out):
    with ExitStack() as local:
        core.local = local
        def sbuf(name, shape, dtype=F32):
            return local.enter_context(nc.sbuf_tensor(name, shape, dtype))

        ln = Norm(core, sbuf, "s6_ln")
        logits = sbuf("s6_logits", [P, G, E6])
        best = sbuf("s6_best", [P, G, 8])
        where = sbuf("s6_where", [P, G, 8], U32)
        index = sbuf("s6_index", [P, G])
        chosen = sbuf("s6_chosen", [P, G, E6], BF16)
        score = sbuf("s6_score", [P, G])
        scaled = sbuf("s6_scaled", [P, G, D])
        scaledT = sbuf("s6_scaledT", [P, GT])
        silu = sbuf("s6_silu", [P, 2, GT])
        shared = sbuf("s6_shared", [P, 2, GT])
        mask = sbuf("s6_mask", [P, E6, GT], BF16)
        masked = sbuf("s6_masked", [P, 2, GT])
        hidden = sbuf("s6_hidden", [P, GT])
        yT = sbuf("s6_yT", [P, GT])

        sem = core.semaphore
        chain_v = sem("s6_chain_v")
        logits_done = sem("s6_logits_done")
        best_ready = sem("s6_best_ready")
        tanh_ready = sem("s6_tanh_ready")
        chosen_ready = sem("s6_chosen_ready")
        scaled_ready = sem("s6_scaled_ready")
        scaled_flipped = sem("s6_scaled_flipped")
        scaledT_ready = sem("s6_scaledT_ready")
        shared_done = sem("s6_shared_done")
        silu_ready = sem("s6_silu_ready")
        shared_ready = sem("s6_shared_ready")
        shared_read = sem("s6_shared_read")
        mask_done = sem("s6_mask_done")
        mask_ready = sem("s6_mask_ready")
        masked_ready = sem("s6_masked_ready")
        masked_read = sem("s6_masked_read")
        hidden_ready = sem("s6_hidden_ready")
        yT_ready = sem("s6_yT_ready")
        y_flipped = sem("s6_y_flipped")
        x_ready = sem("s6_x_ready")
        out_landed = core.plain_semaphore("s6_out_landed")
        core.start_stage(w.landed["s6"], w.count["s6"])
        bank = core.bank
        MISC, LOGITS, MASK, GATE, UP, SUM, OUT = 0, 1, 2, 4, 5, 6, 7

        with nc.Block() as block:
            @block.sync
            def _(sp):
                with sp.Fori(0, GROUPS) as i:
                    sp.wait_ge(x_ready, at(i, 1, 1))
                    sp.dma_start(out.rearrange("n t d -> t n d")[:, bass.ts(i, G), :],
                                 core.x[:, bass.ts(i, G), :]).then_inc(out_landed, 16)
                sp.wait_ge(out_landed, GROUPS * 16)

            @block.gpsimd
            def _(pool):
                with pool.Fori(0, GROUPS) as i:
                    ln.rstd_by_gpsimd(pool, i)

            @block.scalar
            def _(act):
                def score_of(i):
                    act.wait_ge(best_ready, at(i, 1, 1))
                    nc.scalar.activation(score[:, :], best[:, :, 0], ACT.Tanh, scale=0.5).then_inc(tanh_ready, 1)

                def scaledT_of(i):
                    act.wait_ge(scaled_flipped, at(i, 1, 1))
                    nc.scalar.copy(scaledT[:, :], bank[:, MISC, :]).then_inc(scaledT_ready, 1)

                def keep_mask(i, e):
                    act.wait_ge(mask_done, at(i, E6, e + 1))
                    act.wait_ge(masked_ready, at(i, 2 * E6, e + 1 - E6 if e < 2 else 0))
                    nc.scalar.copy(mask[:, e, :], bank[:, MASK + e % 2, :]).then_inc(mask_ready, 1)

                def prepare(i):
                    ln.xnT_by_scalar(act, i, bank[:, MISC, :])
                    score_of(i)
                    scaledT_of(i)
                    keep_mask(i, 0)
                    keep_mask(i, 1)

                def turn(i, more):
                    for e in range(2, E6):
                        keep_mask(i, e)
                    act.wait_ge(masked_read, at(i, 2 * E6, E6))
                    nc.scalar.activation(silu[:, 0, :], bank[:, GATE, :], ACT.Silu).then_inc(silu_ready, 1)
                    for c in range(SHARED):
                        act.wait_ge(shared_done, at(i, SHARED, c + 1))
                        if c == 1:
                            act.wait_ge(hidden_ready, at(i, 1, 1))
                        else:
                            act.wait_ge(shared_ready, at(i, SHARED, max(c - 1, 0)))
                        nc.scalar.activation(silu[:, (c + 1) % 2, :], bank[:, GATE if c % 2 else MASK, :],
                                             ACT.Silu).then_inc(silu_ready, 1)
                    if more:
                        prepare(i + 1)
                    act.wait_ge(masked_read, at(i, 2 * E6, 2 * E6))
                    nc.scalar.copy(yT[:, :], bank[:, SUM, :]).then_inc(yT_ready, 1)

                nc.scalar.preload_act_table_set("silu_and_others")
                prepare(0)
                turns(act, turn)

            @block.vector
            def _(dve):
                def find_best(i, chain):
                    dve.wait_ge(logits_done, at(i, 1, 1))
                    chain.link(nc.vector.tensor_copy(
                        logits[:, :, :], bank[:, LOGITS, 0:G * E6].rearrange("p (n e) -> p n e", e=E6)))
                    core.hold_vector()
                    for n in range(G):
                        last = nc.vector.max(best[:, n, :], logits[:, n, :])
                    last.then_inc(best_ready, 1)
                    dve.wait_ge(best_ready, at(i, 1, 1))
                    core.hold_vector()
                    for n in range(G):
                        last = nc.vector.max_index(where[:, n, :], best[:, n, :], logits[:, n, :])
                    chain.link(last)

                def choose(chain):
                    chain.link(nc.vector.tensor_copy(index[:, :], where[:, :, 0]))
                    for n in range(G):
                        last = nc.vector.tensor_scalar(chosen[:, n, :], w.s6_count[:, :], index[:, n:n + 1], None,
                                                       ALU.is_equal)
                    last.then_inc(chosen_ready, 1)

                def scale_tokens(i, chain):
                    dve.wait_ge(tanh_ready, at(i, 1, 1))
                    chain.link(nc.vector.tensor_scalar(score[:, :], score[:, :], 0.5, 0.5, ALU.mult, ALU.add))
                    for n in range(G):
                        last = nc.vector.tensor_scalar(scaled[:, n, :], ln.xn[:, n, :], score[:, n:n + 1], None,
                                                       ALU.mult)
                    last.then_inc(scaled_ready, 1)

                def mask_tokens(i, k):
                    e = k % E6
                    dve.wait_ge(mask_ready, at(i, E6, e + 1))
                    dve.wait_ge(masked_read, at(i, 2 * E6, k - 1))
                    nc.vector.tensor_tensor(masked[:, k % 2, :], scaledT[:, :] if k < E6 else hidden[:, :],
                                            mask[:, e, :], ALU.mult).then_inc(masked_ready, 1)

                def first_masks(i):
                    dve.wait_ge(scaledT_ready, at(i, 1, 1))
                    mask_tokens(i, 0)
                    mask_tokens(i, 1)

                def turn(i, more):
                    chain = Chain(dve, chain_v, i + 1, 5)
                    for e in range(2, E6):
                        mask_tokens(i, e)
                        if e == 6 and more:
                            ln.moments_by_vector(chain, ln.source(i + 1))
                        if e == 9 and more:
                            ln.scaled_by_vector(dve, i + 1, ln.xn, ln.source(i + 1), ln.xn_ready)
                    dve.wait_ge(masked_read, at(i, 2 * E6, E6))
                    dve.wait_ge(silu_ready, at(i, SHARED + 1, 1))
                    nc.vector.tensor_tensor(hidden[:, :], bank[:, UP, :], silu[:, 0, :],
                                            ALU.mult).then_inc(hidden_ready, 1)
                    for c in range(SHARED):
                        dve.wait_ge(silu_ready, at(i, SHARED + 1, c + 2))
                        dve.wait_ge(shared_read, at(i, SHARED, max(c - 1, 0)))
                        nc.vector.tensor_tensor(shared[:, c % 2, :], bank[:, UP if c % 2 else MASK + 1, :],
                                                silu[:, (c + 1) % 2, :], ALU.mult).then_inc(shared_ready, 1)
                        if c < 2:
                            dve.wait_ge(hidden_ready, at(i, 1, 1))
                            mask_tokens(i, E6 + c)
                    for e in range(2, E6):
                        mask_tokens(i, E6 + e)
                        if more and e == 6:
                            find_best(i + 1, chain)
                        if more and e == 7:
                            choose(chain)
                        if more and e == 8:
                            scale_tokens(i + 1, chain)
                    if more:
                        first_masks(i + 1)
                    dve.wait_ge(y_flipped, at(i, 1, 1))
                    x = core.x[:, bass.ts(i, G), :]
                    nc.vector.tensor_tensor(x, bank[:, OUT, :].rearrange("p (n d) -> p n d", d=D), x,
                                            ALU.add).then_inc(x_ready, 1)

                first = Chain(dve, chain_v, 0, 5)
                ln.norm_by_vector(dve, 0, first)
                find_best(0, first)
                choose(first)
                scale_tokens(0, first)
                first.end()
                first_masks(0)
                turns(dve, turn)

            @block.tensor
            def _(pe):
                def logits_of(i):
                    pe.wait_ge(ln.xnT_ready, at(i, 1, 1))
                    for n in range(G):
                        last = nc.tensor.matmul(bank[:, LOGITS, n * E6:(n + 1) * E6], ln.xnT[:, n * T:(n + 1) * T],
                                                w.s6_routerT[:, :], start=True, stop=True)
                    last.then_inc(logits_done, 1)

                def flip_scaled(i):
                    pe.wait_ge(scaled_ready, at(i, 1, 1))
                    for n in range(G):
                        last = nc.tensor.transpose(bank[:, MISC, n * T:(n + 1) * T], scaled[:, n, :], core.ident[:, :])
                    last.then_inc(scaled_flipped, 1)

                def mask_of(i, e):
                    pe.wait_ge(chosen_ready, at(i, 1, 1))
                    pe.wait_ge(mask_ready, at(i, E6, max(e - 1, 0)))
                    for n in range(G):
                        last = nc.tensor.matmul(bank[:, MASK + e % 2, n * T:(n + 1) * T],
                                                chosen[:, n, e:e + 1].to_broadcast([P, P]), core.ident_bf[:, :],
                                                start=True, stop=True)
                    last.then_inc(mask_done, 1)

                def shared_hidden(i, c):
                    if c == 0:
                        pe.wait_ge(mask_ready, at(i, E6, E6))
                    elif c == 1:
                        pe.wait_ge(hidden_ready, at(i, 1, 1))
                    else:
                        pe.wait_ge(shared_ready, at(i, SHARED, c - 1))
                    nc.tensor.matmul(bank[:, GATE if c % 2 else MASK, :], w.s6_sgateT[:, c * P:(c + 1) * P],
                                     ln.xnT[:, :], start=True, stop=True)
                    nc.tensor.matmul(bank[:, UP if c % 2 else MASK + 1, :], w.s6_supT[:, c * P:(c + 1) * P],
                                     ln.xnT[:, :], start=True, stop=True).then_inc(shared_done, 1)

                def shared_down(i, c):
                    pe.wait_ge(shared_ready, at(i, SHARED, c + 1))
                    if c == 0:
                        pe.wait_ge(yT_ready, at(i, 1, 0))
                    nc.tensor.matmul(bank[:, SUM, :], w.s6_sdownT[:, c, :], shared[:, c % 2, :], start=(c == 0),
                                     stop=False).then_inc(shared_read, 1)

                def turn(i, more):
                    for e in range(E6):
                        pe.wait_ge(masked_ready, at(i, 2 * E6, e + 1))
                        nc.tensor.matmul(bank[:, GATE, :], w.s6_gateup[:, e, 0:P], masked[:, e % 2, :],
                                         start=(e == 0), stop=(e == E6 - 1))
                        nc.tensor.matmul(bank[:, UP, :], w.s6_gateup[:, e, P:EXP6], masked[:, e % 2, :],
                                         start=(e == 0), stop=(e == E6 - 1)).then_inc(masked_read, 1)
                        if e + 2 < E6:
                            mask_of(i, e + 2)
                    shared_hidden(i, 0)
                    shared_hidden(i, 1)
                    for c in range(SHARED):
                        if c + 2 < SHARED:
                            shared_hidden(i, c + 2)
                        shared_down(i, c)
                    if more:
                        ln.flip_by_tensor(pe, i + 1, bank[:, MISC, :])
                    for e in range(E6):
                        pe.wait_ge(masked_ready, at(i, 2 * E6, E6 + e + 1))
                        nc.tensor.matmul(bank[:, SUM, :], w.s6_down[:, e, :], masked[:, e % 2, :], start=False,
                                         stop=(e == E6 - 1)).then_inc(masked_read, 1)
                        if e == 1 and more:
                            logits_of(i + 1)
                        if e == 10 and more:
                            flip_scaled(i + 1)
                        if e == 12 and more:
                            mask_of(i + 1, 0)
                        if e == 13 and more:
                            mask_of(i + 1, 1)
                    pe.wait_ge(yT_ready, at(i, 1, 1))
                    pe.wait_ge(x_ready, at(i, 1, 0))
                    for n in range(G):
                        last = nc.tensor.transpose(bank[:, OUT, n * T:(n + 1) * T], yT[:, n * T:(n + 1) * T],
                                                   core.ident[:, :])
                    last.then_inc(y_flipped, 1)

                ln.flip_by_tensor(pe, 0, bank[:, MISC, :])
                logits_of(0)
                flip_scaled(0)
                mask_of(0, 0)
                mask_of(0, 1)
                turns(pe, turn)



def laid_out(inputs):
    f = {k: np.asarray(v) for k, v in inputs.items()}
    band, upto, minus_after, own = level_constants()
    out = {"x": f["x"], "band": band, "upto": upto, "minus_after": minus_after, "own": own}
    out["s1_wq"], out["s1_wk"], out["s1_wv"] = f["L0_attn_Wq"], f["L0_attn_Wk"], f["L0_attn_Wv"]
    out["s1_woT"] = f["L0_attn_Wo"].T
    levels = f["L0_attn_Wdl"].reshape(H1, -1, D)[:, :LEVELS].transpose(1, 0, 2).reshape(LEVELS * H1, D)
    out["s1_small"] = np.concatenate([f["L0_attn_Wg"], levels]).T
    out["s1_bias"] = np.concatenate([f["L0_attn_bg"], f["L0_attn_Lparam"][:, :LEVELS].T.reshape(-1)])
    out["s1_g"], out["s1_b"] = f["L0_attn_ln_g"], f["L0_attn_ln_b"]
    out["flip"] = np.eye(P, dtype=np.float32)[::-1]
    out["ctxT"] = f["ctx_1024"].reshape(BATCH * M, D).T
    out["head_of"] = narrow_constants()
    for name in ("q", "k", "v", "o"):
        out[f"s2_w{name}T"] = f[f"L0_xattn_W{name}"].T
        out[f"s2_b{name}"] = f[f"L0_xattn_b{name}"]
    out["s3_norm"], out["s3_gateT"] = f["L0_ffn_norm_weight"], f["L0_ffn_gate_w"].T
    out["s3_w1T"] = f["L0_ffn_w1"].reshape(E3 * HID, D).T
    out["s3_b1T"] = f["L0_ffn_b1"].reshape(E3 * CHUNKS, P).T
    out["s3_w2T"] = f["L0_ffn_w2"].transpose(0, 2, 1).reshape(E3 * HID, D)
    out["s3_b2"] = f["L0_ffn_b2"]
    out["count"] = np.arange(16, dtype=np.float32)
    for k, name in enumerate(("q", "k", "v")):
        out[f"s4_w{name}T"] = f["L1_attn_Wqkv"][k * D:(k + 1) * D].T
    out["s4_woT"] = f["L1_attn_Wout"].T
    out["ramp"], out["s4_coeffsT"], out["s4_wposT"] = ramp_constants(), f["L1_attn_coeffs"].T, f["L1_attn_Wpos"].T
    out["s5_gamma"], out["s5_beta"] = f["L1_xattn_ln_gamma"], f["L1_xattn_ln_beta"]
    out["s5_wqT"], out["s5_wo"] = f["L1_xattn_w_q"].T, f["L1_xattn_w_out"]
    out["s5_wkT"], out["s5_wvT"] = f["L1_xattn_w_kv"][:, :H * DH5].T, f["L1_xattn_w_kv"][:, H * DH5:].T
    out["s5_bo"], out["s5_gate"] = f["L1_xattn_b_out"], f["L1_xattn_gate"]
    out["s6_routerT"], out["s6_gateup"] = f["L1_ffn_router_w"].T, f["L1_ffn_gate_up_proj"]
    out["s6_down"], out["s6_sgateT"] = f["L1_ffn_down_proj"], f["L1_ffn_shared_gate_w"].T
    out["s6_supT"], out["s6_sdownT"] = f["L1_ffn_shared_up_w"].T, f["L1_ffn_shared_down_w"].T
    return {k: np.ascontiguousarray(v) for k, v in out.items()}


def program(nc, a, out):
    scratch = nc.dram_tensor("lam_scratch", [P, LEVELS, G * H1], F32, kind="Internal").ap()
    bias_dram = nc.dram_tensor("bias_scratch", [H, SPAN], F32, kind="Internal").ap()
    with ExitStack() as ctx:
        core = Core(nc, ctx)
        w = Weights(core)
        stage1_weights(w, a)
        s2 = narrow_weights(w, a, "s2")
        stage3_weights(w, a)
        s4 = narrow_weights(w, a, "s4")
        bias_weights(w, a)
        stage5_weights(w, a)
        stage6_weights(w, a)

        x_landed = ctx.enter_context(nc.semaphore("x_landed"))
        setup_step = ctx.enter_context(nc.semaphore("setup_step"))
        with nc.Block() as block:
            @block.sync
            def _(sp):
                w.start_loads(sp, lambda stage: stage == "s1")
                sp.dma_start(core.x[:, :, :], a["x"].rearrange("n t d -> t n d")).then_inc(x_landed, 16)
                sp.wait_ge(x_landed, 16)

            @block.gpsimd
            def _(pool):
                nc.gpsimd.memset(core.minus_half[:, :], -0.5)
                for eps, tile in core.eps.items():
                    nc.gpsimd.memset(tile[:, :], eps)
                nc.gpsimd.memset(core.ident[:, :], 0.0).then_inc(setup_step, 1)
                pool.wait_ge(setup_step, 1)
                nc.gpsimd.affine_select(out=core.ident[:, :], in_=core.ident[:, :], compare_op=ALU.not_equal, fill=1.0,
                                        base=0, pattern=[[-1, P]], channel_multiplier=1).then_inc(setup_step, 1)
                pool.wait_ge(setup_step, 2)
                nc.gpsimd.tensor_copy(core.ident_bf[:, :], core.ident[:, :])

        stage1(nc, core, w, scratch)
        narrow_attention(nc, core, w, "s2", s2, ctxT_dram=a["ctxT"])
        stage3(nc, core, w)
        make_bias(nc, core, w, bias_dram)
        narrow_attention(nc, core, w, "s4", s4, bias=w.bias)
        stage5(nc, core, w, a["ctxT"])
        stage6(nc, core, w, out)

        with nc.Block() as block:
            @block.sync
            def _(sp):
                for stage in w.landed:
                    sp.wait_ge(w.landed[stage], w.count[stage])


def kernel(**inputs):
    import concourse.bacc as bacc
    from concourse.bass_utils import run_bass_kernel_spmd

    nc = bacc.Bacc("TRN2", target_bir_lowering=False, num_devices=1)
    arrays = laid_out(inputs)
    a = {name: nc.dram_tensor(name, v.shape, mybir.dt.from_np(v.dtype), kind="ExternalInput").ap()
         for name, v in arrays.items()}
    out = nc.dram_tensor("out", (BATCH, T, D), F32, kind="ExternalOutput").ap()
    program(nc, a, out)
    return run_bass_kernel_spmd(nc, [arrays], core_ids=[0]).results[0]["out"]
```
